# Optimizing a Trainium2 kernel written in Bass

```python
import numpy as np
import jax
import jax.numpy as jnp

def _softmax(x, axis=-1):
    return jax.nn.softmax(x, axis=axis)

def _gelu(x):
    return jax.nn.gelu(x, approximate=True)

def _silu(x):
    return jax.nn.silu(x)

def _sigmoid(x):
    return jax.nn.sigmoid(x)

def _layernorm(x, axis=-1, eps=1e-05):
    m = jnp.mean(x, axis=axis, keepdims=True)
    v = jnp.var(x, axis=axis, keepdims=True)
    return (x - m) / jnp.sqrt(v + eps)

def _scatter_add(tgt, idx, src, axis=0):
    return tgt.at[idx].add(src)

def _segment_sum(src, seg, n):
    return jax.ops.segment_sum(src, seg, n)
kernel_name = 'mk_early_fusion_embed_d1_tok_img1024_r4_98c23c'

def setup_inputs(seed: int=0):
    np.random.seed(seed)
    _w = jnp.asarray

    def _rec_inputs():
        import jax
        import jax.numpy as jnp
        _rk = jax.random.key(seed)
        x = -0.00016672 + 0.999947 * jax.random.normal(jax.random.fold_in(_rk, 1), (8, 3, 96, 96), jnp.float32)
        x_txt = jax.random.randint(jax.random.fold_in(_rk, 51), (8, 128), 0, 30521, jnp.int32)
        mask_BS_i1_0 = jnp.where(jnp.ones((8, 128), dtype=bool), 1, 0).astype(jnp.int32)
        return (x, x_txt, mask_BS_i1_0)
    x, x_txt, mask_BS_i1_0 = _rec_inputs()

    def _L0_tok_setup():
        import jax, jax.numpy as jnp
        import numpy as np
        EMBED_DIM = 256
        IMAGE_SIZE = 96
        CHANNELS = 3
        PATCH = 16
        NUM_PATCHES = (IMAGE_SIZE // PATCH) ** 2
        PATCH_DIM = PATCH * PATCH * CHANNELS

        def _patchify(x, patch):
            B, C, H, W = x.shape
            hp, wp = (H // patch, W // patch)
            x = x.reshape(B, C, hp, patch, wp, patch)
            x = x.transpose(0, 2, 4, 1, 3, 5)
            return x.reshape(B, hp * wp, C * patch * patch)
        key = jax.random.key(seed)
        k_x, k_w, k_b, k_cls, k_pos = jax.random.split(key, 5)
        x = jax.random.normal(k_x, (64, CHANNELS, IMAGE_SIZE, IMAGE_SIZE), dtype=jnp.float32)
        W = jax.random.normal(k_w, (EMBED_DIM, PATCH_DIM), dtype=jnp.float32) / np.sqrt(PATCH_DIM)
        b = jax.random.normal(k_b, (EMBED_DIM,), dtype=jnp.float32) * 0.01
        cls_token = jax.random.normal(k_cls, (1, 1, EMBED_DIM), dtype=jnp.float32)
        pos_embedding = jax.random.normal(k_pos, (1, 1 + NUM_PATCHES, EMBED_DIM), dtype=jnp.float32)
        return {'x': x, 'W': W, 'b': b, 'cls_token': cls_token, 'pos_embedding': pos_embedding}
    _L0_tok_all = _L0_tok_setup()
    _L0_tok_in = {k: v for k, v in _L0_tok_all.items() if k in ('W', 'b', 'cls_token', 'pos_embedding')}
    del _L0_tok_all

    def _L0_txt_setup():
        import jax, jax.numpy as jnp
        import numpy as np
        EPS = 1e-05
        key = jax.random.key(seed)
        ks = jax.random.split(key, 5)
        B, S, V, H, P, T = (32, 128, 30522, 256, 128, 2)
        input_ids = jax.random.randint(ks[0], (B, S), 0, V)
        token_type_ids = jax.random.randint(ks[1], (B, S), 0, T)
        token_W = jax.random.normal(ks[2], (V, H), dtype=jnp.float32)
        pos_W = jax.random.normal(ks[3], (P, H), dtype=jnp.float32)
        type_W = jax.random.normal(ks[4], (T, H), dtype=jnp.float32)
        ln_w = jnp.ones((H,), dtype=jnp.float32)
        ln_b = jnp.zeros((H,), dtype=jnp.float32)
        return {'input_ids': input_ids, 'token_type_ids': token_type_ids, 'token_W': token_W, 'pos_W': pos_W, 'type_W': type_W, 'ln_w': ln_w, 'ln_b': ln_b}
    _L0_txt_all = _L0_txt_setup()
    _L0_txt_in = {k: v for k, v in _L0_txt_all.items() if k in ('token_W', 'pos_W', 'type_W', 'ln_w', 'ln_b')}
    del _L0_txt_all

    def _L0_attn_setup():
        import jax, jax.numpy as jnp
        import numpy as np
        N_HEADS = 16

        def _rope_cos_sin(hs, T, dtype):
            t = jnp.arange(1, T + 1, dtype=dtype)[:, None]
            i = jnp.arange(hs // 2, dtype=dtype)
            theta = (1.0 / 10000.0) ** (2.0 * i / hs)
            ang = t * theta
            return (jnp.cos(ang), jnp.sin(ang))

        def _apply_rope(u, cos, sin):
            ue = u[..., ::2]
            uo = u[..., 1::2]
            real = cos * ue - sin * uo
            out = jnp.stack([real, jnp.zeros_like(real)], axis=-1)
            return out.reshape(u.shape)
        key = jax.random.key(seed)
        ks = jax.random.split(key, 6)
        B, T, H = (2, 512, 256)
        scale = 0.02
        return {'x': jax.random.normal(ks[0], (B, T, H), dtype=jnp.float32), 'Wq': jax.random.normal(ks[1], (H, H), dtype=jnp.float32) * scale, 'bq': jnp.zeros((H,), dtype=jnp.float32), 'Wk': jax.random.normal(ks[2], (H, H), dtype=jnp.float32) * scale, 'bk': jnp.zeros((H,), dtype=jnp.float32), 'Wv': jax.random.normal(ks[3], (H, H), dtype=jnp.float32) * scale, 'bv': jnp.zeros((H,), dtype=jnp.float32), 'Wo': jax.random.normal(ks[4], (H, H), dtype=jnp.float32) * scale, 'bo': jnp.zeros((H,), dtype=jnp.float32)}
    _L0_attn_all = _L0_attn_setup()
    _L0_attn_in = {k: v for k, v in _L0_attn_all.items() if k in ('Wq', 'bq', 'Wk', 'bk', 'Wv', 'bv', 'Wo', 'bo')}
    del _L0_attn_all

    def _L0_ffn_setup():
        import jax, jax.numpy as jnp
        import numpy as np
        D_MODEL = 256
        D_FF = 1024
        N_EXPERTS = 4
        key = jax.random.key(seed)
        ks = jax.random.split(key, 8)
        s_in = 1.0 / np.sqrt(D_MODEL)
        s_ff = 1.0 / np.sqrt(D_FF)
        x = jax.random.normal(ks[0], (4, 512, D_MODEL), dtype=jnp.float32)
        W1 = jax.random.uniform(ks[1], (N_EXPERTS, D_MODEL, D_FF), jnp.float32, -s_in, s_in)
        b1 = jax.random.uniform(ks[2], (N_EXPERTS, D_FF), jnp.float32, -s_in, s_in)
        W2 = jax.random.uniform(ks[3], (N_EXPERTS, D_FF, D_MODEL), jnp.float32, -s_ff, s_ff)
        b2 = jax.random.uniform(ks[4], (N_EXPERTS, D_MODEL), jnp.float32, -s_ff, s_ff)
        Wg = jax.random.uniform(ks[5], (D_MODEL, N_EXPERTS), jnp.float32, -s_in, s_in)
        bg = jax.random.uniform(ks[6], (N_EXPERTS,), jnp.float32, -s_in, s_in)
        return {'x': x, 'W1': W1, 'b1': b1, 'W2': W2, 'b2': b2, 'Wg': Wg, 'bg': bg}
    _L0_ffn_all = _L0_ffn_setup()
    _L0_ffn_in = {k: v for k, v in _L0_ffn_all.items() if k in ('W1', 'b1', 'W2', 'b2', 'Wg', 'bg')}
    del _L0_ffn_all
    return {'x': x, 'x_txt': x_txt, 'mask_BS_i1_0': mask_BS_i1_0, 'L0_tok_W': _L0_tok_in['W'], 'L0_tok_b': _L0_tok_in['b'], 'L0_tok_cls_token': _L0_tok_in['cls_token'], 'L0_tok_pos_embedding': _L0_tok_in['pos_embedding'], 'L0_txt_token_W': _L0_txt_in['token_W'], 'L0_txt_pos_W': _L0_txt_in['pos_W'], 'L0_txt_type_W': _L0_txt_in['type_W'], 'L0_txt_ln_w': _L0_txt_in['ln_w'], 'L0_txt_ln_b': _L0_txt_in['ln_b'], 'L0_attn_Wq': _L0_attn_in['Wq'], 'L0_attn_bq': _L0_attn_in['bq'], 'L0_attn_Wk': _L0_attn_in['Wk'], 'L0_attn_bk': _L0_attn_in['bk'], 'L0_attn_Wv': _L0_attn_in['Wv'], 'L0_attn_bv': _L0_attn_in['bv'], 'L0_attn_Wo': _L0_attn_in['Wo'], 'L0_attn_bo': _L0_attn_in['bo'], 'L0_ffn_W1': _L0_ffn_in['W1'], 'L0_ffn_b1': _L0_ffn_in['b1'], 'L0_ffn_W2': _L0_ffn_in['W2'], 'L0_ffn_b2': _L0_ffn_in['b2'], 'L0_ffn_Wg': _L0_ffn_in['Wg'], 'L0_ffn_bg': _L0_ffn_in['bg']}

def reference(x, x_txt, mask_BS_i1_0, L0_tok_W, L0_tok_b, L0_tok_cls_token, L0_tok_pos_embedding, L0_txt_token_W, L0_txt_pos_W, L0_txt_type_W, L0_txt_ln_w, L0_txt_ln_b, L0_attn_Wq, L0_attn_bq, L0_attn_Wk, L0_attn_bk, L0_attn_Wv, L0_attn_bv, L0_attn_Wo, L0_attn_bo, L0_ffn_W1, L0_ffn_b1, L0_ffn_W2, L0_ffn_b2, L0_ffn_Wg, L0_ffn_bg):
    import jax
    import jax.numpy as jnp

    def _L0_tok_ref(x, W, b, cls_token, pos_embedding):
        import jax, jax.numpy as jnp
        import numpy as np
        EMBED_DIM = 256
        IMAGE_SIZE = 96
        CHANNELS = 3
        PATCH = 16
        NUM_PATCHES = (IMAGE_SIZE // PATCH) ** 2
        PATCH_DIM = PATCH * PATCH * CHANNELS

        def _patchify(x, patch):
            B, C, H, W = x.shape
            hp, wp = (H // patch, W // patch)
            x = x.reshape(B, C, hp, patch, wp, patch)
            x = x.transpose(0, 2, 4, 1, 3, 5)
            return x.reshape(B, hp * wp, C * patch * patch)
        B = x.shape[0]
        patches = _patchify(x, PATCH)
        tokens = jnp.einsum('bnd,ed->bne', patches, W) + b
        cls = jnp.broadcast_to(cls_token, (B, 1, EMBED_DIM))
        out = jnp.concatenate([cls, tokens], axis=1)
        return out + pos_embedding

    def _L0_txt_ref(input_ids, token_type_ids, token_W, pos_W, type_W, ln_w, ln_b):
        import jax, jax.numpy as jnp
        import numpy as np
        EPS = 1e-05
        S = input_ids.shape[-1]
        te = token_W[input_ids]
        tte = type_W[token_type_ids]
        pe = pos_W[:S][None, :, :]
        e = te + tte + pe
        mean = jax.lax.stop_gradient(jnp.mean(e, axis=-1, keepdims=True))
        var = jax.lax.stop_gradient(jnp.var(e, axis=-1, keepdims=True))
        normalized = (e - mean) / jnp.sqrt(var + EPS)
        return normalized * ln_w + ln_b

    def _L0_attn_ref(x, Wq, bq, Wk, bk, Wv, bv, Wo, bo):
        import jax, jax.numpy as jnp
        import numpy as np
        N_HEADS = 16

        def _rope_cos_sin(hs, T, dtype):
            t = jnp.arange(1, T + 1, dtype=dtype)[:, None]
            i = jnp.arange(hs // 2, dtype=dtype)
            theta = (1.0 / 10000.0) ** (2.0 * i / hs)
            ang = t * theta
            return (jnp.cos(ang), jnp.sin(ang))

        def _apply_rope(u, cos, sin):
            ue = u[..., ::2]
            uo = u[..., 1::2]
            real = cos * ue - sin * uo
            out = jnp.stack([real, jnp.zeros_like(real)], axis=-1)
            return out.reshape(u.shape)
        B, T, H = x.shape
        nh = N_HEADS
        hs = H // nh

        def proj(W, b):
            y = jnp.einsum('bth,oh->bto', x, W) + b
            return y.reshape(B, T, nh, hs).transpose(0, 2, 1, 3)
        Q = proj(Wq, bq)
        K = proj(Wk, bk)
        V = proj(Wv, bv)
        cos, sin = _rope_cos_sin(hs, T, x.dtype)
        Q = _apply_rope(Q, cos, sin)
        K = _apply_rope(K, cos, sin)
        scores = jnp.einsum('bhqd,bhkd->bhqk', Q, K) * (1.0 / jnp.sqrt(jnp.asarray(hs, x.dtype)))
        causal = jnp.tril(jnp.ones((T, T), dtype=bool))
        scores = jnp.where(causal, scores, jnp.asarray(-10000000000.0, x.dtype))
        att = jax.nn.softmax(scores, axis=-1)
        y = jnp.einsum('bhqk,bhkd->bhqd', att, V)
        y = y.transpose(0, 2, 1, 3).reshape(B, T, H)
        return jnp.einsum('bth,oh->bto', y, Wo) + bo

    def _L0_ffn_ref(x, W1, b1, W2, b2, Wg, bg):
        import jax, jax.numpy as jnp
        import numpy as np
        D_MODEL = 256
        D_FF = 1024
        N_EXPERTS = 4
        gate_logits = jnp.einsum('bld,de->ble', x, Wg) + bg
        idx = jnp.argmax(jax.nn.softmax(gate_logits, axis=-1), axis=-1)
        h = jnp.einsum('bld,edf->belf', x, W1) + b1[None, :, None, :]
        h = jax.nn.gelu(h, approximate=False)
        y = jnp.einsum('belf,efd->beld', h, W2) + b2[None, :, None, :]
        onehot = jax.nn.one_hot(idx, N_EXPERTS, dtype=x.dtype)
        out = jnp.einsum('beld,ble->bld', y, onehot)
        return out
    h = _L0_tok_ref(x, L0_tok_W, L0_tok_b, L0_tok_cls_token, L0_tok_pos_embedding)
    h = jnp.concatenate([h, _L0_txt_ref(x_txt, mask_BS_i1_0, L0_txt_token_W, L0_txt_pos_W, L0_txt_type_W, L0_txt_ln_w, L0_txt_ln_b)], axis=1)
    h = h + _L0_attn_ref(_layernorm(h, axis=-1), L0_attn_Wq, L0_attn_bq, L0_attn_Wk, L0_attn_bk, L0_attn_Wv, L0_attn_bv, L0_attn_Wo, L0_attn_bo)
    h = h + _L0_ffn_ref(_layernorm(h, axis=-1), L0_ffn_W1, L0_ffn_b1, L0_ffn_W2, L0_ffn_b2, L0_ffn_Wg, L0_ffn_bg)
    return h

_drawn_inputs = setup_inputs


def setup_inputs(seed=0):
    import zlib

    import numpy as np

    out = dict(_drawn_inputs(seed))
    spreads = {'L0_txt_ln_w': (1.0, 0.2),
     'L0_txt_ln_b': (0.0, 0.1),
     'L0_attn_bq': (0.0, 0.8),
     'L0_attn_bk': (0.0, 0.8),
     'L0_attn_bv': (0.0, 0.1),
     'L0_attn_bo': (0.0, 0.1)}
    factors = {'L0_tok_b': 8.0,
     'L0_attn_Wq': 8.0,
     'L0_attn_Wk': 8.0,
     'L0_ffn_b1': 5.199,
     'L0_ffn_b2': 3.798}
    for name, (base, spread) in spreads.items():
        noise = np.random.default_rng([zlib.crc32(name.encode()), seed]).standard_normal(out[name].shape)
        drawn = base * np.exp(spread * noise) if base else spread * noise
        out[name] = jnp.asarray(drawn.astype(out[name].dtype))
    for name, factor in factors.items():
        out[name] = (out[name] * factor).astype(out[name].dtype)
    return out
```

```python
import numpy as np
import concourse.bass as bass
from concourse import mybir
from contextlib import ExitStack

f32 = mybir.dt.float32
f16 = mybir.dt.float16
bf16 = mybir.dt.bfloat16
i32 = mybir.dt.int32
u32 = mybir.dt.uint32
ALU = mybir.AluOpType
ACT = mybir.ActivationFunctionType
AX = mybir.AxisListType

B, TXT, PATCHES = 8, 128, 36
IMG = PATCHES + 1
T = IMG + TXT
D, HEADS, HD = 256, 16, 16
ROT = HD // 2
PDIM = 768
FF, NE = 1024, 4
VOCAB = 30522
P = 128
K2 = D // P
KP = PDIM // P
KF = FF // P
GRP = 4
Q2 = T - P
QB = 64
QB0 = T - QB
IPB = 3
IT = -(-B // IPB)
TILES = B + IT
CAP = 14
assert CAP == (B * T + NE * (P - 1)) // P
SLOTS = CAP * P
NJ = CAP
NONE = 1 << 20
WS = 64.0
EPS = 1e-5
LNP = float(np.log(1024.0))
SC = 1.0 / np.sqrt(np.float32(HD))
CH = 3
HC2 = 8


def img_rows(i):
    n = min(IPB, B - IPB * i)
    return n, n * IMG


class Steps:

    LEAD = 2

    def __init__(self, sem, names, by=1):
        self.sem, self.names, self.by = sem, list(names), by
        self.head = self.LEAD * len(self.names) * by

    def at(self, r, name=None):
        k = len(self.names) if name is None else self.names.index(name) + 1
        return r * (len(self.names) * self.by) + (k * self.by + self.head)


def program(nc, tok_tab, patches, w_patch, base_pos, base_add, pos_txt, ids, types, w_small, cols, rows_b,
            w1, w2, c_f32, c_bits, none_tab, out):
    ctx = ExitStack()
    with ctx:
        def sb(name, shape, dt):
            return ctx.enter_context(nc.sbuf_tensor(name, shape, dt))

        def sem(name):
            return ctx.enter_context(nc.semaphore(name))

        def steps(name, names, by=1):
            return Steps(sem(name), names.split(), by)

        cf = sb("cf", [P, CF_N], f32)
        ident = cf[:, CF["ident"]:CF["ident"] + P]
        cosw = cf[:, CF["cos"]:CF["cos"] + T]
        sinw = cf[:, CF["sin"]:CF["sin"] + T]
        fold = cf[:, CF["fold"]:CF["fold"] + QB]
        headmask = cf[:, CF["headmask"]:CF["headmask"] + GRP]
        rowid = cf[:, CF["rowid"]:CF["rowid"] + TILES]
        ebase = cf[:, CF["ebase"]:CF["ebase"] + NE]
        order = cf[:, CF["order"]:CF["order"] + NE]
        jrow = cf[:, CF["jrow"]:CF["jrow"] + NJ]
        cb = sb("cb", [P, CB_N], bf16)
        identb = cb[:, CB["ident"]:CB["ident"] + P]
        mask_a = cb[:, CB["mask_a"]:CB["mask_a"] + P]
        mask_b = cb[:, CB["mask_b"]:CB["mask_b"] + T]
        mask_t = cb[:, CB["mask_t"]:CB["mask_t"] + T]
        mask_t2 = cb[:, CB["mask_t2"]:CB["mask_t2"] + Q2]
        before = cb[:, CB["before"]:CB["before"] + P]
        onesb = cb[:, CB["ones"]:CB["ones"] + P]
        selcol = cb[:, CB["sel"]:CB["sel"] + HEADS]
        sel = sb("sel", [P, HEADS, P], bf16)
        wst = [sb(f"wst{i}", [P, K2 * FF], f32) for i in range(2)]
        wp = wst[0][:, 0:KP * D].rearrange("p (k n) -> p k n", k=KP)
        xp = wst[1][:, 0:KP * B * IMG].rearrange("p (k n) -> p k n", k=KP)
        wsm = sb("wsm", [P, W_SMALL], f32)
        wsh = sb("wsh", [P, W_SMALL], f16)
        wsl = sb("wsl", [P, W_SMALL], f16)

        def small(w, base, width):
            return w[:, base:base + K2 * width].rearrange("p (k n) -> p k n", k=K2)

        col = sb("col", [P, COLS], f32)
        bqk64 = sb("bqk64", [P, 4], f32)
        rb = sb("rb", [P, ROWS], f32)

        def row(name, n=1):
            return rb[:, RB[name]:RB[name] + n * D]

        w1h = sb("w1h", [P, NE * K2 * FF], f16)
        w1l = sb("w1l", [P, NE * K2 * FF], f16)
        w2h = sb("w2h", [P, NE * KF * D], f16)
        w2l = sb("w2l", [P, NE * KF * D], f16)
        ids_sb = sb("ids_sb", [P, B], i32)
        types_i = sb("types_i", [P, B], i32)
        types_f = sb("types_f", [P, B], f32)
        ptype = sb("ptype", [P, D], f32)
        typd = sb("typd", [P, D], f32)
        lnp = sb("lnp", [P, 1], f32)
        neghalf = sb("neghalf", [P, 4], f32)

        h_txt = sb("h_txt", [P, B, D], f32)
        h_img = sb("h_img", [P, IT, D], f32)
        base1 = sb("base1", [P, D], f32)
        base2 = sb("base2", [P, D], f32)
        x1 = sb("x1", [P, IT, D], f32)
        xT = sb("xT", [P, 2, K2, B, T], f16)
        st6 = sb("st6", [P, IT, 6], f32)
        mv = sb("mv", [P, IT, 2], f32)
        veps = sb("veps", [P, 4], f32)
        rstd = sb("rstd", [P, 4], f32)

        rot_a = sb("rot_a", [P, 2, T], f32)
        rot_b = sb("rot_b", [P, 2, T], f32)
        rot = sb("rot", [P, 2, T], f32)
        parts = [sb(f"parts{i}", [P, 2, 2, T], f16) for i in range(2)]
        stk = [sb(f"stk{i}", [P, 2, GRP, T], f16) for i in range(2)]
        flat = [sb(n, [P, HEADS * T], f16) for n in ("kz0", "kz1", "ph", "pl")]
        kz0, kz1, ph, pl = (t[:, :].rearrange("p (h n) -> p h n", h=HEADS) for t in flat)
        kz = [kz0, kz1]
        vh = [sb(f"vh{i}", [P, HEADS, HD + 1], f16) for i in range(2)]
        vl = [sb(f"vl{i}", [P, HEADS, HD + 1], f16) for i in range(2)]
        vh2 = [sb(f"vh2{i}", [Q2, HEADS, HD + 1], f16) for i in range(2)]
        vl2 = [sb(f"vl2{i}", [Q2, HEADS, HD + 1], f16) for i in range(2)]
        mx_a = sb("mx_a", [P, HEADS], f32)
        mx_b = sb("mx_b", [P, GRP, 2], f32)
        mx_w = sb("mx_w", [P, GRP, 2, 2], f32)
        nm = [sb(f"nm{i}", [P, T], bf16) for i in range(2)]
        pf = [sb(f"pf{i}", [P, CH * T], f32) for i in range(2)]
        ph2 = sb("ph2", [Q2, HEADS, Q2], f16)
        pl2 = sb("pl2", [Q2, HEADS, Q2], f16)
        rden = sb("rden", [P, 2, HEADS], f32)
        yn = sb("yn", [P, D], f32)
        yn2 = sb("yn2", [Q2, D], f32)
        yT = sb("yT", [P, 2, K2, T], f16)
        yTi = sb("yTi", [P, 2 * K2, B, IMG], f16)

        rows = [sb(f"rows{i}", [P, 2 * D], f32) for i in range(2)]
        g6 = sb("g6", [P, 6], f32)
        gmv = sb("gmv", [P, 2], f32)
        gve = sb("gve", [P, 1], f32)
        grs = sb("grs", [P, 1], f32)
        junk = sb("junk", [P, NE, D], f32)
        logit = sb("logit", [P, NE], f32)
        logb = sb("logb", [P, NE], f32)
        gmax = sb("gmax", [P, 1], f32)
        pick = sb("pick", [P, NE], f32)
        pmax = sb("pmax", [P, 1], f32)
        ohc = [sb(f"ohc{i}", [P, NE], bf16) for i in range(2)]
        ohsum = sb("ohsum", [P, NE], bf16)
        sl4 = sb("sl4", [P, NE], f32)
        sl4b = sb("sl4b", [P, NE], f32)
        slotf = sb("slotf", [P, 1], f32)
        sloti = [sb(f"sloti{i}", [P, 1], i32) for i in range(2)]
        rid = [sb(f"rid{i}", [P, 1], f32) for i in range(2)]
        nf = sb("nf", [1, NE], f32)
        ni = sb("ni", [1, NE], i32)
        nt = sb("nt", [1, NE], f32)
        cum = sb("cum", [1, NE], f32)
        ge = sb("ge", [1, 3, NJ], f32)
        tex = sb("tex", [1, 2, NJ], f32)
        tei = sb("tei", [1, 2, NJ], i32)
        NTAB = NE * CAP
        tab = sb("tab", [NTAB, P], f32)
        tabT = sb("tabT", [P, NTAB], f32)
        tabo = sb("tabo", [P, NTAB], i32)
        tabg = sb("tabg", [P, NTAB], i32)
        none_sb = sb("none_sb", [NTAB, P], f32)

        idg = [sb(f"idg{i}", [P, 1], i32) for i in range(2)]
        ido = [sb(f"ido{i}", [P, 1], i32) for i in range(2)]
        old = [t[:, :] for t in flat]
        xg = [o[:, 0:4 * D].bitcast(f32) for o in old[0:2]]
        hb = [o[:, 4 * D:6 * D].bitcast(f32) for o in old[0:2]]
        yo = [o[:, 6 * D:8 * D].bitcast(f32) for o in old[0:2]]
        gh = [o[:, 0:FF].rearrange("p (k n) -> p k n", k=KF) for o in old[2:4]]
        gl = [o[:, FF:2 * FF].rearrange("p (k n) -> p k n", k=KF) for o in old[2:4]]
        xs = [o[:, 2 * FF:2 * FF + 2 * D].rearrange("p (a k n) -> p a k n", a=2, k=K2) for o in old[2:4]]
        gf = junk[:, :, :].rearrange("p e n -> p (e n)").rearrange("p (k n) -> p k n", k=KF)

        bank = [ctx.enter_context(nc.psum_tensor(f"bank{i}", [P, 512], f32)) for i in range(8)]
        bQ, bK, bV, bM, bS, bY = bank[0], bank[1], bank[2], bank[3:5], bank[5:7], bank[7]

        scr = [nc.dram_tensor(f"scr{i}", (2, 2, P, T), f16, kind="Internal").ap() for i in range(2)]
        tokrows = nc.dram_tensor("tokrows", (B * T, 2 * D), f32, kind="Internal").ap()
        slot_tab = nc.dram_tensor("slot_tab", (NE * SLOTS, 1), f32, kind="Internal").ap()

        ld_c, ld_x, ld_small, ld_rows, ld_ids, ld_pos = (sem(n) for n in
                                                         "ld_c ld_x ld_small ld_rows ld_ids ld_pos".split())
        te_in = sem("te_in")
        ld_w = [sem(f"ld_w{i}") for i in range(2)]
        spare = sem("spare")
        none_ld, none_st = sem("none_ld"), sem("none_st")
        pool_c = sem("pool_c")
        wsplit_a, wsplit_v = sem("wsplit_a"), sem("wsplit_v")
        emb_ps = sem("emb_ps")
        img = sem("img")
        img_rs = sem("img_rs")
        xt_ps, xt_hi, xt_lo = sem("xt_ps"), sem("xt_hi"), sem("xt_lo")
        txt = steps("txt", "e0 e1 e s0 s1 m0 m1 v h0 h1 hw hb t0 t1 n0 n1 w x0 x1")
        txt_rs = steps("txt_rs", "first second bo")
        tt_ps = steps("tt_ps", "t")
        tt_hi = steps("tt_hi", "t")
        tt_lo = steps("tt_lo", "t")

        qkv = steps("qkv", "q k v")
        rope = steps("rope", "qe qo ke ko rot lo")
        rope_hi = steps("rope_hi", "hi")
        v_hi = steps("v_hi", "v1 v2")
        v_lo = steps("v_lo", "v1 v2")
        scr_w = [sem(f"scr_w{i}") for i in range(2)]
        stk_in = [sem(f"stk_in{i}") for i in range(2)]
        kz_ok = steps("kz_ok", "h0 h1 h2 h3")
        mps = steps("mps", "a0 b0 a1 b1 a2 b2 a3 b3 t")
        mx = steps("mx", "a0 b0 a1 b1 a2 b2 a3 b3 w0 w1")
        nm_hi = steps("nm_hi", "n")
        nm_lo = steps("nm_lo", "n")
        sps = steps("sps", "d0 d1 c0 c1 c2 c3 c4 c5")
        ex = steps("ex", "d0 d1 c0 c1 c2 c3 c4 c5")
        pv_h = steps("pv_h", "d0 d1 c0 c1 c2 c3 c4 c5")
        pv_l = steps("pv_l", "d0 d1 c0 c1 c2 c3 c4 c5")
        yps = steps("yps", "y")
        ynorm = steps("ynorm", "r1 r2 y1 y2")
        ytp = steps("ytp", "t")
        yt_hi = steps("yt_hi", "k0 k1")
        yt_lo = steps("yt_lo", "k0 k1")
        yti = steps("yti", "c")
        wops = steps("wops", "o")
        fin = steps("fin", "h s m x g0 g1 g2 g3 l lm p pm z oh")
        fin_rs = steps("fin_rs", "e r")
        rk_ps = steps("rk_ps", "r")
        slot = steps("slot", "a s i sum")
        scat = [sem(f"scat{i}") for i in range(2)]
        rid_ok = steps("rid_ok", "r")
        store = [sem(f"store{i}") for i in range(2)]
        w64 = steps("w64", "s h")
        wlo = steps("wlo", "l")
        cnt_ps, cnt = sem("cnt_ps"), sem("cnt")
        tab_in, tab_ps = sem("tab_in"), sem("tab_ps")

        gat = [sem(f"gat{i}") for i in range(2)]
        idc = steps("idc", "g o")
        hbs = steps("hbs", "b")
        xtp = steps("xtp", "t")
        xsh = steps("xsh", "h")
        xsl = steps("xsl", "l")
        l1 = steps("l1", "a b")
        gel = steps("gel", " ".join(f"g{i}" for i in range(KF)))
        gsp_h = steps("gsp_h", "a b")
        gsp_l = steps("gsp_l", "a b")
        l2 = steps("l2", "o")
        yok = steps("yok", "o")
        osc = [sem(f"osc{i}") for i in range(2)]

        chunks = [("d0", 0, HC2), ("d1", HC2, HC2)] + [(f"c{c}", CH * c, min(CH, HEADS - CH * c))
                                                       for c in range(-(-HEADS // CH))]
        W_LOADS = [(w1, w1h, w1l, e) for e in range(NE)] + [(w2, w2h, w2l, e) for e in range(NE)]
        WN = K2 * FF
        assert WN == KF * D and len(W_LOADS) == B

        block = ctx.enter_context(nc.Block())

        @block.sync
        def _(sp):
            for i in range(2):
                sp.sem_inc(stk_in[i], 128 * Steps.LEAD)
                sp.sem_inc(store[i], 16 * Steps.LEAD)
            sp.dma_start(cf[:, :], c_f32).then_inc(ld_c, 16)
            for k in range(KP):
                sp.dma_start(xp[:, k, :], patches[:, k, :]).then_inc(ld_x, 16)
                sp.dma_start(wp[:, k, :], w_patch[:, k, :]).then_inc(ld_x, 16)
            sp.dma_start(base1[0:IPB * IMG, :], base_pos).then_inc(ld_pos, 16)
            sp.dma_start(base2[0:IPB * IMG, :], base_add).then_inc(ld_pos, 16)
            sp.dma_start(ptype[:, :], pos_txt).then_inc(ld_pos, 16)
            sp.dma_start(rb[:, :], rows_b.partition_broadcast(P)).then_inc(ld_rows, 16)
            sp.dma_start(wsm[:, :], w_small).then_inc(ld_small, 16)
            sp.dma_start(col[:, :], cols).then_inc(ld_small, 16)
            sp.dma_start(cb[:, :].bitcast(mybir.dt.uint16), c_bits).then_inc(ld_small, 16)
            sp.dma_start(none_sb[:, :], none_tab).then_inc(none_ld, 16)
            sp.wait_ge(none_ld, 16)
            sp.dma_start(slot_tab.rearrange("(t p) o -> t (p o)", p=P), none_sb[:, :]).then_inc(none_st, 16)

            def w_load(src, n, e):
                s = src[e].rearrange("(k p) n -> p k n", p=P)
                sp.dma_start(wst[n % 2][:, :].rearrange("p (k n) -> p k n", k=s.shape[1]), s).then_inc(ld_w[n % 2], 16)

            sp.wait_ge(emb_ps, IT)
            w_load(w1, 0, 0)
            w_load(w1, 1, 1)

            def stack(b, par, half):
                sp.wait_ge(rope.sem, rope.at(b, "lo"))
                sp.wait_ge(rope_hi.sem, rope_hi.at(b))
                sp.wait_ge(stk_in[par], 128 * Steps.LEAD + half * 128)
                sp.dma_start(scr[par].rearrange("a c p n -> p (a c) n"),
                             parts[par][:, :, :, :].rearrange("p a c n -> p (a c) n")).then_inc(scr_w[par], 16)
                sp.wait_ge(scr_w[par], half * 16 + 16)
                sp.wait_ge(sps.sem, sps.at(b - 2))
                for a in range(2):
                    for c in range(2):
                        g = 2 * a + c
                        for w, hl in ((0, a), (1, c)):
                            sp.dma_start(stk[par][32 * g:32 * g + 32, w, :, :],
                                         scr[par][hl, w].rearrange("(g p) n -> p g n", p=32)).then_inc(stk_in[par], 16)

            def keep(b, par):
                sp.wait_ge(fin.sem, fin.at(b, "x"))
                sp.dma_start(tokrows[bass.ds(b * T + IMG, TXT), :], rows[par][:, :]).then_inc(store[par], 16)

            stack(0, 0, 0)
            stack(1, 1, 0)
            sp.wait_ge(wlo.sem, wlo.at(0))
            w_load(w1, 2, 2)
            keep(0, 0)
            for i in range(3):
                for par in (1, 0):
                    t = 2 * i + 2 - par
                    stack(t + 1, 1 - par, (t + 1) // 2)
                    if t + 2 < B:
                        sp.wait_ge(wlo.sem, wlo.at(t))
                        src, _, _, e = W_LOADS[t + 2]
                        w_load(src, t + 2, e)
                    keep(t, par)
            keep(7, 1)
            for i in range(IT):
                n, m = img_rows(i)
                sp.wait_ge(fin.sem, fin.at(B + i, "x"))
                for j in range(n):
                    last = sp.dma_start(tokrows[(IPB * i + j) * T:(IPB * i + j) * T + IMG, :],
                                        rows[(B + i) % 2][j * IMG:(j + 1) * IMG, :])
                    last.then_inc(store[(B + i) % 2], 16)
            sp.wait_ge(scat[0], 16 * 6)
            sp.wait_ge(scat[1], 16 * 5)
            sp.dma_start(tab[:, :], slot_tab.rearrange("(t p) o -> t (p o)", p=P)).then_inc(tab_in, 16)
            sp.wait_ge(osc[0], 16 * ((NJ + 1) // 2))
            sp.wait_ge(osc[1], 16 * (NJ // 2))

        @block.gpsimd
        def _(pool):
            for s in (txt_rs, pv_l, fin_rs, rid_ok, wlo, yti, idc):
                pool.sem_inc(s.sem, s.head)
            pool.dma_start(ids_sb[:, :], ids).then_inc(ld_ids, 16)
            pool.dma_start(types_i[:, :], types).then_inc(ld_ids, 16)
            pool.memset(neghalf[:, :], -0.5)
            for i in range(2):
                pool.memset(nm[i][:, :], 0.0)
                pool.memset(vh[i][:, :, :], 1.0)
                pool.memset(vl[i][:, :, :], 0.0)
                pool.memset(vh2[i][:, :, :], 1.0)
                pool.memset(vl2[i][:, :, :], 0.0)
                pool.memset(ohc[i][:, :], 0.0)
            pool.memset(mx_w[:, :, :, :], 0.0)
            pool.memset(ohsum[:, :], 0.0)
            pool.memset(mv[:, :, :], 1.0)
            pool.memset(lnp[:, :], LNP).then_inc(pool_c, 1)
            pool.wait_ge(ld_ids, 32)
            for b in range(B):
                pool.indirect_dma_start(h_txt[:, b, :], None, tok_tab,
                                        bass.IndirectOffsetOnAxis(ids_sb[:, b:b + 1], 0)).then_inc(te_in, 16)
            pool.wait_ge(img, 3 * IT + 2)
            pool.wait_ge(pool_c, 1)
            pool.tensor_tensor(rstd[:, 0:IT], veps[:, 0:IT], neghalf[:, 0:IT], ALU.pow).then_inc(img_rs, 1)
            pool.wait_ge(img, 4 * IT + 2)
            pool.wait_ge(ld_rows, 16)
            for i in range(IT):
                n, m = img_rows(i)
                pool.tensor_tensor(h_img[0:m, i, :], h_img[0:m, i, :], row("bo")[0:m, :], ALU.add).then_inc(img_rs, 1)
            with pool.Fori(0, B // 2) as i:
                pool.wait_ge(txt.sem, txt.at(i, "v"))
                pool.tensor_tensor(rstd[:, 0:2], veps[:, 0:2], neghalf[:, 0:2], ALU.pow).then_inc(txt_rs.sem, 1)
                pool.wait_ge(txt.sem, txt.at(i, "w"))
                pool.tensor_tensor(rstd[:, 2:4], veps[:, 2:4], neghalf[:, 0:2], ALU.pow).then_inc(txt_rs.sem, 1)
                pool.wait_ge(txt.sem, txt.at(i, "x1"))
                h2 = h_txt[:, bass.ds(2 * i, 2), :]
                pool.tensor_tensor(h2, h2, row("bo").unsqueeze(1).to_broadcast([P, 2, D]), ALU.add)\
                    .then_inc(txt_rs.sem, 1)

            def attend(b, par):
                for n, (name, h0, hn) in enumerate(chunks):
                    pool.wait_ge(pv_h.sem, pv_h.at(b, name))
                    if name[0] == "d":
                        pool.tensor_tensor(pl2[:, h0:h0 + hn, :], pf[n % 2][0:Q2, 0:hn * Q2].rearrange("p (h n) -> p h n", h=hn),
                                           ph2[:, h0:h0 + hn, :], ALU.subtract).then_inc(pv_l.sem, 1)
                    else:
                        pool.tensor_tensor(pl[:, h0:h0 + hn, :], pf[n % 2][:, 0:hn * T].rearrange("p (h n) -> p h n", h=hn),
                                           ph[:, h0:h0 + hn, :], ALU.subtract).then_inc(pv_l.sem, 1)
                pool.wait_ge(yt_hi.sem, yt_hi.at(b))
                pool.wait_ge(yt_lo.sem, yt_lo.at(b))
                pool.tensor_copy(yTi[:, :, bass.ds(b, 1), :].rearrange("p a b n -> p a (b n)"),
                                 yT[:, :, :, 0:IMG].rearrange("p a k n -> p (a k) n")).then_inc(yti.sem, 1)

            def finish(r):
                pool.wait_ge(fin.sem, fin.at(r, "m"))
                pool.tensor_scalar(gve[:, :], gmv[:, 1:2], EPS, None, ALU.add).then_inc(fin_rs.sem, 1)
                pool.wait_ge(fin_rs.sem, fin_rs.at(r, "e"))
                pool.tensor_tensor(grs[:, :], gve[:, :], neghalf[:, 0:1], ALU.pow).then_inc(fin_rs.sem, 1)

            def scatter(r, par, half, m=P):
                if not isinstance(half, int) or half > 0:
                    pool.wait_ge(scat[par], half * 16)
                pool.tensor_copy(rid[par][:, :], rowid[:, bass.ds(r, 1)]).then_inc(rid_ok.sem, 1)
                pool.wait_ge(rid_ok.sem, rid_ok.at(r))
                pool.wait_ge(slot.sem, slot.at(r, "i"))
                pool.sem_inc(spare, 1)
                pool.indirect_dma_start(slot_tab, bass.IndirectOffsetOnAxis(sloti[par][0:m, :], 0),
                                        rid[par][0:m, :], None).then_inc(scat[par], 16)

            def w_low(n, hi, lo, e):
                pool.wait_ge(w64.sem, w64.at(n, "h"))
                pool.tensor_tensor(lo[:, e * WN:(e + 1) * WN], wst[n % 2][:, :], hi[:, e * WN:(e + 1) * WN],
                                   ALU.subtract).then_inc(wlo.sem, 1)

            pool.wait_ge(none_st, 16)
            w_low(0, w1h, w1l, 0)
            attend(0, 0)
            finish(0)
            for i in range(3):
                for par in (1, 0):
                    t = 2 * i + 2 - par
                    _, hi, lo, e = W_LOADS[t]
                    w_low(t, hi, lo, e)
                    attend(t, par)
                    scatter(t - 1, 1 - par, (t - 1) // 2)
                    finish(t)
            w_low(7, w2h, w2l, 3)
            attend(7, 1)
            scatter(6, 0, 3)
            finish(7)
            for i in range(IT):
                scatter(B + i - 1, (B + i - 1) % 2, (B + i - 1) // 2, P if i == 0 else img_rows(i - 1)[1])
                finish(B + i)
            scatter(B + IT - 1, (B + IT - 1) % 2, (B + IT - 1) // 2, img_rows(IT - 1)[1])

            pool.wait_ge(cnt, CNT_DONE)
            pool.wait_ge(store[0], 16 * (Steps.LEAD + 4 + 3 + 2))
            pool.wait_ge(store[1], 16 * (Steps.LEAD + 4 + 3))

            def gather(j, par):
                c = pool.value_load(tei[0:1, 0, bass.ds(j, 1)], min_val=0, max_val=NTAB - 1)
                pool.wait_ge(yok.sem, yok.at(j - 2))
                pool.tensor_copy(idg[par][:, :], tabg[:, bass.ds(c, 1)]).then_inc(idc.sem, 1)
                pool.tensor_copy(ido[par][:, :], tabo[:, bass.ds(c, 1)]).then_inc(idc.sem, 1)
                pool.wait_ge(idc.sem, idc.at(j))
                pool.sem_inc(spare, 1)
                pool.indirect_dma_start(xg[par][:, :], None, tokrows,
                                        bass.IndirectOffsetOnAxis(idg[par][:, :], 0)).then_inc(gat[par], 16)

            def scatter_out(j, par):
                pool.wait_ge(yok.sem, yok.at(j))
                pool.sem_inc(spare, 1)
                pool.indirect_dma_start(out, bass.IndirectOffsetOnAxis(ido[par][:, :], 0), yo[par][:, :], None,
                                        bounds_check=B * T - 1, oob_is_err=False).then_inc(osc[par], 16)

            gather(0, 0)
            gather(1, 1)
            with pool.Fori(0, NJ // 2 - 1) as i:
                for par in range(2):
                    scatter_out(2 * i + par, par)
                    pool.wait_ge(osc[par], i * 16 + 16)
                    gather(2 * i + par + 2, par)
            scatter_out(NJ - 2, 0)
            scatter_out(NJ - 1, 1)

        @block.scalar
        def _(act):
            for s in (tt_hi, rope_hi, v_hi, nm_hi, ex, yt_hi, w64, xsh, gel):
                act.sem_inc(s.sem, s.head)
            act.wait_ge(ld_small, 48)
            act.activation(wsm[:, :], wsm[:, :], ACT.Copy, scale=WS).then_inc(wsplit_a, 1)
            act.wait_ge(wsplit_a, 1)
            act.activation(wsh[:, :], wsm[:, :], ACT.Copy).then_inc(wsplit_a, 1)
            act.activation(bqk64[:, :], col[:, 0:4], ACT.Copy, scale=WS).then_inc(wsplit_a, 1)
            for i in range(IT):
                n, m = img_rows(i)
                act.wait_ge(xt_ps, i + 1)
                act.activation(xT[:, 0, :, IPB * i:IPB * i + n, 0:IMG],
                               bank[i][:, 0:K2 * m].rearrange("p (k b n) -> p k b n", k=K2, b=n), ACT.Copy)\
                   .then_inc(xt_hi, 1)
            with act.Fori(0, B // 2) as i:
                act.wait_ge(tt_ps.sem, tt_ps.at(i))
                act.activation(xT[:, 0, :, bass.ds(2 * i, 2), IMG:T],
                               bank[3][:, :].rearrange("p (k b n) -> p k b n", k=K2, b=2), ACT.Copy)\
                   .then_inc(tt_hi.sem, 1)

            def project(b, par):
                act.wait_ge(qkv.sem, qkv.at(b, "v"))
                act.wait_ge(yps.sem, yps.at(b - 2))
                act.activation(vh[par][:, :, 0:HD], bV[:, 0:D].rearrange("p (h n) -> p h n", h=HEADS), ACT.Copy,
                               scale=1 / WS).then_inc(v_hi.sem, 1)
                act.activation(vh2[par][:, :, 0:HD], bV[0:Q2, D:2 * D].rearrange("p (h n) -> p h n", h=HEADS), ACT.Copy,
                               scale=1 / WS).then_inc(v_hi.sem, 1)
                act.wait_ge(rope.sem, rope.at(b, "rot"))
                act.activation(parts[par][:, 0, :, :], rot[:, :, :], ACT.Copy).then_inc(rope_hi.sem, 1)

            def attend(b, par):
                for n, (name, h0, hn) in enumerate(chunks):
                    act.wait_ge(sps.sem, sps.at(b, name))
                    back = chunks[n - 2][0]
                    act.wait_ge(pv_l.sem, pv_l.at(b if n >= 2 else b - 1, back))
                    if name[0] == "d":
                        act.activation(pf[n % 2][0:Q2, 0:hn * Q2], bS[n % 2][0:Q2, 0:hn * Q2], ACT.Exp,
                                       bias=lnp[0:Q2, :], scale=SC).then_inc(ex.sem, 1)
                    else:
                        act.activation(pf[n % 2][:, 0:hn * T], bS[n % 2][:, 0:hn * T], ACT.Exp,
                                       bias=lnp[:, :], scale=SC).then_inc(ex.sem, 1)
                act.wait_ge(ytp.sem, ytp.at(b))
                act.wait_ge(wops.sem, wops.at(b - 1))
                act.wait_ge(yti.sem, yti.at(b - 1))
                for k in range(K2):
                    act.activation(yT[:, 0, k, :], bV[:, k * T:(k + 1) * T], ACT.Identity, bias=col[:, 4 + k:5 + k])\
                       .then_inc(yt_hi.sem, 1)

            def maxima(b, par):
                act.wait_ge(mps.sem, mps.at(b, "t"))
                act.wait_ge(sps.sem, sps.at(b - 2))
                act.activation(nm[par][0:HEADS, :], bM[0][0:HEADS, 0:T], ACT.Copy, scale=-1.0).then_inc(nm_hi.sem, 1)

            def w_high(n, hi, e):
                act.wait_ge(ld_w[n % 2], 16 * (n // 2 + 1))
                act.activation(wst[n % 2][:, :], wst[n % 2][:, :], ACT.Copy, scale=WS).then_inc(w64.sem, 1)
                act.wait_ge(w64.sem, w64.at(n, "s"))
                act.activation(hi[:, e * WN:(e + 1) * WN], wst[n % 2][:, :], ACT.Copy).then_inc(w64.sem, 1)

            act.wait_ge(pool_c, 1)
            w_high(0, w1h, 0)
            project(0, 0)
            maxima(0, 0)
            project(1, 1)
            attend(0, 0)
            maxima(1, 1)
            for i in range(3):
                for par in (1, 0):
                    t = 2 * i + 2 - par
                    project(t + 1, 1 - par)
                    _, hi, _, e = W_LOADS[t]
                    w_high(t, hi, e)
                    attend(t, par)
                    maxima(t + 1, 1 - par)
            w_high(7, w2h, 3)
            attend(7, 1)

            def expert_x(j, par):
                act.wait_ge(xtp.sem, xtp.at(j))
                act.wait_ge(l1.sem, l1.at(j - 2))
                act.activation(xs[par][:, 0, :, :], bank[0][:, 0:D].rearrange("p (k n) -> p k n", k=K2), ACT.Copy)\
                   .then_inc(xsh.sem, 1)

            def gelus(j, par):
                e = act.value_load(tei[0:1, 1, bass.ds(j, 1)], min_val=0, max_val=NE - 1)
                for n in range(KF):
                    if n % 4 == 0:
                        half = "ab"[n // 4]
                        act.wait_ge(l1.sem, l1.at(j, half))
                        act.wait_ge(gsp_l.sem, gsp_l.at(j - 1, half))
                    act.activation(gf[:, n, :], bank[1 + n // 4][:, (n % 4) * P:(n % 4 + 1) * P], ACT.Gelu,
                                   bias=col[:, bass.ds(e * KF + (6 + n), 1)], scale=1 / WS).then_inc(gel.sem, 1)

            act.wait_ge(cnt, CNT_DONE)
            expert_x(0, 0)
            with act.Fori(0, NJ // 2 - 1) as i:
                for par in range(2):
                    expert_x(2 * i + par + 1, 1 - par)
                    gelus(2 * i + par, par)
            expert_x(NJ - 1, 1)
            gelus(NJ - 2, 0)
            gelus(NJ - 1, 1)

        @block.vector
        def _(dve):
            v = dve
            for s in (txt, tt_lo, rope, v_lo, kz_ok, mx, nm_lo, pv_h, ynorm, yt_lo, fin, slot, hbs, xsl, gsp_h, gsp_l,
                      yok):
                dve.sem_inc(s.sem, s.head)
            dve.wait_ge(ld_pos, 48)
            v.tensor_tensor(base1[0:IPB * IMG, :], base1[0:IPB * IMG, :], base2[0:IPB * IMG, :], ALU.add).then_inc(img, 1)
            dve.wait_ge(img, 1)
            dve.wait_ge(pool_c, 1)
            for i in range(IT):
                n, m = img_rows(i)
                dve.wait_ge(emb_ps, i + 1)
                v.tensor_tensor(h_img[0:m, i, :], bank[i][0:m, 0:D], base1[0:m, :], ALU.add).then_inc(img, 1)
            for i in range(IT):
                n, m = img_rows(i)
                dve.wait_ge(img, i + 2)
                v.bn_stats(st6[0:m, i, :], h_img[0:m, i, :]).then_inc(img, 1)
            for i in range(IT):
                n, m = img_rows(i)
                dve.wait_ge(img, IT + 2 + i)
                v.bn_aggr(mv[0:m, i, :], st6[0:m, i, :]).then_inc(img, 1)
            dve.wait_ge(img, 3 * IT + 1)
            v.tensor_scalar(veps[:, 0:IT], mv[:, :, 1], EPS, None, ALU.add).then_inc(img, 1)
            dve.wait_ge(img_rs, 1)
            for i in range(IT):
                n, m = img_rows(i)
                v.tensor_scalar(x1[0:m, i, :], h_img[0:m, i, :], mv[0:m, i, 0:1], rstd[0:m, i:i + 1],
                                ALU.subtract, ALU.mult).then_inc(img, 1)
            for i in range(IT):
                n, m = img_rows(i)
                dve.wait_ge(xt_hi, i + 1)
                v.tensor_tensor(xT[:, 1, :, IPB * i:IPB * i + n, 0:IMG],
                                bank[i][:, 0:K2 * m].rearrange("p (k b n) -> p k b n", k=K2, b=n),
                                xT[:, 0, :, IPB * i:IPB * i + n, 0:IMG], ALU.subtract).then_inc(xt_lo, 1)
            dve.wait_ge(wsplit_a, 2)
            v.tensor_tensor(wsl[:, :], wsm[:, :], wsh[:, :], ALU.subtract).then_inc(wsplit_v, 1)
            v.tensor_copy(sel[:, :, :], selcol.unsqueeze(2).to_broadcast([P, HEADS, P])).then_inc(wsplit_v, 1)
            dve.wait_ge(ld_rows, 16)
            v.tensor_tensor(ptype[:, :], ptype[:, :], row("type0"), ALU.add).then_inc(wsplit_v, 1)
            v.tensor_tensor(typd[:, :], row("type1"), row("type0"), ALU.subtract).then_inc(wsplit_v, 1)
            dve.wait_ge(ld_ids, 32)
            v.tensor_copy(types_f[:, :], types_i[:, :]).then_inc(wsplit_v, 1)
            dve.wait_ge(wsplit_v, 5)
            dve.wait_ge(te_in, 16 * B)
            with dve.Fori(0, B // 2) as i:
                def both(x):
                    return x.unsqueeze(1).to_broadcast([P, 2, D])

                h2 = h_txt[:, bass.ds(2 * i, 2), :]
                dve.wait_ge(tt_ps.sem, tt_ps.at(i - 1))
                for k in range(2):
                    hk = h_txt[:, bass.ds(2 * i + k, 1), :].rearrange("p b n -> p (b n)")
                    v.scalar_tensor_tensor(x1[:, k, :], typd[:, :], types_f[:, bass.ds(2 * i + k, 1)], hk,
                                           ALU.mult, ALU.add).then_inc(txt.sem, 1)
                dve.wait_ge(txt.sem, txt.at(i, "e1"))
                v.tensor_tensor(x1[:, 0:2, :], x1[:, 0:2, :], both(ptype[:, :]), ALU.add).then_inc(txt.sem, 1)
                dve.wait_ge(txt.sem, txt.at(i, "e"))
                dve.sem_inc(spare, 1)
                for k in range(2):
                    v.bn_stats(st6[:, k, :], x1[:, k, :]).then_inc(txt.sem, 1)
                for k in range(2):
                    dve.wait_ge(txt.sem, txt.at(i, f"s{k}"))
                    dve.sem_inc(spare, 1)
                    v.bn_aggr(mv[:, k, :], st6[:, k, :]).then_inc(txt.sem, 1)
                dve.wait_ge(txt.sem, txt.at(i, "m1"))
                v.tensor_scalar(veps[:, 0:2], mv[:, 0:2, 1], EPS, None, ALU.add).then_inc(txt.sem, 1)
                dve.wait_ge(txt_rs.sem, txt_rs.at(i, "first"))
                for k in range(2):
                    hk = h_txt[:, bass.ds(2 * i + k, 1), :].rearrange("p b n -> p (b n)")
                    v.tensor_scalar(hk, x1[:, k, :], mv[:, k, 0:1], rstd[:, k:k + 1], ALU.subtract, ALU.mult)\
                     .then_inc(txt.sem, 1)
                dve.wait_ge(txt.sem, txt.at(i, "h1"))
                v.tensor_tensor(h2, h2, both(row("ln_w")), ALU.mult).then_inc(txt.sem, 1)
                dve.wait_ge(txt.sem, txt.at(i, "hw"))
                v.tensor_tensor(h2, h2, both(row("ln_b")), ALU.add).then_inc(txt.sem, 1)
                dve.wait_ge(txt.sem, txt.at(i, "hb"))
                dve.sem_inc(spare, 1)
                for k in range(2):
                    hk = h_txt[:, bass.ds(2 * i + k, 1), :].rearrange("p b n -> p (b n)")
                    v.bn_stats(st6[:, k, :], hk).then_inc(txt.sem, 1)
                for k in range(2):
                    dve.wait_ge(txt.sem, txt.at(i, f"t{k}"))
                    dve.sem_inc(spare, 1)
                    v.bn_aggr(mv[:, k, :], st6[:, k, :]).then_inc(txt.sem, 1)
                dve.wait_ge(txt.sem, txt.at(i, "n1"))
                v.tensor_scalar(veps[:, 2:4], mv[:, 0:2, 1], EPS, None, ALU.add).then_inc(txt.sem, 1)
                dve.wait_ge(txt_rs.sem, txt_rs.at(i, "second"))
                for k in range(2):
                    hk = h_txt[:, bass.ds(2 * i + k, 1), :].rearrange("p b n -> p (b n)")
                    v.tensor_scalar(x1[:, k, :], hk, mv[:, k, 0:1], rstd[:, 2 + k:3 + k], ALU.subtract, ALU.mult)\
                     .then_inc(txt.sem, 1)
                dve.wait_ge(tt_hi.sem, tt_hi.at(i))
                x2 = xT[:, :, :, bass.ds(2 * i, 2), IMG:T]
                v.tensor_tensor(x2[:, 1], bank[3][:, :].rearrange("p (k b n) -> p k b n", k=K2, b=2), x2[:, 0],
                                ALU.subtract).then_inc(tt_lo.sem, 1)

            def project(b, par, half):
                for a, (bk, one, two) in enumerate(((bQ, "qe", "qo"), (bK, "ke", "ko"))):
                    dve.wait_ge(qkv.sem, qkv.at(b, "qk"[a]))
                    if a == 0:
                        dve.wait_ge(rope_hi.sem, rope_hi.at(b - 1))
                    v.scalar_tensor_tensor(rot_a[:, a, :], bk[:, 0:T], bqk64[:, 2 * a:2 * a + 1], cosw, ALU.add, ALU.mult)\
                     .then_inc(rope.sem, 1)
                    v.scalar_tensor_tensor(rot_b[:, a, :], bk[:, T:2 * T], bqk64[:, 2 * a + 1:2 * a + 2], sinw,
                                           ALU.add, ALU.mult).then_inc(rope.sem, 1)
                dve.wait_ge(rope.sem, rope.at(b, "ko"))
                v.tensor_tensor(rot[:, :, :], rot_a[:, :, :], rot_b[:, :, :], ALU.subtract).then_inc(rope.sem, 1)
                dve.wait_ge(v_hi.sem, v_hi.at(b))
                v.scalar_tensor_tensor(vl[par][:, :, 0:HD], bV[:, 0:D].rearrange("p (h n) -> p h n", h=HEADS), 1 / WS,
                                       vh[par][:, :, 0:HD], ALU.mult, ALU.subtract).then_inc(v_lo.sem, 1)
                v.scalar_tensor_tensor(vl2[par][:, :, 0:HD], bV[0:Q2, D:2 * D].rearrange("p (h n) -> p h n", h=HEADS),
                                       1 / WS, vh2[par][:, :, 0:HD], ALU.mult, ALU.subtract).then_inc(v_lo.sem, 1)
                dve.wait_ge(rope_hi.sem, rope_hi.at(b))
                if not isinstance(half, int) or half > 0:
                    dve.wait_ge(scr_w[par], half * 16)
                v.tensor_tensor(parts[par][:, 1, :, :], rot[:, :, :], parts[par][:, 0, :, :], ALU.subtract)\
                 .then_inc(rope.sem, 1)

            def spread(b, par, half):
                dve.wait_ge(stk_in[par], 128 * (Steps.LEAD + 1) + half * 128)
                dve.wait_ge(sps.sem, sps.at(b - 2))
                kv = kz[par][:, :, :].rearrange("p (g h) n -> p g h n", g=GRP)
                for h in range(GRP):
                    v.tensor_scalar(kv[:, :, h, :], stk[par][:, 1, :, :], headmask[:, h:h + 1], None, ALU.mult)\
                     .then_inc(kz_ok.sem, 1)

            def maxima(b, par):
                for g in range(GRP):
                    dve.wait_ge(mps.sem, mps.at(b, f"a{g}"))
                    if g == 0:
                        dve.wait_ge(mps.sem, mps.at(b - 1))
                    v.tensor_reduce(mx_a[:, GRP * g:GRP * g + GRP], bM[0][:, :].rearrange("p (h n) -> p h n", h=GRP),
                                    AX.X, ALU.max).then_inc(mx.sem, 1)
                    dve.wait_ge(mps.sem, mps.at(b, f"b{g}"))
                    v.tensor_reduce(mx_b[:, g, :], bM[1][:, 0:2 * T].rearrange("p (h n) -> p h n", h=2),
                                    AX.X, ALU.max).then_inc(mx.sem, 1)
                dve.wait_ge(mx.sem, mx.at(b, "b3"))
                for u in range(2):
                    v.tensor_copy(mx_w[QB * u:QB * u + QB, :, u, :], mx_b[QB * u:QB * u + QB, :, :]).then_inc(mx.sem, 1)
                dve.wait_ge(nm_hi.sem, nm_hi.at(b))
                dve.wait_ge(sps.sem, sps.at(b - 2))
                v.scalar_tensor_tensor(nm[par][32:32 + HEADS, :], bM[0][0:HEADS, 0:T], -1.0, nm[par][0:HEADS, :],
                                       ALU.mult, ALU.subtract).then_inc(nm_lo.sem, 1)

            def attend(b, par, middle):
                for n, (name, h0, hn) in enumerate(chunks):
                    dve.wait_ge(ex.sem, ex.at(b, name))
                    if n == 0:
                        dve.wait_ge(yps.sem, yps.at(b - 1))
                    if name[0] == "d":
                        v.tensor_copy(ph2[:, h0:h0 + hn, :], pf[n % 2][0:Q2, 0:hn * Q2]
                                      .rearrange("p (h n) -> p h n", h=hn)).then_inc(pv_h.sem, 1)
                    else:
                        v.tensor_copy(ph[:, h0:h0 + hn, :], pf[n % 2][:, 0:hn * T]
                                      .rearrange("p (h n) -> p h n", h=hn)).then_inc(pv_h.sem, 1)
                middle()
                dve.wait_ge(yps.sem, yps.at(b))
                y1 = bY[:, 0:HEADS * (HD + 1)].rearrange("p (h n) -> p h n", h=HEADS)
                y2 = bK[0:Q2, 0:HEADS * (HD + 1)].rearrange("p (h n) -> p h n", h=HEADS)
                v.reciprocal(rden[:, 0, :], y1[:, :, HD]).then_inc(ynorm.sem, 1)
                v.reciprocal(rden[0:Q2, 1, :], y2[:, :, HD]).then_inc(ynorm.sem, 1)
                dve.wait_ge(ytp.sem, ytp.at(b - 1))
                dve.wait_ge(ynorm.sem, ynorm.at(b, "r1"))
                v.tensor_tensor(yn[:, :].rearrange("p (h n) -> p h n", h=HEADS), y1[:, :, 0:HD],
                                rden[:, 0, :].unsqueeze(2).to_broadcast([P, HEADS, HD]), ALU.mult).then_inc(ynorm.sem, 1)
                dve.wait_ge(ynorm.sem, ynorm.at(b, "r2"))
                v.tensor_tensor(yn2[:, :].rearrange("p (h n) -> p h n", h=HEADS), y2[:, :, 0:HD],
                                rden[0:Q2, 1, :].unsqueeze(2).to_broadcast([Q2, HEADS, HD]), ALU.mult)\
                 .then_inc(ynorm.sem, 1)
                dve.wait_ge(yt_hi.sem, yt_hi.at(b))
                for k in range(K2):
                    v.scalar_tensor_tensor(yT[:, 1, k, :], bV[:, k * T:(k + 1) * T], col[:, 4 + k:5 + k], yT[:, 0, k, :],
                                           ALU.add, ALU.subtract).then_inc(yt_lo.sem, 1)

            def finish(r, par, kept, residual, m=P):
                dve.wait_ge(wops.sem, wops.at(r))
                dve.wait_ge(store[par], kept)
                hr = rows[par][0:m, D:2 * D]
                xr = rows[par][0:m, 0:D]
                v.scalar_tensor_tensor(hr, bQ[0:m, 0:D], 1 / WS, residual, ALU.mult, ALU.add).then_inc(fin.sem, 1)
                dve.wait_ge(fin.sem, fin.at(r, "h"))
                dve.sem_inc(spare, 1)
                v.bn_stats(g6[0:m, :], hr).then_inc(fin.sem, 1)
                dve.wait_ge(fin.sem, fin.at(r, "s"))
                dve.wait_ge(fin_rs.sem, fin_rs.at(r - 1))
                dve.sem_inc(spare, 1)
                v.bn_aggr(gmv[0:m, :], g6[0:m, :]).then_inc(fin.sem, 1)
                dve.wait_ge(fin_rs.sem, fin_rs.at(r))
                v.tensor_scalar(xr, hr, gmv[0:m, 0:1], grs[0:m, :], ALU.subtract, ALU.mult).then_inc(fin.sem, 1)
                dve.wait_ge(fin.sem, fin.at(r, "x"))
                for e in range(NE):
                    v.tensor_tensor_reduce(out=junk[0:m, e, :], in0=xr, in1=rb[0:m, RB["wg"] + e * D:RB["wg"] + (e + 1) * D],
                                           scale=1.0, scalar=0.0, op0=ALU.mult, op1=ALU.add,
                                           accum_out=logit[0:m, e:e + 1]).then_inc(fin.sem, 1)
                dve.wait_ge(fin.sem, fin.at(r, "g3"))
                v.tensor_tensor(logb[0:m, :], logit[0:m, :], rb[0:m, RB["bg"]:RB["bg"] + NE], ALU.add).then_inc(fin.sem, 1)
                dve.wait_ge(fin.sem, fin.at(r, "l"))
                v.tensor_reduce(gmax[0:m, :], logb[0:m, :], AX.X, ALU.max).then_inc(fin.sem, 1)
                dve.wait_ge(fin.sem, fin.at(r, "lm"))
                v.scalar_tensor_tensor(pick[0:m, :], logb[0:m, :], gmax[0:m, :], order[0:m, :], ALU.is_ge, ALU.mult)\
                 .then_inc(fin.sem, 1)
                dve.wait_ge(fin.sem, fin.at(r, "p"))
                v.tensor_reduce(pmax[0:m, :], pick[0:m, :], AX.X, ALU.max).then_inc(fin.sem, 1)
                dve.wait_ge(rk_ps.sem, rk_ps.at(r - 2))
                dve.wait_ge(slot.sem, slot.at(r - 2))
                v.memset(ohc[par][:, :], 0.0).then_inc(fin.sem, 1)
                dve.wait_ge(fin.sem, fin.at(r, "z"))
                v.tensor_scalar(ohc[par][0:m, :], pick[0:m, :], pmax[0:m, :], None, ALU.is_equal).then_inc(fin.sem, 1)

            def slots(r, par, half):
                dve.wait_ge(rk_ps.sem, rk_ps.at(r))
                v.tensor_tensor(sl4[:, :], bM[1][:, 0:NE], ebase, ALU.add).then_inc(slot.sem, 1)
                dve.wait_ge(slot.sem, slot.at(r, "a"))
                v.tensor_tensor_reduce(out=sl4b[:, :], in0=sl4[:, :], in1=ohc[par][:, :], scale=1.0, scalar=0.0,
                                       op0=ALU.mult, op1=ALU.add, accum_out=slotf[:, :]).then_inc(slot.sem, 1)
                dve.wait_ge(slot.sem, slot.at(r, "s"))
                if not isinstance(half, int) or half > 0:
                    dve.wait_ge(scat[par], half * 16)
                v.tensor_copy(sloti[par][:, :], slotf[:, :]).then_inc(slot.sem, 1)
                v.tensor_tensor(ohsum[:, :], ohsum[:, :], ohc[par][:, :], ALU.add).then_inc(slot.sem, 1)

            def text_rows(b):
                return h_txt[:, bass.ds(b, 1), :].rearrange("p b n -> p (b n)")

            L = Steps.LEAD
            dve.wait_ge(wsplit_a, 3)
            dve.wait_ge(ld_c, 16)
            project(0, 0, 0)
            spread(0, 0, 0)
            maxima(0, 0)
            project(1, 1, 0)
            attend(0, 0, lambda: spread(1, 1, 0))
            maxima(1, 1)
            dve.wait_ge(txt_rs.sem, txt_rs.at(B // 2 - 1))
            finish(0, 0, 16 * L, text_rows(0))
            for_pairs = dve.Fori(0, 3)
            with for_pairs as i:
                for par in (1, 0):
                    t = 2 * i + (2 - par)
                    nxt, cur = i + 1, (i if par else i + 1)
                    project(t + 1, 1 - par, nxt)
                    slots(t - 1, 1 - par, i)
                    attend(t, par, lambda t=t, par=par, nxt=nxt: spread(t + 1, 1 - par, nxt))
                    maxima(t + 1, 1 - par)
                    finish(t, par, 16 * L + cur * 16, text_rows(t))
            slots(6, 0, 3)
            attend(7, 1, lambda: None)
            finish(7, 1, 16 * (L + 3), text_rows(7))
            KEPT = {8: L + 4, 9: L + 4, 10: L + 4 + IPB}
            for i in range(IT):
                r = B + i
                slots(r - 1, (r - 1) % 2, (r - 1) // 2)
                n, m = img_rows(i)
                if i == 0:
                    dve.wait_ge(img_rs, 1 + IT)
                finish(r, r % 2, 16 * KEPT[r], h_img[0:m, i, :], m)
            slots(B + IT - 1, (B + IT - 1) % 2, (B + IT - 1) // 2)

            def link(ins, n):
                ins.then_inc(cnt, 1)
                dve.wait_ge(cnt, n)

            dve.wait_ge(cnt_ps, 1)
            link(v.tensor_scalar(nf[:, :], bM[0][0:1, 0:NE], float(P - 1), None, ALU.add), 1)
            link(v.tensor_copy(ni[:, :], nf[:, :]), 2)
            link(v.tensor_scalar(ni[:, :], ni[:, :], 7, None, ALU.arith_shift_right), 3)
            link(v.tensor_copy(nt[:, :], ni[:, :]), 4)
            link(v.tensor_copy(cum[:, 0:1], nt[:, 0:1]), 5)
            link(v.tensor_tensor(cum[:, 1:2], cum[:, 0:1], nt[:, 1:2], ALU.add), 6)
            link(v.tensor_tensor(cum[:, 2:3], cum[:, 1:2], nt[:, 2:3], ALU.add), 7)
            jr = jrow[0:1, :]
            link(v.tensor_tensor(ge[:, :, :], jr.unsqueeze(1).to_broadcast([1, 3, NJ]),
                                 cum[:, 0:3].unsqueeze(2).to_broadcast([1, 3, NJ]), ALU.is_ge), 8)
            link(v.tensor_reduce(tex[:, 1, :], ge[:, :, :].rearrange("p e j -> p j e"), AX.X, ALU.add), 9)
            link(v.tensor_tensor(ge[:, :, :], ge[:, :, :], nt[:, 0:3].unsqueeze(2).to_broadcast([1, 3, NJ]), ALU.mult), 10)
            link(v.tensor_reduce(tex[:, 0, :], ge[:, :, :].rearrange("p e j -> p j e"), AX.X, ALU.add), 11)
            link(v.tensor_tensor(tex[:, 0, :], jr, tex[:, 0, :], ALU.subtract), 12)
            link(v.scalar_tensor_tensor(tex[:, 0, :], tex[:, 1, :], float(CAP), tex[:, 0, :], ALU.mult, ALU.add), 13)
            link(v.tensor_copy(tei[:, :, :], tex[:, :, :]), 14)
            dve.wait_ge(tab_ps, 1)
            link(v.tensor_copy(tabo[:, :], bM[1][:, 0:NTAB]), 15)
            link(v.tensor_scalar(tabT[:, :], bM[1][:, 0:NTAB], float(B * T - 1), None, ALU.min), 16)
            link(v.tensor_copy(tabg[:, :], tabT[:, :]), 17)

            def expert_x(j, par, half):
                dve.wait_ge(xsh.sem, xsh.at(j))
                v.tensor_tensor(xs[par][:, 1, :, :], bank[0][:, 0:D].rearrange("p (k n) -> p k n", k=K2),
                                xs[par][:, 0, :, :], ALU.subtract).then_inc(xsl.sem, 1)
                e = dve.value_load(tei[0:1, 1, bass.ds(j, 1)], min_val=0, max_val=NE - 1)
                dve.wait_ge(gat[par], 16 + 16 * half)
                v.tensor_tensor(hb[par][:, :], xg[par][:, D:2 * D], rb[:, bass.ds(e * D + RB["b2"], D)], ALU.add)\
                 .then_inc(hbs.sem, 1)

            def split(j, par):
                for n, half in enumerate("ab"):
                    s = slice(4 * n, 4 * n + 4)
                    dve.wait_ge(gel.sem, gel.at(j, f"g{4 * n + 3}"))
                    dve.wait_ge(l2.sem, l2.at(j - 2))
                    v.tensor_copy(gh[par][:, s, :], gf[:, s, :]).then_inc(gsp_h.sem, 1)
                    dve.wait_ge(gsp_h.sem, gsp_h.at(j, half))
                    v.tensor_tensor(gl[par][:, s, :], gf[:, s, :], gh[par][:, s, :], ALU.subtract).then_inc(gsp_l.sem, 1)

            def result(j, par, half):
                dve.wait_ge(l2.sem, l2.at(j))
                if not isinstance(half, int) or half > 0:
                    dve.wait_ge(osc[par], half * 16)
                v.scalar_tensor_tensor(yo[par][:, :], bank[5 + par][:, 0:D], 1 / WS, hb[par][:, :], ALU.mult, ALU.add)\
                 .then_inc(yok.sem, 1)

            expert_x(0, 0, 0)
            expert_x(1, 1, 0)
            split(0, 0)
            with dve.Fori(0, NJ // 2 - 1) as i:
                for par in (1, 0):
                    j = 2 * i + (2 - par)
                    if par:
                        result(j - 1, 0, i)
                        expert_x(j + 1, 0, i + 1)
                    else:
                        result(j - 1, 1, i)
                        expert_x(j + 1, 1, i + 1)
                    split(j, par)
            result(NJ - 2, 0, NJ // 2 - 1)
            split(NJ - 1, 1)
            result(NJ - 1, 1, NJ // 2 - 1)

        @block.tensor
        def _(pe):
            mm = nc.tensor.matmul
            for s in (tt_ps, qkv, mps, sps, yps, ytp, wops, rk_ps, xtp, l1, l2):
                pe.sem_inc(s.sem, s.head)
            pe.wait_ge(ld_x, 32 * KP)
            for i in range(IT):
                n, m = img_rows(i)
                for k in range(KP):
                    last = mm(bank[i][0:m, 0:D], xp[:, k, IPB * i * IMG:IPB * i * IMG + m], wp[:, k, :],
                              start=k == 0, stop=k == KP - 1)
                last.then_inc(emb_ps, 1)
            pe.wait_ge(ld_c, 16)
            for i in range(IT):
                n, m = img_rows(i)
                pe.wait_ge(img, 3 * IT + 3 + i)
                for k in range(K2):
                    last = nc.tensor.transpose(bank[i][:, k * m:(k + 1) * m], x1[0:m, i, k * P:(k + 1) * P],
                                               ident[0:m, 0:m])
                last.then_inc(xt_ps, 1)
            with pe.Fori(0, B // 2) as i:
                pe.wait_ge(tt_lo.sem, tt_lo.at(i - 1))
                for b in range(2):
                    pe.wait_ge(txt.sem, txt.at(i, f"x{b}"))
                    for k in range(K2):
                        last = nc.tensor.transpose(bank[3][:, (2 * k + b) * P:(2 * k + b + 1) * P],
                                                   x1[:, b, k * P:(k + 1) * P], ident)
                last.then_inc(tt_ps.sem, 1)

            qkh, qkl = small(wsh, 0, 4 * P), small(wsl, 0, 4 * P)
            vwh, vwl = small(wsh, K2 * 4 * P, D), small(wsl, K2 * 4 * P, D)
            owh, owl = small(wsh, K2 * (4 * P + D), D), small(wsl, K2 * (4 * P + D), D)

            def project(b, par):
                xh, xl = ([xT[:, a, k, bass.ds(b, 1), :].rearrange("p b n -> p (b n)") for k in range(K2)] for a in range(2))
                pe.wait_ge(fin.sem, fin.at(b - 2, "h"))
                for a, bk in enumerate((bQ, bK)):
                    if a == 1:
                        pe.wait_ge(ynorm.sem, ynorm.at(b - 2))
                    for eo in range(2):
                        m = 2 * a + eo
                        for k in range(K2):
                            for c, (w, x) in enumerate(((qkh, xh), (qkl, xh), (qkh, xl))):
                                last = mm(bk[:, eo * T:(eo + 1) * T], w[:, k, m * P:(m + 1) * P], x[k],
                                          start=k == 0 and c == 0, stop=k == K2 - 1 and c == 2)
                    last.then_inc(qkv.sem, 1)
                pe.wait_ge(yt_lo.sem, yt_lo.at(b - 2))
                for s in range(2):
                    o = bV[:, 0:D] if s == 0 else bV[0:Q2, D:2 * D]
                    for k in range(K2):
                        for c, (a, w) in enumerate(((0, vwh), (0, vwl), (1, vwh))):
                            x = xT[:, a, k, bass.ds(b, 1), (0 if s == 0 else P):(P if s == 0 else T)]\
                                .rearrange("p b n -> p (b n)")
                            last = mm(o, x, w[:, k, :], start=k == 0 and c == 0, stop=k == K2 - 1 and c == 2)
                last.then_inc(qkv.sem, 1)

            def maxima(b, par):
                pe.wait_ge(kz_ok.sem, kz_ok.at(b))
                for g in range(GRP):
                    if g == 0:
                        pe.wait_ge(nm_lo.sem, nm_lo.at(b - 1))
                    else:
                        pe.wait_ge(mx.sem, mx.at(b, f"a{g - 1}"))
                    mm(bM[0][:, :], identb, mask_a.unsqueeze(1).to_broadcast([P, GRP, P]), start=True, stop=False)
                    mm(bM[0][:, :], stk[par][:, 0, g, 0:P], kz[par][:, GRP * g:GRP * g + GRP, 0:P], start=False, stop=True)\
                        .then_inc(mps.sem, 1)
                    if g == 0:
                        pe.wait_ge(slot.sem, slot.at(b - 2, "a"))
                    else:
                        pe.wait_ge(mx.sem, mx.at(b, f"b{g - 1}"))
                    mm(bM[1][:, 0:2 * T], identb, mask_b.unsqueeze(1).to_broadcast([P, 2, T]), start=True, stop=False,
                       skip_group_check=True)
                    for u in range(2):
                        last = mm(bM[1][QB * u:QB * u + QB, 0:2 * T], stk[par][:, 0, g, QB0:T],
                                  kz[par][:, GRP * g + 2 * u:GRP * g + 2 * u + 2, :], start=False, stop=True,
                                  skip_group_check=True)
                    last.then_inc(mps.sem, 1)
                pe.wait_ge(mx.sem, mx.at(b, "w1"))
                mm(bM[0][0:HEADS, 0:P], mx_a[:, :], ident, start=True, stop=True)
                mm(bM[0][0:HEADS, P:T], mx_w[:, :, :, :].rearrange("p g u e -> p (g u e)"), fold[:, QB - Q2:QB],
                   start=True, stop=True).then_inc(mps.sem, 1)

            def attend(b, par, nxt):
                pe.wait_ge(nm_lo.sem, nm_lo.at(b))

                def products(name, h0, hn):
                    pe.wait_ge(pv_l.sem, pv_l.at(b, name))
                    if name == "c0":
                        pe.wait_ge(ynorm.sem, ynorm.at(b - 1))
                        if nxt:
                            pe.wait_ge(rope.sem, rope.at(b + 1, "ko"))
                    for h in range(h0, h0 + hn):
                        o1 = bY[:, h * (HD + 1):(h + 1) * (HD + 1)]
                        mm(o1, ph[:, h, 0:P], vh[par][:, h, :], start=True, stop=False)
                        mm(o1, ph[:, h, 0:P], vl[par][:, h, :], start=False, stop=False)
                        mm(o1, pl[:, h, 0:P], vh[par][:, h, :], start=False, stop=True)
                        o2 = bK[0:Q2, h * (HD + 1):(h + 1) * (HD + 1)]
                        mm(o2, ph[:, h, P:T], vh[par][:, h, :], start=True, stop=False)
                        mm(o2, ph[:, h, P:T], vl[par][:, h, :], start=False, stop=False)
                        mm(o2, pl[:, h, P:T], vh[par][:, h, :], start=False, stop=False)
                        mm(o2, ph2[:, h, :], vh2[par][:, h, :], start=False, stop=False)
                        mm(o2, ph2[:, h, :], vl2[par][:, h, :], start=False, stop=False)
                        last = mm(o2, pl2[:, h, :], vh2[par][:, h, :], start=False, stop=True)
                    return last

                for n, (name, h0, hn) in enumerate(chunks):
                    back = chunks[n - 2][0]
                    pe.wait_ge(ex.sem, ex.at(b if n >= 2 else b - 1, back))
                    o = bS[n % 2]
                    if name[0] == "d":
                        pe.sem_inc(spare, 1)
                        mm(o[0:Q2, 0:hn * Q2], identb[0:Q2, 0:Q2], mask_t2[0:Q2, :].unsqueeze(1).to_broadcast([Q2, hn, Q2]),
                           start=True, stop=False)
                    else:
                        mm(o[:, 0:hn * T], identb, mask_t.unsqueeze(1).to_broadcast([P, hn, T]), start=True, stop=False)
                    for h in range(h0, h0 + hn):
                        j = h - h0
                        if name[0] == "d":
                            oj, kk, qq = o[0:Q2, j * Q2:(j + 1) * Q2], slice(P, T), slice(P, T)
                        else:
                            oj, kk, qq = o[:, j * T:(j + 1) * T], slice(0, P), slice(0, T)
                        mm(oj, sel[:, h, 0:kk.stop - kk.start], nm[par][:, qq], start=False, stop=False)
                        last = mm(oj, kz[par][:, h, kk], stk[par][:, 0, h // GRP, qq], start=False, stop=h == h0 + hn - 1)
                    last.then_inc(sps.sem, 1)
                    if n >= 4:
                        products(*chunks[n - 2])
                products(*chunks[-2])
                products(*chunks[-1]).then_inc(yps.sem, 1)

            def turn(b, nxt):
                pe.wait_ge(ynorm.sem, ynorm.at(b))
                if nxt:
                    pe.wait_ge(v_lo.sem, v_lo.at(b + 1))
                for k in range(K2):
                    nc.tensor.transpose(bV[:, k * T:k * T + P], yn[:, k * P:(k + 1) * P], ident)
                    last = nc.tensor.transpose(bV[:, k * T + P:(k + 1) * T], yn2[:, k * P:(k + 1) * P],
                                               ident[0:Q2, 0:Q2])
                last.then_inc(ytp.sem, 1)

            def finish(r, nxt, at, m=P):
                if nxt:
                    pe.wait_ge(rope.sem, rope.at(r + 1, "qo"))
                for k in range(K2):
                    for c, (a, w) in enumerate(((0, owh), (0, owl), (1, owh))):
                        last = mm(bQ[0:m, 0:D], at(a, k), w[:, k, :], start=k == 0 and c == 0, stop=k == K2 - 1 and c == 2)
                last.then_inc(wops.sem, 1)

            def text_y(a, k):
                return yT[:, a, k, IMG:T]

            def rank(r, par):
                pe.wait_ge(fin.sem, fin.at(r, "oh"))
                pe.wait_ge(slot.sem, slot.at(r - 1))
                mm(bM[1][:, 0:NE], before, ohc[par][:, :], start=True, stop=False)
                mm(bM[1][:, 0:NE], onesb, ohsum[:, :], start=False, stop=True).then_inc(rk_ps.sem, 1)

            pe.wait_ge(wsplit_v, 2)
            pe.wait_ge(ld_small, 48)
            pe.wait_ge(pool_c, 1)
            pe.wait_ge(xt_lo, IT)
            pe.wait_ge(tt_lo.sem, tt_lo.at(B // 2 - 1))
            project(0, 0)
            maxima(0, 0)
            project(1, 1)
            attend(0, 0, True)
            turn(0, True)
            maxima(1, 1)
            pe.wait_ge(yt_lo.sem, yt_lo.at(0))
            finish(0, True, text_y)
            with pe.Fori(0, 3) as i:
                for par in (1, 0):
                    t = 2 * i + (2 - par)
                    project(t + 1, 1 - par)
                    rank(t - 1, 1 - par)
                    attend(t, par, True)
                    turn(t, True)
                    maxima(t + 1, 1 - par)
                    pe.wait_ge(yt_lo.sem, yt_lo.at(t))
                    finish(t, True, text_y)
            rank(6, 0)
            attend(7, 1, False)
            turn(7, False)
            pe.wait_ge(yt_lo.sem, yt_lo.at(7))
            pe.wait_ge(fin.sem, fin.at(6, "h"))
            finish(7, False, text_y)
            pe.wait_ge(yti.sem, yti.at(7))
            for i in range(IT):
                n, m = img_rows(i)
                pe.wait_ge(fin.sem, fin.at(B + i - 1, "h"))
                finish(B + i, False, lambda a, k, i=i, n=n: yTi[:, K2 * a + k, IPB * i:IPB * i + n, :]
                       .rearrange("p b n -> p (b n)"), m)
                rank(B + i - 1, (B + i - 1) % 2)
            rank(B + IT - 1, (B + IT - 1) % 2)
            pe.wait_ge(slot.sem, slot.at(B + IT - 1))
            mm(bM[0][0:1, 0:NE], onesb[:, 0:1], ohsum[:, :], start=True, stop=True).then_inc(cnt_ps, 1)
            pe.wait_ge(tab_in, 16)
            nc.tensor.transpose(bM[1][:, 0:NTAB], tab[:, :], ident[0:NTAB, 0:NTAB]).then_inc(tab_ps, 1)

            def expert_x(j, par, half):
                pe.wait_ge(gat[par], 16 + 16 * half)
                pe.wait_ge(xsl.sem, xsl.at(j - 1))
                for k in range(K2):
                    last = nc.tensor.transpose(bank[0][:, k * P:(k + 1) * P], xg[par][:, k * P:(k + 1) * P], ident)
                last.then_inc(xtp.sem, 1)

            def first(j, par):
                e = pe.value_load(tei[0:1, 1, bass.ds(j, 1)], min_val=0, max_val=NE - 1)
                pe.wait_ge(xsl.sem, xsl.at(j))
                for n in range(KF):
                    if n % 4 == 0:
                        pe.wait_ge(gel.sem, gel.at(j - 1, f"g{n + 3}"))
                    for k in range(K2):
                        at = e * WN + (k * FF + n * P)
                        o = bank[1 + n // 4][:, (n % 4) * P:(n % 4 + 1) * P]
                        mm(o, w1h[:, bass.ds(at, P)], xs[par][:, 0, k, :], start=k == 0, stop=False)
                        mm(o, w1h[:, bass.ds(at, P)], xs[par][:, 1, k, :], start=False, stop=False)
                        last = mm(o, w1l[:, bass.ds(at, P)], xs[par][:, 0, k, :], start=False, stop=k == K2 - 1)
                    if n % 4 == 3:
                        last.then_inc(l1.sem, 1)

            def second(j, par):
                e = pe.value_load(tei[0:1, 1, bass.ds(j, 1)], min_val=0, max_val=NE - 1)
                pe.wait_ge(yok.sem, yok.at(j - 2))
                o = bank[5 + par][:, 0:D]
                for n in range(KF):
                    if n % 4 == 0:
                        pe.wait_ge(gsp_l.sem, gsp_l.at(j, "ab"[n // 4]))
                    at = e * WN + n * D
                    mm(o, gh[par][:, n, :], w2h[:, bass.ds(at, D)], start=n == 0, stop=False)
                    mm(o, gl[par][:, n, :], w2h[:, bass.ds(at, D)], start=False, stop=False)
                    last = mm(o, gh[par][:, n, :], w2l[:, bass.ds(at, D)], start=False, stop=n == KF - 1)
                last.then_inc(l2.sem, 1)

            pe.wait_ge(cnt, CNT_DONE)
            pe.wait_ge(wlo.sem, wlo.at(B - 1))
            expert_x(0, 0, 0)
            first(0, 0)
            expert_x(1, 1, 0)
            with pe.Fori(0, NJ // 2 - 1) as i:
                for par in (1, 0):
                    j = 2 * i + (2 - par)
                    first(j, par)
                    second(j - 1, 1 - par)
                    expert_x(j + 1, 1 - par, i + 1)
            first(NJ - 1, 1)
            second(NJ - 2, 0)
            second(NJ - 1, 1)


CNT_DONE = 17


def layout(parts):
    at, n = {}, 0
    for name, width in parts:
        at[name] = n
        n += width
    return at, n


CF, CF_N = layout([("ident", P), ("cos", T), ("sin", T), ("fold", QB), ("headmask", GRP), ("rowid", TILES),
                   ("ebase", NE), ("order", NE), ("jrow", NJ)])
CB, CB_N = layout([("ident", P), ("mask_a", P), ("mask_b", T), ("mask_t", T), ("mask_t2", Q2), ("before", P),
                   ("ones", P), ("sel", HEADS)])
RB, ROWS = layout([("ln_w", D), ("ln_b", D), ("bo", D), ("type0", D), ("type1", D), ("wg", NE * D), ("b2", NE * D),
                   ("bg", NE)])
W_SMALL = K2 * (4 * P + 2 * D)
COLS = 4 + K2 + NE * KF


def constants():
    p = np.arange(P)
    f = np.zeros((P, CF_N), np.float32)
    f[:, CF["ident"]:CF["ident"] + P] = np.eye(P)
    t = np.arange(1, T + 1, dtype=np.float32)
    i = np.arange(ROT, dtype=np.float32)
    theta = np.power(np.float32(1.0 / 10000.0), np.float32(2.0) * i / np.float32(HD)).astype(np.float32)
    ang = t[None, :] * theta[p % ROT][:, None]
    f[:, CF["cos"]:CF["cos"] + T] = np.cos(ang) / WS
    f[:, CF["sin"]:CF["sin"] + T] = np.sin(ang) / WS
    f[:, CF["fold"]:CF["fold"] + QB] = p[:, None] % QB == np.arange(QB)[None, :]
    f[:, CF["headmask"]:CF["headmask"] + GRP] = (p[:, None] // ROT) % GRP == np.arange(GRP)[None, :]
    for b in range(B):
        f[:, CF["rowid"] + b] = b * T + IMG + p
    for j in range(IT):
        f[:, CF["rowid"] + B + j] = (IPB * j + p // IMG) * T + p % IMG
    f[:, CF["ebase"]:CF["ebase"] + NE] = np.arange(NE) * SLOTS
    f[:, CF["order"]:CF["order"] + NE] = NE - np.arange(NE)
    f[:, CF["jrow"]:CF["jrow"] + NJ] = np.arange(NJ)
    c = np.zeros((P, CB_N), np.float32)
    neg = np.float32(-4e10)
    c[:, CB["ident"]:CB["ident"] + P] = np.eye(P)
    c[:, CB["mask_a"]:CB["mask_a"] + P] = np.where(p[None, :] > p[:, None], neg, 0)
    key, query = np.arange(T), np.arange(T)
    c[:, CB["mask_b"]:CB["mask_b"] + T] = np.where(key[None, :] > QB0 + p[:, None] % QB, neg, 0)
    c[:, CB["mask_t"]:CB["mask_t"] + T] = np.where(p[:, None] > query[None, :], neg, 0)
    c[:, CB["mask_t2"]:CB["mask_t2"] + Q2] = np.where(p[:, None] > np.arange(Q2)[None, :], neg, 0)
    c[:, CB["before"]:CB["before"] + P] = p[:, None] < p[None, :]
    c[:, CB["ones"]:CB["ones"] + P] = 1
    c[:, CB["sel"]:CB["sel"] + HEADS] = (p[:, None] % 32 == np.arange(HEADS)[None, :]) & (p[:, None] < 64)
    bits = (c.view(np.uint32) >> 16).astype(np.uint16)
    return f, bits, np.full((NE * CAP, P), NONE, np.float32)


def kernel(x, x_txt, mask_BS_i1_0, L0_tok_W, L0_tok_b, L0_tok_cls_token, L0_tok_pos_embedding, L0_txt_token_W,
           L0_txt_pos_W, L0_txt_type_W, L0_txt_ln_w, L0_txt_ln_b, L0_attn_Wq, L0_attn_bq, L0_attn_Wk, L0_attn_bk,
           L0_attn_Wv, L0_attn_bv, L0_attn_Wo, L0_attn_bo, L0_ffn_W1, L0_ffn_b1, L0_ffn_W2, L0_ffn_b2, L0_ffn_Wg,
           L0_ffn_bg):
    import concourse.bacc as bacc
    from concourse.bass_utils import run_bass_kernel_spmd

    a = {k: np.asarray(v) for k, v in locals().items() if k[0] in "xmL"}

    def blocks(w):
        return np.ascontiguousarray(w.reshape(-1, P, w.shape[1]).transpose(1, 0, 2))

    s = 96 // 16
    pt = a["x"].reshape(B, 3, s, 16, s, 16).transpose(1, 3, 5, 0, 2, 4).reshape(PDIM, B, PATCHES)
    pt = np.concatenate([np.zeros((PDIM, B, 1), pt.dtype), pt], axis=2).reshape(PDIM, B * IMG)
    pos = a["L0_tok_pos_embedding"][0]
    add = np.concatenate([a["L0_tok_cls_token"][0], np.tile(a["L0_tok_b"][None], (PATCHES, 1))])

    def even_odd(w):
        w = w.reshape(HEADS, ROT, 2, -1)
        return [w[:, :, j].reshape(P, -1) for j in range(2)]

    qk = np.concatenate(even_odd(a["L0_attn_Wq"]) + even_odd(a["L0_attn_Wk"])).T
    w_small = np.concatenate([blocks(w).reshape(P, -1) for w in (qk, a["L0_attn_Wv"].T, a["L0_attn_Wo"].T)], axis=1)
    cols = np.concatenate(even_odd(a["L0_attn_bq"]) + even_odd(a["L0_attn_bk"])
                          + [a["L0_attn_bv"].reshape(K2, P).T, a["L0_ffn_b1"].reshape(NE * KF, P).T], axis=1)
    rows = {"ln_w": a["L0_txt_ln_w"], "ln_b": a["L0_txt_ln_b"], "bo": a["L0_attn_bo"], "type0": a["L0_txt_type_W"][0],
            "type1": a["L0_txt_type_W"][1], "wg": a["L0_ffn_Wg"].T, "b2": a["L0_ffn_b2"], "bg": a["L0_ffn_bg"]}
    f, bits, none = constants()
    arrays = {
        "tok_tab": a["L0_txt_token_W"], "patches": blocks(pt), "w_patch": blocks(a["L0_tok_W"].T),
        "base_pos": np.tile(pos, (IPB, 1)), "base_add": np.tile(add, (IPB, 1)), "pos_txt": a["L0_txt_pos_W"],
        "ids": a["x_txt"].T, "types": a["mask_BS_i1_0"].T, "w_small": w_small, "cols": cols,
        "rows_b": np.concatenate([rows[k].reshape(-1) for k in RB]), "w1": a["L0_ffn_W1"], "w2": a["L0_ffn_W2"],
        "c_f32": f, "c_bits": bits, "none_tab": none,
    }
    arrays = {k: np.ascontiguousarray(v) for k, v in arrays.items()}
    nc = bacc.Bacc("TRN2", target_bir_lowering=False, num_devices=1)
    aps = {k: nc.dram_tensor(k, v.shape, mybir.dt.from_np(v.dtype), kind="ExternalInput").ap()
           for k, v in arrays.items()}
    out = nc.dram_tensor("out", (B * T, D), f32, kind="ExternalOutput").ap()
    program(nc, **aps, out=out)
    r = run_bass_kernel_spmd(nc, [arrays], core_ids=[0])
    return r.results[0]["out"].reshape(B, T, D)
```

```python
import numpy as np
import concourse.bass as bass
from concourse import mybir
from contextlib import ExitStack

f32 = mybir.dt.float32
f16 = mybir.dt.float16
bf16 = mybir.dt.bfloat16
i32 = mybir.dt.int32
u32 = mybir.dt.uint32
ALU = mybir.AluOpType
ACT = mybir.ActivationFunctionType
AX = mybir.AxisListType

B, TXT, PATCHES = 8, 128, 36
IMG = PATCHES + 1
T = IMG + TXT
D, HEADS, HD = 256, 16, 16
ROT = HD // 2
PDIM = 768
FF, NE = 1024, 4
VOCAB = 30522
P = 128
K2 = D // P
KP = PDIM // P
KF = FF // P
GRP = 4
Q2 = T - P
QB = 64
QB0 = T - QB
IPB = 3
IT = -(-B // IPB)
TILES = B + IT
CAP = 14
assert CAP == (B * T + NE * (P - 1)) // P
NJ = CAP
NONE = 1 << 20
WS = 64.0
EPS = 1e-5
LNP = float(np.log(1024.0))
SC = 1.0 / np.sqrt(np.float32(HD))
NPF = 4
CH = 3
HC2 = 8


def img_rows(i):
    n = min(IPB, B - IPB * i)
    return n, n * IMG


class Steps:

    LEAD = 4

    def __init__(self, sem, names, by=1):
        self.sem, self.names, self.by = sem, list(names), by
        self.head = self.LEAD * len(self.names) * by

    def at(self, r, name=None):
        k = len(self.names) if name is None else self.names.index(name) + 1
        return r * (len(self.names) * self.by) + (k * self.by + self.head)


def program(nc, tok_tab, patches, w_patch, base_pos, base_add, pos_txt, ids, types, w_small, cols, rows_b,
            w1, w2, c_f32, c_bits, out):
    ctx = ExitStack()
    with ctx:
        def sb(name, shape, dt):
            return ctx.enter_context(nc.sbuf_tensor(name, shape, dt))

        def sem(name):
            return ctx.enter_context(nc.semaphore(name))

        def steps(name, names, by=1):
            return Steps(sem(name), names.split(), by)

        cf = sb("cf", [P, CF_N], f32)
        ident = cf[:, CF["ident"]:CF["ident"] + P]
        cosw = cf[:, CF["cos"]:CF["cos"] + T]
        sinw = cf[:, CF["sin"]:CF["sin"] + T]
        fold = cf[:, CF["fold"]:CF["fold"] + QB]
        headmask = cf[:, CF["headmask"]:CF["headmask"] + GRP]
        rowid = cf[:, CF["rowid"]:CF["rowid"] + TILES]
        valid = cf[:, CF["valid"]:CF["valid"] + TILES]
        lanes = cf[:, CF["lanes"]:CF["lanes"] + P]
        order = cf[:, CF["order"]:CF["order"] + NE]
        jrow = cf[:, CF["jrow"]:CF["jrow"] + NJ]
        cb = sb("cb", [P, CB_N], bf16)
        identb = cb[:, CB["ident"]:CB["ident"] + P]
        mask_a = cb[:, CB["mask_a"]:CB["mask_a"] + P]
        mask_b = cb[:, CB["mask_b"]:CB["mask_b"] + T]
        mask_t = cb[:, CB["mask_t"]:CB["mask_t"] + T]
        mask_t2 = cb[:, CB["mask_t2"]:CB["mask_t2"] + Q2]
        before = cb[:, CB["before"]:CB["before"] + P]
        onesb = cb[:, CB["ones"]:CB["ones"] + P]
        selcol = cb[:, CB["sel"]:CB["sel"] + HEADS]
        sel = sb("sel", [P, HEADS, P], bf16)
        kz_at = 2 * K2 * FF
        shared = sb("shared", [P, kz_at + HEADS * T], f32)
        xg = [shared[:, i * 2 * D:(i + 1) * 2 * D] for i in range(2)]
        yo = [shared[:, (4 + i) * D:(5 + i) * D] for i in range(2)]
        res = shared[:, 6 * D:(6 + NJ) * D].rearrange("p (j n) -> p j n", j=NJ)
        wst = [shared[:, i * K2 * FF:(i + 1) * K2 * FF] for i in range(2)]
        kz = [shared[:, kz_at + i * HEADS * T // 2:kz_at + (i + 1) * HEADS * T // 2].bitcast(f16)
              .rearrange("p (h n) -> p h n", h=HEADS) for i in range(2)]
        wp = wst[0][:, 0:KP * D].rearrange("p (k n) -> p k n", k=KP)
        xp = wst[1][:, 0:KP * B * IMG].rearrange("p (k n) -> p k n", k=KP)
        wsm = shared[:, kz_at:kz_at + W_SMALL]
        wsh = sb("wsh", [P, W_SMALL], f16)
        wsl = sb("wsl", [P, W_SMALL], f16)

        def small(w, base, width):
            return w[:, base:base + K2 * width].rearrange("p (k n) -> p k n", k=K2)

        col = sb("col", [P, COLS], f32)
        bqk64 = sb("bqk64", [P, 4], f32)
        rb = sb("rb", [P, ROWS], f32)

        def row(name, n=1):
            return rb[:, RB[name]:RB[name] + n * D]

        w1h = sb("w1h", [P, NE * K2 * FF], f16)
        w1l = sb("w1l", [P, NE * K2 * FF], f16)
        w2h = sb("w2h", [P, NE * KF * D], f16)
        w2l = sb("w2l", [P, NE * KF * D], f16)
        ids_sb = sb("ids_sb", [P, B], i32)
        types_i = sb("types_i", [P, B], i32)
        types_f = sb("types_f", [P, B], f32)
        ptype = sb("ptype", [P, D], f32)
        typd = sb("typd", [P, D], f32)
        lnp = sb("lnp", [P, 1], f32)
        neghalf = sb("neghalf", [P, 4], f32)

        h_txt = sb("h_txt", [P, B, D], f32)
        h_img = sb("h_img", [P, IT, D], f32)
        base1 = sb("base1", [P, D], f32)
        base2 = sb("base2", [P, D], f32)
        x1 = sb("x1", [P, IT, D], f32)
        xT = sb("xT", [P, 2, K2, B, T], f16)
        st6 = sb("st6", [P, IT, 6], f32)
        mv = sb("mv", [P, IT, 2], f32)
        veps = sb("veps", [P, 4], f32)
        rstd = sb("rstd", [P, 4], f32)

        rot_a = sb("rot_a", [P, 2, T], f32)
        rot_b = sb("rot_b", [P, 2, T], f32)
        rot = sb("rot", [P, 2, T], f32)
        parts = [sb(f"parts{i}", [P, 2, 2, T], f16) for i in range(2)]
        stk = [sb(f"stk{i}", [P, 2, GRP, T], f16) for i in range(2)]
        flat = [sb(n, [P, HEADS * T], f16) for n in ("ph", "pl")]
        ph, pl = (t[:, :].rearrange("p (h n) -> p h n", h=HEADS) for t in flat)
        vh = [sb(f"vh{i}", [P, HEADS, HD + 1], f16) for i in range(2)]
        vl = [sb(f"vl{i}", [P, HEADS, HD + 1], f16) for i in range(2)]
        vh2 = [sb(f"vh2{i}", [Q2, HEADS, HD + 1], f16) for i in range(2)]
        vl2 = [sb(f"vl2{i}", [Q2, HEADS, HD + 1], f16) for i in range(2)]
        mx_a = sb("mx_a", [P, HEADS], f32)
        mx_b = sb("mx_b", [P, GRP, 2], f32)
        mx_w = sb("mx_w", [P, GRP, 2, 2], f32)
        nm = [sb(f"nm{i}", [P, T], bf16) for i in range(2)]
        pf = [sb(f"pf{i}", [P, CH * T], f32) for i in range(NPF)]
        ph2 = sb("ph2", [Q2, HEADS, Q2], f16)
        pl2 = sb("pl2", [Q2, HEADS, Q2], f16)
        rden = sb("rden", [P, 2, HEADS], f32)
        yn = sb("yn", [P, D], f32)
        yn2 = sb("yn2", [Q2, D], f32)
        yT = sb("yT", [P, 2, K2, T], f16)
        yTi = sb("yTi", [P, 2 * K2, B, IMG], f16)

        rows = [sb(f"rows{i}", [P, 2 * D], f32) for i in range(3)]
        g6 = [sb(f"g6_{i}", [P, 6], f32) for i in range(2)]
        gmv = [sb(f"gmv{i}", [P, 2], f32) for i in range(2)]
        gve = [sb(f"gve{i}", [P, 1], f32) for i in range(2)]
        grs = [sb(f"grs{i}", [P, 1], f32) for i in range(2)]
        junk = sb("junk", [P, NE, D], f32)
        logit = sb("logit", [P, TILES, NE], f32)
        gmax = sb("gmax", [P, TILES], f32)
        pick = sb("pick", [P, TILES, NE], f32)
        pmax = sb("pmax", [P, TILES], f32)
        chosen = sb("chosen", [P, 2 * TILES - 1, NE], bf16)
        choice = chosen[:, TILES - 1:2 * TILES - 1, :]
        gates = [sb(f"gates{i}", [P, NE], f32) for i in range(2)]
        ntiles = sb("ntiles", [P, NE], f32)
        ntiles_i = sb("ntiles_i", [P, NE], i32)
        first_tile = sb("first_tile", [P, NE], f32)
        place4 = sb("place4", [P, TILES, NE], f32)
        place = sb("place", [P, TILES], f32)
        place_i = sb("place_i", [P, TILES], i32)
        tile_of = sb("tile_of", [P, TILES], f32)
        lane_of = sb("lane_of", [P, TILES], f32)
        in_tile = sb("in_tile", [P, TILES, NJ], f32)
        id_in_tile = sb("id_in_tile", [P, TILES, NJ], f16)
        in_lane = sb("in_lane", [P, TILES, P], f16)
        behind = sb("behind", [1, NE - 1, NJ], f32)
        expert_f = sb("expert_f", [1, NJ], f32)
        expert_of = sb("expert_of", [1, NJ], i32)
        empty = sb("empty", [P, NJ], f32)
        rows_f = sb("rows_f", [P, NJ], f32)
        rows_g = sb("rows_g", [P, NJ], f32)
        to_rows = sb("to_rows", [P, NJ], i32)
        from_rows = sb("from_rows", [P, NJ], i32)

        from_ids = [sb(f"from_ids{i}", [P, 1], i32) for i in range(2)]
        to_ids = [sb(f"to_ids{i}", [P, 1], i32) for i in range(2)]

        old = [t[:, :] for t in flat]
        gh = [o[:, 0:FF].rearrange("p (k n) -> p k n", k=KF) for o in old]
        gl = [o[:, FF:2 * FF].rearrange("p (k n) -> p k n", k=KF) for o in old]
        xs = [o[:, 2 * FF:2 * FF + 2 * D].rearrange("p (a k n) -> p a k n", a=2, k=K2) for o in old]
        gf = junk[:, :, :].rearrange("p e n -> p (e n)").rearrange("p (k n) -> p k n", k=KF)

        bank = [ctx.enter_context(nc.psum_tensor(f"bank{i}", [P, 512], f32)) for i in range(8)]
        bQ, bK, bV, bM, bS, bY = bank[0], bank[1], bank[2], bank[3:5], bank[5:7], bank[7]

        scr = [nc.dram_tensor(f"scr{i}", (2, 2, P, T), f16, kind="Internal").ap() for i in range(2)]
        tokrows = nc.dram_tensor("tokrows", (B * T, 2 * D), f32, kind="Internal").ap()

        ld_c, ld_x, ld_small, ld_rows, ld_ids, ld_pos = (sem(n) for n in
                                                         "ld_c ld_x ld_small ld_rows ld_ids ld_pos".split())
        te_in = sem("te_in")
        ld_w = [sem(f"ld_w{i}") for i in range(2)]
        spare = sem("spare")
        pool_c = sem("pool_c")
        wsplit_a, wsplit_v = sem("wsplit_a"), sem("wsplit_v")
        emb_ps = sem("emb_ps")
        img = sem("img")
        img_rs = sem("img_rs")
        xt_ps, xt_hi, xt_lo = sem("xt_ps"), sem("xt_hi"), sem("xt_lo")
        txt = steps("txt", "e0 e1 e s0 s1 m0 m1 v h0 h1 hw hb t0 t1 n0 n1 w x0 x1")
        txt_rs = steps("txt_rs", "first second bo")
        tt_ps = steps("tt_ps", "t")
        tt_hi = steps("tt_hi", "t")
        tt_lo = steps("tt_lo", "t")

        qkv = steps("qkv", "q k v")
        rope = steps("rope", "qe qo ke ko rot lo")
        rope_hi = steps("rope_hi", "hi")
        v_hi = steps("v_hi", "v1 v2")
        v_lo = steps("v_lo", "v1 v2")
        scr_w = [sem(f"scr_w{i}") for i in range(2)]
        stk_in = [sem(f"stk_in{i}") for i in range(2)]
        kz_ok = steps("kz_ok", "h0 h1 h2 h3")
        mps = steps("mps", "a0 b0 a1 b1 a2 b2 a3 b3 t")
        mx = steps("mx", "a0 b0 a1 b1 a2 b2 a3 b3 w0 w1")
        nm_hi = steps("nm_hi", "n")
        nm_lo = steps("nm_lo", "n")
        sps = steps("sps", "d0 d1 c0 c1 c2 c3 c4 c5")
        ex = steps("ex", "d0 d0h d1 d1h c0 c0h c1 c1h c2 c2h c3 c3h c4 c4h c5 c5h")
        pv_l = steps("pv_l", "d0 d1 c0 c1 c2 c3 c4 c5")
        yps = steps("yps", "y")
        ynorm = steps("ynorm", "r1 r2 y1 y2")
        ytp = steps("ytp", "t")
        yt_hi = steps("yt_hi", "k0 k1")
        yt_lo = steps("yt_lo", "k0 k1")
        yti = steps("yti", "c")
        wops = [steps(f"wops{i}", "o") for i in range(2)]
        fin = [steps(f"fin{i}", "h s m x g0 g1 g2 g3 l") for i in range(2)]
        fin_rs = [steps(f"fin_rs{i}", "e r") for i in range(2)]
        store = [sem(f"store{i}") for i in range(3)]
        w64 = steps("w64", "s0 h0 s1 h1")
        wlo = steps("wlo", "l0 l1")
        total_ps, rank_ps, rows_ps = sem("total_ps"), sem("rank_ps"), sem("rows_ps")
        sort = Steps(sem("sort"), SORT_STEPS)
        sort.head = 0
        gat = [sem(f"gat{i}") for i in range(2)]
        idg, ids_out = steps("idg", "c"), steps("ids_out", "c")
        hbs = steps("hbs", "b")
        xtp = steps("xtp", "t")
        xsh = steps("xsh", "h")
        xsl = steps("xsl", "l")
        l1 = steps("l1", "a b")
        gel = steps("gel", " ".join(f"g{i}" for i in range(KF)))
        gsp_h = steps("gsp_h", "a b")
        gsp_l = steps("gsp_l", "a b")
        l2 = steps("l2", "o")
        yok = steps("yok", "o")
        osc = [sem(f"osc{i}") for i in range(2)]

        chunks = [("d0", 0, HC2), ("d1", HC2, HC2)] + [(f"c{c}", CH * c, min(CH, HEADS - CH * c))
                                                       for c in range(-(-HEADS // CH))]
        W_LOADS = [(w1, w1h, w1l, e) for e in range(NE)] + [(w2, w2h, w2l, e) for e in range(NE)]
        WN = K2 * FF
        assert WN == KF * D and len(W_LOADS) == B

        STK = 128

        block = ctx.enter_context(nc.Block())

        @block.sync
        def _(sp):
            for i in range(2):
                sp.sem_inc(stk_in[i], STK * Steps.LEAD)
            for i in range(3):
                sp.sem_inc(store[i], 16 * Steps.LEAD)
            sp.dma_start(cf[:, :], c_f32).then_inc(ld_c, 16)
            for k in range(KP):
                sp.dma_start(xp[:, k, :], patches[:, k, :]).then_inc(ld_x, 16)
                sp.dma_start(wp[:, k, :], w_patch[:, k, :]).then_inc(ld_x, 16)
            sp.dma_start(base1[0:IPB * IMG, :], base_pos).then_inc(ld_pos, 16)
            sp.dma_start(base2[0:IPB * IMG, :], base_add).then_inc(ld_pos, 16)
            sp.dma_start(ptype[:, :], pos_txt).then_inc(ld_pos, 16)
            sp.dma_start(rb[:, :], rows_b.partition_broadcast(P)).then_inc(ld_rows, 16)
            sp.dma_start(wsm[:, :], w_small).then_inc(ld_small, 16)
            sp.dma_start(col[:, :], cols).then_inc(ld_small, 16)
            sp.dma_start(cb[:, :].bitcast(mybir.dt.uint16), c_bits).then_inc(ld_small, 16)
            def w_load(src, n, e):
                s = src[e].rearrange("(k p) n -> p k n", p=P)
                sp.dma_start(wst[n % 2][:, :].rearrange("p (k n) -> p k n", k=s.shape[1]), s).then_inc(ld_w[n % 2], 16)

            sp.wait_ge(emb_ps, IT)
            w_load(w1, 0, 0)
            w_load(w1, 1, 1)

            def stack(b, par, half):
                sp.wait_ge(rope.sem, rope.at(b, "lo"))
                sp.wait_ge(rope_hi.sem, rope_hi.at(b))
                sp.wait_ge(stk_in[par], STK * Steps.LEAD + half * STK)
                sp.dma_start(scr[par].rearrange("a c p n -> p (a c) n"),
                             parts[par][:, :, :, :].rearrange("p a c n -> p (a c) n")).then_inc(scr_w[par], 16)
                sp.wait_ge(scr_w[par], half * 16 + 16)
                sp.wait_ge(sps.sem, sps.at(b - 2))
                for a in range(2):
                    for c in range(2):
                        g = 2 * a + c
                        for w, hl in ((0, a), (1, c)):
                            sp.dma_start(stk[par][32 * g:32 * g + 32, w, :, :],
                                         scr[par][hl, w].rearrange("(g p) n -> p g n", p=32)).then_inc(stk_in[par], 16)

            def keep(b, buf):
                sp.wait_ge(fin[0].sem, fin[0].at(b, "x"))
                sp.dma_start(tokrows[bass.ds(b * T + IMG, TXT), :], rows[buf][:, :]).then_inc(store[buf], 16)

            def keep_img(i):
                n, m = img_rows(i)
                sp.wait_ge(fin[1].sem, fin[1].at(i, "x"))
                for j in range(n):
                    sp.dma_start(tokrows[(IPB * i + j) * T:(IPB * i + j) * T + IMG, :],
                                 rows[2][j * IMG:(j + 1) * IMG, :]).then_inc(store[2], 16)

            def weights(t):
                sp.wait_ge(wlo.sem, wlo.at(t))
                src, _, _, e = W_LOADS[t + 2]
                w_load(src, t + 2, e)

            stack(0, 0, 0)
            stack(1, 1, 0)
            stack(2, 0, 1)
            weights(0)
            for i in range(2):
                for par in (1, 0):
                    t = 2 * i + 2 - par
                    keep(t - 1, 1 - par)
                    stack(t + 2, par, (t + 2) // 2)
                    weights(t)
            keep(4, 0)
            stack(7, 1, 3)
            weights(5)
            keep_img(0)
            keep(5, 1)
            keep_img(1)
            keep(6, 0)
            keep(7, 1)
            keep_img(2)
            sp.wait_ge(osc[0], 16 * ((NJ + 1) // 2))
            sp.wait_ge(osc[1], 16 * (NJ // 2))

        @block.gpsimd
        def _(pool):
            for s in (txt_rs, pv_l, *fin_rs, wlo, yti, idg, ids_out):
                pool.sem_inc(s.sem, s.head)
            pool.dma_start(ids_sb[:, :], ids).then_inc(ld_ids, 16)
            pool.dma_start(types_i[:, :], types).then_inc(ld_ids, 16)
            pool.memset(neghalf[:, :], -0.5)
            for i in range(2):
                pool.memset(nm[i][:, :], 0.0)
                pool.memset(vh[i][:, :, :], 1.0)
                pool.memset(vl[i][:, :, :], 0.0)
                pool.memset(vh2[i][:, :, :], 1.0)
                pool.memset(vl2[i][:, :, :], 0.0)
            pool.memset(mx_w[:, :, :, :], 0.0)
            pool.memset(logit[:, :, :], 0.0)
            pool.memset(first_tile[:, :], 0.0)
            pool.memset(chosen[:, :, :], 0.0)
            pool.memset(mv[:, :, :], 1.0)
            for i in range(2):
                pool.memset(gmv[i][:, :], 1.0)
            pool.memset(lnp[:, :], LNP).then_inc(pool_c, 1)
            pool.wait_ge(ld_ids, 32)
            for b in range(B):
                pool.indirect_dma_start(h_txt[:, b, :], None, tok_tab,
                                        bass.IndirectOffsetOnAxis(ids_sb[:, b:b + 1], 0)).then_inc(te_in, 16)
            pool.wait_ge(img, 3 * IT + 2)
            pool.wait_ge(pool_c, 1)
            pool.tensor_tensor(rstd[:, 0:IT], veps[:, 0:IT], neghalf[:, 0:IT], ALU.pow).then_inc(img_rs, 1)
            pool.wait_ge(img, 4 * IT + 2)
            pool.wait_ge(ld_rows, 16)
            for i in range(IT):
                n, m = img_rows(i)
                pool.tensor_tensor(h_img[0:m, i, :], h_img[0:m, i, :], row("bo")[0:m, :], ALU.add).then_inc(img_rs, 1)
            with pool.Fori(0, B // 2) as i:
                pool.wait_ge(txt.sem, txt.at(i, "v"))
                pool.tensor_tensor(rstd[:, 0:2], veps[:, 0:2], neghalf[:, 0:2], ALU.pow).then_inc(txt_rs.sem, 1)
                pool.wait_ge(txt.sem, txt.at(i, "w"))
                pool.tensor_tensor(rstd[:, 2:4], veps[:, 2:4], neghalf[:, 0:2], ALU.pow).then_inc(txt_rs.sem, 1)
                pool.wait_ge(txt.sem, txt.at(i, "x1"))
                h2 = h_txt[:, bass.ds(2 * i, 2), :]
                pool.tensor_tensor(h2, h2, row("bo").unsqueeze(1).to_broadcast([P, 2, D]), ALU.add)\
                    .then_inc(txt_rs.sem, 1)

            def low(b, n):
                name, h0, hn = chunks[n]
                pool.wait_ge(ex.sem, ex.at(b, name + "h"))
                if name[0] == "d":
                    pool.tensor_tensor(pl2[:, h0:h0 + hn, :], pf[n % NPF][0:Q2, 0:hn * Q2]
                                       .rearrange("p (h n) -> p h n", h=hn), ph2[:, h0:h0 + hn, :], ALU.subtract)\
                        .then_inc(pv_l.sem, 1)
                else:
                    pool.tensor_tensor(pl[:, h0:h0 + hn, :], pf[n % NPF][:, 0:hn * T]
                                       .rearrange("p (h n) -> p h n", h=hn), ph[:, h0:h0 + hn, :], ALU.subtract)\
                        .then_inc(pv_l.sem, 1)

            def image_columns(b):
                pool.wait_ge(yt_hi.sem, yt_hi.at(b))
                pool.wait_ge(yt_lo.sem, yt_lo.at(b))
                pool.tensor_copy(yTi[:, :, bass.ds(b, 1), :].rearrange("p a b n -> p a (b n)"),
                                 yT[:, :, :, 0:IMG].rearrange("p a k n -> p (a k) n")).then_inc(yti.sem, 1)

            def inverse_std(r, u):
                pool.wait_ge(fin[u].sem, fin[u].at(r, "m"))
                pool.tensor_scalar(gve[u][:, :], gmv[u][:, 1:2], EPS, None, ALU.add).then_inc(fin_rs[u].sem, 1)
                pool.wait_ge(fin_rs[u].sem, fin_rs[u].at(r, "e"))
                pool.tensor_tensor(grs[u][:, :], gve[u][:, :], neghalf[:, 0:1], ALU.pow).then_inc(fin_rs[u].sem, 1)

            def w_low(n, k):
                _, hi, lo, e = W_LOADS[n]
                c = slice(k * WN // 2, (k + 1) * WN // 2)
                pool.wait_ge(w64.sem, w64.at(n, f"h{k}"))
                pool.tensor_tensor(lo[:, e * WN + c.start:e * WN + c.stop], wst[n % 2][:, c],
                                   hi[:, e * WN + c.start:e * WN + c.stop], ALU.subtract).then_inc(wlo.sem, 1)

            def batch(t, prev=True, img=None):
                w_low(t, 0)
                low(t, 0)
                low(t, 1)
                w_low(t, 1)
                if img is not None:
                    inverse_std(img, 1)
                low(t, 2)
                if prev:
                    image_columns(t - 1)
                low(t, 3)
                low(t, 4)
                low(t, 5)
                if prev:
                    inverse_std(t - 1, 0)
                low(t, 6)
                low(t, 7)

            batch(0, prev=False)
            for t in range(1, 6):
                batch(t)
            batch(6, img=0)
            batch(7, img=1)
            image_columns(7)
            inverse_std(7, 0)
            inverse_std(2, 1)

            pool.wait_ge(store[0], 16 * (Steps.LEAD + B // 2))
            pool.wait_ge(store[1], 16 * (Steps.LEAD + B // 2))
            pool.wait_ge(store[2], 16 * (Steps.LEAD + B))
            pool.wait_ge(sort.sem, sort.at(0, "from_rows"))

            def gather(j, par):
                pool.tensor_copy(from_ids[par][:, :], from_rows[:, bass.ds(j, 1)]).then_inc(idg.sem, 1)
                pool.wait_ge(idg.sem, idg.at(j))
                pool.sem_inc(spare, 1)
                pool.indirect_dma_start(xg[par][:, :], None, tokrows,
                                        bass.IndirectOffsetOnAxis(from_ids[par][:, :], 0)).then_inc(gat[par], 16)

            def scatter_out(j, par):
                pool.tensor_copy(to_ids[par][:, :], to_rows[:, bass.ds(j, 1)]).then_inc(ids_out.sem, 1)
                pool.wait_ge(ids_out.sem, ids_out.at(j))
                pool.wait_ge(yok.sem, yok.at(j))
                pool.sem_inc(spare, 1)
                pool.indirect_dma_start(out, bass.IndirectOffsetOnAxis(to_ids[par][:, :], 0),
                                        yo[par], None,
                                        bounds_check=B * T - 1, oob_is_err=False).then_inc(osc[par], 16)

            def gather_next(j, par):
                pool.wait_ge(xtp.sem, xtp.at(j - 2))
                pool.wait_ge(hbs.sem, hbs.at(j - 2))
                gather(j, par)

            gather(0, 0)
            gather(1, 1)
            pool.wait_ge(sort.sem, sort.at(0, "to_rows"))
            for j in (2, 3):
                gather_next(j, j % 2)
            scatter_out(0, 0)
            gather_next(4, 0)
            scatter_out(1, 1)
            gather_next(5, 1)
            with pool.Fori(1, NJ // 2 - 2) as i:
                for par in range(2):
                    pool.wait_ge(osc[par], i * 16)
                    scatter_out(2 * i + par, par)
                    gather_next(2 * i + par + 4, par)
            for j in range(NJ - 4, NJ):
                pool.wait_ge(osc[j % 2], 16 * (j // 2))
                scatter_out(j, j % 2)

        @block.scalar
        def _(act):
            for s in (tt_hi, rope_hi, v_hi, nm_hi, ex, yt_hi, w64, gel):
                act.sem_inc(s.sem, s.head)
            act.wait_ge(ld_small, 48)
            act.activation(wsm[:, :], wsm[:, :], ACT.Copy, scale=WS).then_inc(wsplit_a, 1)
            act.wait_ge(wsplit_a, 1)
            act.activation(wsh[:, :], wsm[:, :], ACT.Copy).then_inc(wsplit_a, 1)
            act.activation(bqk64[:, :], col[:, 0:4], ACT.Copy, scale=WS).then_inc(wsplit_a, 1)
            for i in range(IT):
                n, m = img_rows(i)
                act.wait_ge(xt_ps, i + 1)
                act.activation(xT[:, 0, :, IPB * i:IPB * i + n, 0:IMG],
                               bank[i][:, 0:K2 * m].rearrange("p (k b n) -> p k b n", k=K2, b=n), ACT.Copy)\
                   .then_inc(xt_hi, 1)
            with act.Fori(0, B // 2) as i:
                act.wait_ge(tt_ps.sem, tt_ps.at(i))
                act.activation(xT[:, 0, :, bass.ds(2 * i, 2), IMG:T],
                               bank[3][:, :].rearrange("p (k b n) -> p k b n", k=K2, b=2), ACT.Copy)\
                   .then_inc(tt_hi.sem, 1)

            def rope_high(b, par):
                act.wait_ge(rope.sem, rope.at(b, "rot"))
                act.wait_ge(scr_w[par], (b // 2) * 16) if b >= 2 else None
                act.activation(parts[par][:, 0, :, :], rot[:, :, :], ACT.Copy).then_inc(rope_hi.sem, 1)

            def v_high(b, par):
                act.wait_ge(qkv.sem, qkv.at(b, "v"))
                act.wait_ge(yps.sem, yps.at(b - 2))
                act.activation(vh[par][:, :, 0:HD], bV[:, 0:D].rearrange("p (h n) -> p h n", h=HEADS), ACT.Copy,
                               scale=1 / WS).then_inc(v_hi.sem, 1)
                act.activation(vh2[par][:, :, 0:HD], bV[0:Q2, D:2 * D].rearrange("p (h n) -> p h n", h=HEADS), ACT.Copy,
                               scale=1 / WS).then_inc(v_hi.sem, 1)

            def exps(b, n):
                name, h0, hn = chunks[n]
                act.wait_ge(sps.sem, sps.at(b, name))
                act.wait_ge(pv_l.sem, pv_l.at(b if n >= NPF else b - 1, chunks[n - NPF][0]))
                m, w = (Q2, Q2) if name[0] == "d" else (P, T)
                s = bS[n % 2][0:m, 0:hn * w]
                act.activation(pf[n % NPF][0:m, 0:hn * w], s, ACT.Exp, bias=lnp[0:m, :], scale=SC).then_inc(ex.sem, 1)
                act.wait_ge(yps.sem, yps.at(b - 1))
                act.activation((ph2 if name[0] == "d" else ph)[:, h0:h0 + hn, :], s.rearrange("p (h n) -> p h n", h=hn),
                               ACT.Exp, bias=lnp[0:m, :], scale=SC).then_inc(ex.sem, 1)

            def turned(b):
                act.wait_ge(ytp.sem, ytp.at(b))
                act.wait_ge(wops[0].sem, wops[0].at(b - 1))
                act.wait_ge(yti.sem, yti.at(b - 1))
                for k in range(K2):
                    act.activation(yT[:, 0, k, :], bV[:, k * T:(k + 1) * T], ACT.Identity, bias=col[:, 4 + k:5 + k])\
                       .then_inc(yt_hi.sem, 1)

            def maxima(b, par):
                act.wait_ge(mps.sem, mps.at(b, "t"))
                act.wait_ge(sps.sem, sps.at(b - 2))
                act.activation(nm[par][0:HEADS, :], bM[0][0:HEADS, 0:T], ACT.Copy, scale=-1.0).then_inc(nm_hi.sem, 1)

            def w_scale(n, k):
                c = slice(k * WN // 2, (k + 1) * WN // 2)
                act.wait_ge(ld_w[n % 2], 16 * (n // 2 + 1))
                act.activation(wst[n % 2][:, c], wst[n % 2][:, c], ACT.Copy, scale=WS).then_inc(w64.sem, 1)

            def w_high(n, k):
                _, hi, _, e = W_LOADS[n]
                c = slice(k * WN // 2, (k + 1) * WN // 2)
                act.wait_ge(w64.sem, w64.at(n, f"s{k}"))
                act.activation(hi[:, e * WN + c.start:e * WN + c.stop], wst[n % 2][:, c], ACT.Copy).then_inc(w64.sem, 1)

            def batch(t, par, prev=True, ahead=2):
                exps(t, 0)
                exps(t, 1)
                if prev:
                    turned(t - 1)
                exps(t, 2)
                if t + 1 < B:
                    w_scale(t + 1, 0)
                exps(t, 3)
                if ahead == 2:
                    rope_high(t + 2, par)
                if t + 1 < B:
                    w_high(t + 1, 0)
                exps(t, 4)
                exps(t, 5)
                if t + 1 < B:
                    w_scale(t + 1, 1)
                exps(t, 6)
                if t + 1 < B:
                    w_high(t + 1, 1)
                exps(t, 7)
                if ahead >= 1:
                    maxima(t + 1, 1 - par)
                if ahead == 2:
                    v_high(t + 2, par)

            act.wait_ge(pool_c, 1)
            for b in range(2):
                rope_high(b, b)
                v_high(b, b)
                for k in range(2):
                    if b == 0:
                        w_scale(0, k)
                        w_high(0, k)
            maxima(0, 0)
            batch(0, 0, prev=False)
            for t in range(1, B):
                batch(t, t % 2, ahead=min(2, B - 1 - t))
            turned(7)

            def gelus(j):
                e = act.value_load(expert_of[0:1, bass.ds(j, 1)], min_val=0, max_val=NE - 1)
                for n in range(KF):
                    if n % 4 == 0:
                        half = "ab"[n // 4]
                        act.wait_ge(l1.sem, l1.at(j, half))
                        act.wait_ge(gsp_l.sem, gsp_l.at(j - 1, half))
                    act.activation(gf[:, n, :], bank[1 + n // 4][:, (n % 4) * P:(n % 4 + 1) * P], ACT.Gelu,
                                   bias=col[:, bass.ds(e * KF + (6 + n), 1)], scale=1 / WS).then_inc(gel.sem, 1)

            act.wait_ge(sort.sem, sort.at(0, "expert_of"))
            gelus(0)
            gelus(1)
            with act.Fori(1, NJ // 2) as i:
                for par in range(2):
                    gelus(2 * i + par)

        @block.vector
        def _(dve):
            v = dve
            for s in (txt, tt_lo, rope, v_lo, kz_ok, mx, nm_lo, ynorm, yt_lo, *fin, hbs, xsl, xsh, gsp_h, gsp_l,
                      yok):
                dve.sem_inc(s.sem, s.head)
            dve.wait_ge(ld_pos, 48)
            v.tensor_tensor(base1[0:IPB * IMG, :], base1[0:IPB * IMG, :], base2[0:IPB * IMG, :], ALU.add).then_inc(img, 1)
            dve.wait_ge(img, 1)
            dve.wait_ge(pool_c, 1)
            for i in range(IT):
                n, m = img_rows(i)
                dve.wait_ge(emb_ps, i + 1)
                v.tensor_tensor(h_img[0:m, i, :], bank[i][0:m, 0:D], base1[0:m, :], ALU.add).then_inc(img, 1)
            for i in range(IT):
                n, m = img_rows(i)
                dve.wait_ge(img, i + 2)
                v.bn_stats(st6[0:m, i, :], h_img[0:m, i, :]).then_inc(img, 1)
            for i in range(IT):
                n, m = img_rows(i)
                dve.wait_ge(img, IT + 2 + i)
                v.bn_aggr(mv[0:m, i, :], st6[0:m, i, :]).then_inc(img, 1)
            dve.wait_ge(img, 3 * IT + 1)
            v.tensor_scalar(veps[:, 0:IT], mv[:, :, 1], EPS, None, ALU.add).then_inc(img, 1)
            dve.wait_ge(img_rs, 1)
            for i in range(IT):
                n, m = img_rows(i)
                v.tensor_scalar(x1[0:m, i, :], h_img[0:m, i, :], mv[0:m, i, 0:1], rstd[0:m, i:i + 1],
                                ALU.subtract, ALU.mult).then_inc(img, 1)
            for i in range(IT):
                n, m = img_rows(i)
                dve.wait_ge(xt_hi, i + 1)
                v.tensor_tensor(xT[:, 1, :, IPB * i:IPB * i + n, 0:IMG],
                                bank[i][:, 0:K2 * m].rearrange("p (k b n) -> p k b n", k=K2, b=n),
                                xT[:, 0, :, IPB * i:IPB * i + n, 0:IMG], ALU.subtract).then_inc(xt_lo, 1)
            dve.wait_ge(wsplit_a, 2)
            v.tensor_tensor(wsl[:, :], wsm[:, :], wsh[:, :], ALU.subtract).then_inc(wsplit_v, 1)
            v.tensor_copy(sel[:, :, :], selcol.unsqueeze(2).to_broadcast([P, HEADS, P])).then_inc(wsplit_v, 1)
            dve.wait_ge(ld_rows, 16)
            v.tensor_tensor(ptype[:, :], ptype[:, :], row("type0"), ALU.add).then_inc(wsplit_v, 1)
            v.tensor_tensor(typd[:, :], row("type1"), row("type0"), ALU.subtract).then_inc(wsplit_v, 1)
            dve.wait_ge(ld_ids, 32)
            v.tensor_copy(types_f[:, :], types_i[:, :]).then_inc(wsplit_v, 1)
            dve.wait_ge(wsplit_v, 5)
            dve.wait_ge(te_in, 16 * B)
            with dve.Fori(0, B // 2) as i:
                def both(x):
                    return x.unsqueeze(1).to_broadcast([P, 2, D])

                h2 = h_txt[:, bass.ds(2 * i, 2), :]
                dve.wait_ge(tt_ps.sem, tt_ps.at(i - 1))
                for k in range(2):
                    hk = h_txt[:, bass.ds(2 * i + k, 1), :].rearrange("p b n -> p (b n)")
                    v.scalar_tensor_tensor(x1[:, k, :], typd[:, :], types_f[:, bass.ds(2 * i + k, 1)], hk,
                                           ALU.mult, ALU.add).then_inc(txt.sem, 1)
                dve.wait_ge(txt.sem, txt.at(i, "e1"))
                v.tensor_tensor(x1[:, 0:2, :], x1[:, 0:2, :], both(ptype[:, :]), ALU.add).then_inc(txt.sem, 1)
                dve.wait_ge(txt.sem, txt.at(i, "e"))
                dve.sem_inc(spare, 1)
                for k in range(2):
                    v.bn_stats(st6[:, k, :], x1[:, k, :]).then_inc(txt.sem, 1)
                for k in range(2):
                    dve.wait_ge(txt.sem, txt.at(i, f"s{k}"))
                    dve.sem_inc(spare, 1)
                    v.bn_aggr(mv[:, k, :], st6[:, k, :]).then_inc(txt.sem, 1)
                dve.wait_ge(txt.sem, txt.at(i, "m1"))
                v.tensor_scalar(veps[:, 0:2], mv[:, 0:2, 1], EPS, None, ALU.add).then_inc(txt.sem, 1)
                dve.wait_ge(txt_rs.sem, txt_rs.at(i, "first"))
                for k in range(2):
                    hk = h_txt[:, bass.ds(2 * i + k, 1), :].rearrange("p b n -> p (b n)")
                    v.tensor_scalar(hk, x1[:, k, :], mv[:, k, 0:1], rstd[:, k:k + 1], ALU.subtract, ALU.mult)\
                     .then_inc(txt.sem, 1)
                dve.wait_ge(txt.sem, txt.at(i, "h1"))
                v.tensor_tensor(h2, h2, both(row("ln_w")), ALU.mult).then_inc(txt.sem, 1)
                dve.wait_ge(txt.sem, txt.at(i, "hw"))
                v.tensor_tensor(h2, h2, both(row("ln_b")), ALU.add).then_inc(txt.sem, 1)
                dve.wait_ge(txt.sem, txt.at(i, "hb"))
                dve.sem_inc(spare, 1)
                for k in range(2):
                    hk = h_txt[:, bass.ds(2 * i + k, 1), :].rearrange("p b n -> p (b n)")
                    v.bn_stats(st6[:, k, :], hk).then_inc(txt.sem, 1)
                for k in range(2):
                    dve.wait_ge(txt.sem, txt.at(i, f"t{k}"))
                    dve.sem_inc(spare, 1)
                    v.bn_aggr(mv[:, k, :], st6[:, k, :]).then_inc(txt.sem, 1)
                dve.wait_ge(txt.sem, txt.at(i, "n1"))
                v.tensor_scalar(veps[:, 2:4], mv[:, 0:2, 1], EPS, None, ALU.add).then_inc(txt.sem, 1)
                dve.wait_ge(txt_rs.sem, txt_rs.at(i, "second"))
                for k in range(2):
                    hk = h_txt[:, bass.ds(2 * i + k, 1), :].rearrange("p b n -> p (b n)")
                    v.tensor_scalar(x1[:, k, :], hk, mv[:, k, 0:1], rstd[:, 2 + k:3 + k], ALU.subtract, ALU.mult)\
                     .then_inc(txt.sem, 1)
                dve.wait_ge(tt_hi.sem, tt_hi.at(i))
                x2 = xT[:, :, :, bass.ds(2 * i, 2), IMG:T]
                v.tensor_tensor(x2[:, 1], bank[3][:, :].rearrange("p (k b n) -> p k b n", k=K2, b=2), x2[:, 0],
                                ALU.subtract).then_inc(tt_lo.sem, 1)

            def rotate(b, a):
                bk, one, two = ((bQ, "qe", "qo"), (bK, "ke", "ko"))[a]
                dve.wait_ge(qkv.sem, qkv.at(b, "qk"[a]))
                if a == 0:
                    dve.wait_ge(rope.sem, rope.at(b - 1, "rot"))
                v.scalar_tensor_tensor(rot_a[:, a, :], bk[:, 0:T], bqk64[:, 2 * a:2 * a + 1], cosw, ALU.add, ALU.mult)\
                 .then_inc(rope.sem, 1)
                v.scalar_tensor_tensor(rot_b[:, a, :], bk[:, T:2 * T], bqk64[:, 2 * a + 1:2 * a + 2], sinw,
                                       ALU.add, ALU.mult).then_inc(rope.sem, 1)
                if a == 1:
                    dve.wait_ge(rope.sem, rope.at(b, "ko"))
                    dve.wait_ge(rope_hi.sem, rope_hi.at(b - 1))
                    v.tensor_tensor(rot[:, :, :], rot_a[:, :, :], rot_b[:, :, :], ALU.subtract).then_inc(rope.sem, 1)

            def rope_low(b, par, half):
                dve.wait_ge(rope_hi.sem, rope_hi.at(b))
                if not isinstance(half, int) or half > 0:
                    dve.wait_ge(scr_w[par], half * 16)
                v.tensor_tensor(parts[par][:, 1, :, :], rot[:, :, :], parts[par][:, 0, :, :], ALU.subtract)\
                 .then_inc(rope.sem, 1)

            def v_low(b, par):
                dve.wait_ge(v_hi.sem, v_hi.at(b))
                v.scalar_tensor_tensor(vl[par][:, :, 0:HD], bV[:, 0:D].rearrange("p (h n) -> p h n", h=HEADS), 1 / WS,
                                       vh[par][:, :, 0:HD], ALU.mult, ALU.subtract).then_inc(v_lo.sem, 1)
                v.scalar_tensor_tensor(vl2[par][:, :, 0:HD], bV[0:Q2, D:2 * D].rearrange("p (h n) -> p h n", h=HEADS),
                                       1 / WS, vh2[par][:, :, 0:HD], ALU.mult, ALU.subtract).then_inc(v_lo.sem, 1)

            def spread(b, par, half):
                dve.wait_ge(stk_in[par], STK * (Steps.LEAD + 1) + half * STK)
                dve.wait_ge(sps.sem, sps.at(b - 2))
                kv = kz[par][:, :, :].rearrange("p (g h) n -> p g h n", g=GRP)
                for h in range(GRP):
                    v.tensor_scalar(kv[:, :, h, :], stk[par][:, 1, :, :], headmask[:, h:h + 1], None, ALU.mult)\
                     .then_inc(kz_ok.sem, 1)

            def maxima(b, g):
                dve.wait_ge(mps.sem, mps.at(b, f"a{g}"))
                if g == 0:
                    dve.wait_ge(mps.sem, mps.at(b - 1))
                v.tensor_reduce(mx_a[:, GRP * g:GRP * g + GRP], bM[0][:, :].rearrange("p (h n) -> p h n", h=GRP),
                                AX.X, ALU.max).then_inc(mx.sem, 1)
                dve.wait_ge(mps.sem, mps.at(b, f"b{g}"))
                v.tensor_reduce(mx_b[:, g, :], bM[1][:, 0:2 * T].rearrange("p (h n) -> p h n", h=2),
                                AX.X, ALU.max).then_inc(mx.sem, 1)
                if g == GRP - 1:
                    dve.wait_ge(mx.sem, mx.at(b, "b3"))
                    for u in range(2):
                        v.tensor_copy(mx_w[QB * u:QB * u + QB, :, u, :], mx_b[QB * u:QB * u + QB, :, :]).then_inc(mx.sem, 1)

            def maxima_low(b, par):
                dve.wait_ge(nm_hi.sem, nm_hi.at(b))
                dve.wait_ge(sps.sem, sps.at(b - 2))
                v.scalar_tensor_tensor(nm[par][32:32 + HEADS, :], bM[0][0:HEADS, 0:T], -1.0, nm[par][0:HEADS, :],
                                       ALU.mult, ALU.subtract).then_inc(nm_lo.sem, 1)

            def normalise(b):
                dve.wait_ge(yps.sem, yps.at(b))
                y1 = bY[:, 0:HEADS * (HD + 1)].rearrange("p (h n) -> p h n", h=HEADS)
                y2 = bK[0:Q2, 0:HEADS * (HD + 1)].rearrange("p (h n) -> p h n", h=HEADS)
                v.reciprocal(rden[:, 0, :], y1[:, :, HD]).then_inc(ynorm.sem, 1)
                v.reciprocal(rden[0:Q2, 1, :], y2[:, :, HD]).then_inc(ynorm.sem, 1)
                dve.wait_ge(ytp.sem, ytp.at(b - 1))
                dve.wait_ge(ynorm.sem, ynorm.at(b, "r1"))
                v.tensor_tensor(yn[:, :].rearrange("p (h n) -> p h n", h=HEADS), y1[:, :, 0:HD],
                                rden[:, 0, :].unsqueeze(2).to_broadcast([P, HEADS, HD]), ALU.mult).then_inc(ynorm.sem, 1)
                dve.wait_ge(ynorm.sem, ynorm.at(b, "r2"))
                v.tensor_tensor(yn2[:, :].rearrange("p (h n) -> p h n", h=HEADS), y2[:, :, 0:HD],
                                rden[0:Q2, 1, :].unsqueeze(2).to_broadcast([Q2, HEADS, HD]), ALU.mult)\
                 .then_inc(ynorm.sem, 1)

            def turned(b):
                dve.wait_ge(yt_hi.sem, yt_hi.at(b))
                for k in range(K2):
                    v.scalar_tensor_tensor(yT[:, 1, k, :], bV[:, k * T:(k + 1) * T], col[:, 4 + k:5 + k], yT[:, 0, k, :],
                                           ALU.add, ALU.subtract).then_inc(yt_lo.sem, 1)

            def residual_rows(r, u, buf, bk, kept, residual, m=P):
                dve.wait_ge(wops[u].sem, wops[u].at(r))
                dve.wait_ge(store[buf], kept)
                hr = rows[buf][0:m, D:2 * D]
                v.scalar_tensor_tensor(hr, bk[0:m, 0:D], 1 / WS, residual, ALU.mult, ALU.add).then_inc(fin[u].sem, 1)
                dve.wait_ge(fin[u].sem, fin[u].at(r, "h"))
                dve.sem_inc(spare, 1)
                v.bn_stats(g6[u][0:m, :], hr).then_inc(fin[u].sem, 1)
                dve.wait_ge(fin[u].sem, fin[u].at(r, "s"))
                dve.wait_ge(fin_rs[u].sem, fin_rs[u].at(r - 1))
                dve.sem_inc(spare, 1)
                v.bn_aggr(gmv[u][0:m, :], g6[u][0:m, :]).then_inc(fin[u].sem, 1)

            def gate(r, u, buf, at, m=P, parts=(0, 1)):
                hr = rows[buf][0:m, D:2 * D]
                xr = rows[buf][0:m, 0:D]
                if 0 in parts:
                    dve.wait_ge(fin_rs[u].sem, fin_rs[u].at(r))
                    v.tensor_scalar(xr, hr, gmv[u][0:m, 0:1], grs[u][0:m, :], ALU.subtract, ALU.mult)\
                     .then_inc(fin[u].sem, 1)
                    dve.wait_ge(fin[u].sem, fin[u].at(r, "x"))
                for e in (e for part in parts for e in range(2 * part, 2 * part + 2)):
                    v.tensor_tensor_reduce(out=junk[0:m, e, :], in0=xr, in1=rb[0:m, RB["wg"] + e * D:RB["wg"] + (e + 1) * D],
                                           scale=1.0, scalar=0.0, op0=ALU.mult, op1=ALU.add,
                                           accum_out=gates[u][0:m, e:e + 1]).then_inc(fin[u].sem, 1)
                if 1 in parts:
                    dve.wait_ge(fin[u].sem, fin[u].at(r, "g3"))
                    v.tensor_tensor(logit[0:m, bass.ds(at, 1), :].rearrange("p r e -> p (r e)"), gates[u][0:m, :],
                                    rb[0:m, RB["bg"]:RB["bg"] + NE], ALU.add).then_inc(fin[u].sem, 1)

            def text_rows(b):
                return h_txt[:, bass.ds(b, 1), :].rearrange("p b n -> p (b n)")

            L = Steps.LEAD

            def batch(t, par, half, before, prev=True, ahead=2, img=None):
                if prev:
                    normalise(t - 1)
                if prev and ahead >= 1:
                    v_low(t + 1, 1 - par)
                if ahead == 2:
                    rotate(t + 2, 0)
                if img is not None:
                    residual_rows(img, 1, 2, bQ, 16 * (L + IPB * img), h_img[0:img_rows(img)[1], img, :], img_rows(img)[1])
                if ahead >= 1:
                    spread(t + 1, 1 - par, before + 1)
                if prev:
                    turned(t - 1)
                if ahead == 2:
                    rotate(t + 2, 1)
                if img is not None:
                    gate(img, 1, 2, B + img, img_rows(img)[1])
                if ahead >= 1:
                    maxima(t + 1, 0)
                if ahead == 2:
                    rope_low(t + 2, par, half + 1)
                if prev:
                    residual_rows(t - 1, 0, 1 - par, bQ, 16 * L + before * 16, text_rows(t - 1))
                if ahead >= 1:
                    maxima(t + 1, 1)
                if ahead >= 1:
                    maxima(t + 1, 2)
                if prev:
                    gate(t - 1, 0, 1 - par, t - 1, parts=(0,))
                if ahead >= 1:
                    maxima(t + 1, 3)
                if prev:
                    gate(t - 1, 0, 1 - par, t - 1, parts=(1,))
                if ahead >= 1:
                    maxima_low(t + 1, 1 - par)

            dve.wait_ge(wsplit_a, 3)
            dve.wait_ge(ld_c, 16)
            for b in range(2):
                rotate(b, 0)
                rotate(b, 1)
                rope_low(b, b, 0)
                v_low(b, b)
            spread(0, 0, 0)
            for g in range(GRP):
                maxima(0, g)
            maxima_low(0, 0)
            dve.wait_ge(txt_rs.sem, txt_rs.at(B // 2 - 1))
            dve.wait_ge(img_rs, 1 + IT)
            batch(0, 0, 0, -1, prev=False)
            with dve.Fori(0, 2) as i:
                batch(2 * i + 1, 1, i, i)
                batch(2 * i + 2, 0, i + 1, i)
            batch(5, 1, 2, 2)
            batch(6, 0, 3, 2, ahead=1, img=0)
            batch(7, 1, 3, 3, ahead=0, img=1)
            normalise(7)
            turned(7)
            residual_rows(7, 0, 1, bQ, 16 * (L + 3), text_rows(7))
            n, m = img_rows(2)
            residual_rows(2, 1, 2, bK, 16 * (L + 2 * IPB), h_img[0:m, 2, :], m)
            gate(7, 0, 1, 7)
            gate(2, 1, 2, B + 2, m)

            def link(ins, name):
                ins.then_inc(sort.sem, 1)
                dve.wait_ge(sort.sem, sort.at(0, name))

            def over_e(x):
                return x.unsqueeze(2).to_broadcast([P, TILES, NE])

            def over_r(x, n):
                return x.unsqueeze(1).to_broadcast([P, TILES, n])

            dve.wait_ge(fin[0].sem, fin[0].at(B - 1))
            dve.wait_ge(fin[1].sem, fin[1].at(IT - 1))
            link(v.tensor_reduce(gmax[:, :], logit[:, :, :], AX.X, ALU.max), "gmax")
            link(v.tensor_tensor(pick[:, :, :], logit[:, :, :], over_e(gmax[:, :]), ALU.is_ge), "is_max")
            link(v.tensor_tensor(pick[:, :, :], pick[:, :, :], over_r(order, NE), ALU.mult), "order")
            link(v.tensor_reduce(pmax[:, :], pick[:, :, :], AX.X, ALU.max), "pmax")
            link(v.tensor_tensor(pick[:, :, :], pick[:, :, :], over_e(pmax[:, :]), ALU.is_equal), "first")
            link(v.tensor_tensor(choice[:, :, :], pick[:, :, :], over_e(valid), ALU.mult), "choice")
            dve.wait_ge(total_ps, 1)
            link(v.tensor_scalar(ntiles[:, :], bM[0][:, 0:NE], float(P - 1), None, ALU.add), "rounded")
            link(v.tensor_copy(ntiles_i[:, :], ntiles[:, :]), "rounded_i")
            link(v.tensor_scalar(ntiles_i[:, :], ntiles_i[:, :], 7, None, ALU.arith_shift_right), "ntiles_i")
            link(v.tensor_copy(ntiles[:, :], ntiles_i[:, :]), "ntiles")
            v.tensor_copy(first_tile[:, 1:2], ntiles[:, 0:1]).then_inc(sort.sem, 1)
            link(v.tensor_tensor(first_tile[:, 2:3], ntiles[:, 0:1], ntiles[:, 1:2], ALU.add), "first2")
            link(v.tensor_tensor(first_tile[:, 3:4], first_tile[:, 2:3], ntiles[:, 2:3], ALU.add), "first3")
            dve.wait_ge(rank_ps, 1)
            link(v.scalar_tensor_tensor(place4[:, :, :], over_r(first_tile[:, :], NE), float(P),
                                        bM[1][:, 0:TILES * NE].rearrange("p (r e) -> p r e", r=TILES),
                                        ALU.mult, ALU.add), "places")
            link(v.tensor_tensor(place4[:, :, :], place4[:, :, :], choice[:, :, :], ALU.mult), "chosen")
            link(v.tensor_reduce(place[:, :], place4[:, :, :], AX.X, ALU.add), "place")
            link(v.tensor_copy(place_i[:, :], place[:, :]), "place_i")
            link(v.tensor_scalar(place_i[:, :], place_i[:, :], 7, None, ALU.arith_shift_right), "tile_i")
            link(v.tensor_copy(tile_of[:, :], place_i[:, :]), "tile")
            v.scalar_tensor_tensor(lane_of[:, :], tile_of[:, :], -float(P), place[:, :], ALU.mult, ALU.add)\
             .then_inc(sort.sem, 1)
            link(v.tensor_tensor(in_tile[:, :, :], over_r(jrow, NJ), tile_of[:, :].unsqueeze(2).to_broadcast([P, TILES, NJ]),
                                 ALU.is_equal), "in_tile")
            v.tensor_tensor(id_in_tile[:, :, :], in_tile[:, :, :], rowid.unsqueeze(2).to_broadcast([P, TILES, NJ]),
                            ALU.mult).then_inc(sort.sem, 1)
            for name, r0, r1 in (("lane_a", 0, TILES // 2), ("lane_b", TILES // 2, TILES)):
                n = r1 - r0
                v.tensor_tensor(in_lane[:, r0:r1, :], lanes.unsqueeze(1).to_broadcast([P, n, P]),
                                lane_of[:, r0:r1].unsqueeze(2).to_broadcast([P, n, P]), ALU.is_equal)\
                 .then_inc(sort.sem, 1)
            link(v.tensor_tensor(behind[:, :, :], jrow[0:1, :].unsqueeze(1).to_broadcast([1, NE - 1, NJ]),
                                 first_tile[0:1, 1:NE].unsqueeze(2).to_broadcast([1, NE - 1, NJ]), ALU.is_ge), "behind")
            link(v.tensor_reduce(expert_f[:, :], behind[:, :, :].rearrange("p e j -> p j e"), AX.X, ALU.add), "expert")
            v.tensor_copy(expert_of[:, :], expert_f[:, :]).then_inc(sort.sem, 1)
            dve.wait_ge(rows_ps, 1)
            link(v.tensor_scalar(empty[:, :], bM[0][:, 0:NJ], 0.0, float(NONE), ALU.is_equal, ALU.mult), "empty")
            link(v.scalar_tensor_tensor(rows_f[:, :], bM[0][:, 0:NJ], -1.0, empty[:, :], ALU.add, ALU.add), "rows")
            link(v.tensor_scalar(rows_g[:, :], rows_f[:, :], float(B * T - 1), None, ALU.min), "rows_g")
            v.tensor_copy(from_rows[:, :], rows_g[:, :]).then_inc(sort.sem, 1)
            link(v.tensor_copy(to_rows[:, :], rows_f[:, :]), "to_rows")

            def expert_x(j, par):
                dve.wait_ge(xtp.sem, xtp.at(j))
                dve.wait_ge(l1.sem, l1.at(j - 2))
                xt = bank[0][:, 0:D].rearrange("p (k n) -> p k n", k=K2)
                v.tensor_copy(xs[par][:, 0, :, :], xt).then_inc(xsh.sem, 1)
                dve.wait_ge(xsh.sem, xsh.at(j))
                v.tensor_tensor(xs[par][:, 1, :, :], xt, xs[par][:, 0, :, :], ALU.subtract).then_inc(xsl.sem, 1)

            def start(j, par, half):
                e = dve.value_load(expert_of[0:1, bass.ds(j, 1)], min_val=0, max_val=NE - 1)
                dve.wait_ge(gat[par], 16 + 16 * half)
                hj = res[:, bass.ds(j, 1), :].rearrange("p j n -> p (j n)")
                v.tensor_tensor(hj, xg[par][:, D:2 * D], rb[:, bass.ds(e * D + RB["b2"], D)], ALU.add).then_inc(hbs.sem, 1)

            def split(j, par):
                for n, half in enumerate("ab"):
                    s = slice(4 * n, 4 * n + 4)
                    dve.wait_ge(gel.sem, gel.at(j, f"g{4 * n + 3}"))
                    dve.wait_ge(l2.sem, l2.at(j - 2))
                    v.tensor_copy(gh[par][:, s, :], gf[:, s, :]).then_inc(gsp_h.sem, 1)
                    dve.wait_ge(gsp_h.sem, gsp_h.at(j, half))
                    v.tensor_tensor(gl[par][:, s, :], gf[:, s, :], gh[par][:, s, :], ALU.subtract).then_inc(gsp_l.sem, 1)

            def result(j, par, half):
                dve.wait_ge(l2.sem, l2.at(j))
                dve.wait_ge(hbs.sem, hbs.at(j))
                if not isinstance(half, int) or half > 0:
                    dve.wait_ge(osc[par], half * 16)
                hj = res[:, bass.ds(j, 1), :].rearrange("p j n -> p (j n)")
                v.scalar_tensor_tensor(yo[par], bank[5 + par][:, 0:D], 1 / WS, hj, ALU.mult, ALU.add).then_inc(yok.sem, 1)

            expert_x(0, 0)
            start(0, 0, 0)
            expert_x(1, 1)
            start(1, 1, 0)
            split(0, 0)
            with dve.Fori(0, NJ // 2 - 1) as i:
                for par in (1, 0):
                    j = 2 * i + (2 - par)
                    expert_x(j + 1, 1 - par)
                    split(j, par)
                    start(j + 1, 1 - par, i + 1)
                    result(j - 1, 1 - par, i)
            split(NJ - 1, 1)
            result(NJ - 2, 0, NJ // 2 - 1)
            result(NJ - 1, 1, NJ // 2 - 1)

        @block.tensor
        def _(pe):
            mm = nc.tensor.matmul
            for s in (tt_ps, qkv, mps, sps, yps, ytp, *wops, xtp, l1, l2):
                pe.sem_inc(s.sem, s.head)
            pe.wait_ge(ld_x, 32 * KP)
            for i in range(IT):
                n, m = img_rows(i)
                for k in range(KP):
                    last = mm(bank[i][0:m, 0:D], xp[:, k, IPB * i * IMG:IPB * i * IMG + m], wp[:, k, :],
                              start=k == 0, stop=k == KP - 1)
                last.then_inc(emb_ps, 1)
            pe.wait_ge(ld_c, 16)
            for i in range(IT):
                n, m = img_rows(i)
                pe.wait_ge(img, 3 * IT + 3 + i)
                for k in range(K2):
                    last = nc.tensor.transpose(bank[i][:, k * m:(k + 1) * m], x1[0:m, i, k * P:(k + 1) * P],
                                               ident[0:m, 0:m])
                last.then_inc(xt_ps, 1)
            with pe.Fori(0, B // 2) as i:
                pe.wait_ge(tt_lo.sem, tt_lo.at(i - 1))
                for b in range(2):
                    pe.wait_ge(txt.sem, txt.at(i, f"x{b}"))
                    for k in range(K2):
                        last = nc.tensor.transpose(bank[3][:, (2 * k + b) * P:(2 * k + b + 1) * P],
                                                   x1[:, b, k * P:(k + 1) * P], ident)
                last.then_inc(tt_ps.sem, 1)

            qkh, qkl = small(wsh, 0, 4 * P), small(wsl, 0, 4 * P)
            vwh, vwl = small(wsh, K2 * 4 * P, D), small(wsl, K2 * 4 * P, D)
            owh, owl = small(wsh, K2 * (4 * P + D), D), small(wsl, K2 * (4 * P + D), D)

            def project(b, a):
                xh, xl = ([xT[:, c, k, bass.ds(b, 1), :].rearrange("p b n -> p (b n)") for k in range(K2)] for c in range(2))
                if a == 0:
                    pe.wait_ge(fin[0].sem, fin[0].at(b - 4, "h"))
                    pe.wait_ge(rope.sem, rope.at(b - 1, "qo"))
                else:
                    pe.wait_ge(ynorm.sem, ynorm.at(b - 3))
                    pe.wait_ge(rope.sem, rope.at(b - 1, "ko"))
                bk = (bQ, bK)[a]
                for eo in range(2):
                    m = 2 * a + eo
                    for k in range(K2):
                        for c, (w, x) in enumerate(((qkh, xh), (qkl, xh), (qkh, xl))):
                            last = mm(bk[:, eo * T:(eo + 1) * T], w[:, k, m * P:(m + 1) * P], x[k],
                                      start=k == 0 and c == 0, stop=k == K2 - 1 and c == 2)
                last.then_inc(qkv.sem, 1)

            def project_v(b):
                pe.wait_ge(yt_lo.sem, yt_lo.at(b - 3))
                pe.wait_ge(v_lo.sem, v_lo.at(b - 1))
                for s in range(2):
                    o = bV[:, 0:D] if s == 0 else bV[0:Q2, D:2 * D]
                    for k in range(K2):
                        for c, (a, w) in enumerate(((0, vwh), (0, vwl), (1, vwh))):
                            x = xT[:, a, k, bass.ds(b, 1), (0 if s == 0 else P):(P if s == 0 else T)]\
                                .rearrange("p b n -> p (b n)")
                            last = mm(o, x, w[:, k, :], start=k == 0 and c == 0, stop=k == K2 - 1 and c == 2)
                last.then_inc(qkv.sem, 1)

            def maxima(b, par, g):
                pe.wait_ge(kz_ok.sem, kz_ok.at(b))
                if g == 0:
                    pe.wait_ge(nm_lo.sem, nm_lo.at(b - 1))
                else:
                    pe.wait_ge(mx.sem, mx.at(b, f"a{g - 1}"))
                mm(bM[0][:, :], identb, mask_a.unsqueeze(1).to_broadcast([P, GRP, P]), start=True, stop=False)
                mm(bM[0][:, :], stk[par][:, 0, g, 0:P], kz[par][:, GRP * g:GRP * g + GRP, 0:P], start=False, stop=True)\
                    .then_inc(mps.sem, 1)
                if g > 0:
                    pe.wait_ge(mx.sem, mx.at(b, f"b{g - 1}"))
                mm(bM[1][:, 0:2 * T], identb, mask_b.unsqueeze(1).to_broadcast([P, 2, T]), start=True, stop=False,
                   skip_group_check=True)
                for u in range(2):
                    last = mm(bM[1][QB * u:QB * u + QB, 0:2 * T], stk[par][:, 0, g, QB0:T],
                              kz[par][:, GRP * g + 2 * u:GRP * g + 2 * u + 2, :], start=False, stop=True,
                              skip_group_check=True)
                last.then_inc(mps.sem, 1)

            def maxima_rows(b):
                pe.wait_ge(mx.sem, mx.at(b, "w1"))
                mm(bM[0][0:HEADS, 0:P], mx_a[:, :], ident, start=True, stop=True)
                mm(bM[0][0:HEADS, P:T], mx_w[:, :, :, :].rearrange("p g u e -> p (g u e)"), fold[:, QB - Q2:QB],
                   start=True, stop=True).then_inc(mps.sem, 1)

            def scores(b, par, n):
                name, h0, hn = chunks[n]
                if n == 0:
                    pe.wait_ge(nm_lo.sem, nm_lo.at(b))
                pe.wait_ge(ex.sem, ex.at(b if n >= 2 else b - 1, chunks[n - 2][0] + "h"))
                o = bS[n % 2]
                if name[0] == "d":
                    pe.sem_inc(spare, 1)
                    mm(o[0:Q2, 0:hn * Q2], identb[0:Q2, 0:Q2], mask_t2[0:Q2, :].unsqueeze(1).to_broadcast([Q2, hn, Q2]),
                       start=True, stop=False)
                else:
                    mm(o[:, 0:hn * T], identb, mask_t.unsqueeze(1).to_broadcast([P, hn, T]), start=True, stop=False)
                for h in range(h0, h0 + hn):
                    j = h - h0
                    if name[0] == "d":
                        oj, kk, qq = o[0:Q2, j * Q2:(j + 1) * Q2], slice(P, T), slice(P, T)
                    else:
                        oj, kk, qq = o[:, j * T:(j + 1) * T], slice(0, P), slice(0, T)
                    mm(oj, sel[:, h, 0:kk.stop - kk.start], nm[par][:, qq], start=False, stop=False)
                    last = mm(oj, kz[par][:, h, kk], stk[par][:, 0, h // GRP, qq], start=False, stop=h == h0 + hn - 1)
                last.then_inc(sps.sem, 1)

            def products(b, par, n, ahead):
                name, h0, hn = chunks[n]
                pe.wait_ge(pv_l.sem, pv_l.at(b, name))
                if name == "c0":
                    pe.wait_ge(v_lo.sem, v_lo.at(b))
                    pe.wait_ge(ynorm.sem, ynorm.at(b - 1))
                    if ahead == 2:
                        pe.wait_ge(rope.sem, rope.at(b + 2, "ko"))
                for h in range(h0, h0 + hn):
                    o1 = bY[:, h * (HD + 1):(h + 1) * (HD + 1)]
                    mm(o1, ph[:, h, 0:P], vh[par][:, h, :], start=True, stop=False)
                    mm(o1, ph[:, h, 0:P], vl[par][:, h, :], start=False, stop=False)
                    mm(o1, pl[:, h, 0:P], vh[par][:, h, :], start=False, stop=True)
                    o2 = bK[0:Q2, h * (HD + 1):(h + 1) * (HD + 1)]
                    mm(o2, ph[:, h, P:T], vh[par][:, h, :], start=True, stop=False)
                    mm(o2, ph[:, h, P:T], vl[par][:, h, :], start=False, stop=False)
                    mm(o2, pl[:, h, P:T], vh[par][:, h, :], start=False, stop=False)
                    mm(o2, ph2[:, h, :], vh2[par][:, h, :], start=False, stop=False)
                    mm(o2, ph2[:, h, :], vl2[par][:, h, :], start=False, stop=False)
                    last = mm(o2, pl2[:, h, :], vh2[par][:, h, :], start=False, stop=True)
                if n == len(chunks) - 1:
                    last.then_inc(yps.sem, 1)

            def turn(b, newest):
                pe.wait_ge(ynorm.sem, ynorm.at(b))
                pe.wait_ge(v_lo.sem, v_lo.at(newest))
                for k in range(K2):
                    nc.tensor.transpose(bV[:, k * T:k * T + P], yn[:, k * P:(k + 1) * P], ident)
                    last = nc.tensor.transpose(bV[:, k * T + P:(k + 1) * T], yn2[:, k * P:(k + 1) * P],
                                               ident[0:Q2, 0:Q2])
                last.then_inc(ytp.sem, 1)

            def output(bk, u, at, m=P):
                for k in range(K2):
                    for c, (a, w) in enumerate(((0, owh), (0, owl), (1, owh))):
                        last = mm(bk[0:m, 0:D], at(a, k), w[:, k, :], start=k == 0 and c == 0, stop=k == K2 - 1 and c == 2)
                last.then_inc(wops[u].sem, 1)

            def text_output(b, ahead, img=None):
                pe.wait_ge(yt_lo.sem, yt_lo.at(b))
                if ahead == 2:
                    pe.wait_ge(rope.sem, rope.at(b + 3, "qo"))
                if img is not None:
                    pe.wait_ge(fin[1].sem, fin[1].at(img, "h"))
                pe.wait_ge(fin[0].sem, fin[0].at(b - 1, "h"))
                output(bQ, 0, lambda a, k: yT[:, a, k, IMG:T])

            def image_output(i, bk):
                n, m = img_rows(i)
                pe.wait_ge(yti.sem, yti.at(IPB * i + n - 1))
                output(bk, 1, lambda a, k: yTi[:, K2 * a + k, IPB * i:IPB * i + n, :].rearrange("p b n -> p (b n)"), m)

            def batch(t, par, prev=True, ahead=2, img=None):
                scores(t, par, 0)
                scores(t, par, 1)
                if ahead == 2:
                    project(t + 2, 0)
                if img is not None:
                    pe.wait_ge(fin[0].sem, fin[0].at(t - 2, "h"))
                    image_output(img, bQ)
                if prev:
                    turn(t - 1, t + min(ahead + 0, 1))
                scores(t, par, 2)
                if ahead == 2:
                    project(t + 2, 1)
                scores(t, par, 3)
                if prev:
                    text_output(t - 1, ahead, img)
                for g in range(GRP):
                    if ahead >= 1:
                        maxima(t + 1, 1 - par, g)
                    scores(t, par, 4 + g)
                    products(t, par, 2 + g, ahead)
                if ahead >= 1:
                    maxima_rows(t + 1)
                if ahead == 2:
                    project_v(t + 2)
                products(t, par, 6, ahead)
                products(t, par, 7, ahead)

            pe.wait_ge(wsplit_v, 2)
            pe.wait_ge(ld_small, 48)
            pe.wait_ge(pool_c, 1)
            pe.wait_ge(xt_lo, IT)
            pe.wait_ge(tt_lo.sem, tt_lo.at(B // 2 - 1))
            for b in range(2):
                project(b, 0)
                project(b, 1)
                project_v(b)
            for g in range(GRP):
                maxima(0, 0, g)
            maxima_rows(0)
            batch(0, 0, prev=False)
            with pe.Fori(0, 2) as i:
                batch(2 * i + 1, 1)
                batch(2 * i + 2, 0)
            batch(5, 1)
            batch(6, 0, ahead=1, img=0)
            batch(7, 1, ahead=0, img=1)
            turn(7, 7)
            pe.wait_ge(fin[0].sem, fin[0].at(6, "h"))
            text_output(7, 0)
            pe.wait_ge(ynorm.sem, ynorm.at(7))
            image_output(2, bK)
            pe.wait_ge(sort.sem, sort.at(0, "choice"))
            for r in range(TILES):
                last = mm(bM[0][:, 0:NE], onesb, choice[:, r, :], start=r == 0, stop=r == TILES - 1)
            last.then_inc(total_ps, 1)
            ch = chosen[:, :, :].rearrange("p r e -> p (r e)")
            for back in range(TILES):
                at = (TILES - 1 - back) * NE
                last = mm(bM[1][:, 0:TILES * NE], onesb if back else before, ch[:, at:at + TILES * NE],
                          start=back == 0, stop=back == TILES - 1)
            last.then_inc(rank_ps, 1)
            pe.wait_ge(sort.sem, sort.at(0, "lane_a"))
            for r in range(TILES):
                if r == TILES // 2:
                    pe.wait_ge(sort.sem, sort.at(0, "lane_b"))
                last = mm(bM[0][:, 0:NJ], in_lane[:, r, :], id_in_tile[:, r, :], start=r == 0, stop=r == TILES - 1)
            last.then_inc(rows_ps, 1)

            def expert_x(j, par, half):
                pe.wait_ge(gat[par], 16 + 16 * half)
                pe.wait_ge(xsl.sem, xsl.at(j - 1))
                for k in range(K2):
                    last = nc.tensor.transpose(bank[0][:, k * P:(k + 1) * P], xg[par][:, k * P:(k + 1) * P], ident)
                last.then_inc(xtp.sem, 1)

            def first(j, par):
                e = pe.value_load(expert_of[0:1, bass.ds(j, 1)], min_val=0, max_val=NE - 1)
                pe.wait_ge(xsl.sem, xsl.at(j))
                for n in range(KF):
                    if n % 4 == 0:
                        pe.wait_ge(gel.sem, gel.at(j - 1, f"g{n + 3}"))
                    for k in range(K2):
                        at = e * WN + (k * FF + n * P)
                        o = bank[1 + n // 4][:, (n % 4) * P:(n % 4 + 1) * P]
                        mm(o, w1h[:, bass.ds(at, P)], xs[par][:, 0, k, :], start=k == 0, stop=False)
                        mm(o, w1h[:, bass.ds(at, P)], xs[par][:, 1, k, :], start=False, stop=False)
                        last = mm(o, w1l[:, bass.ds(at, P)], xs[par][:, 0, k, :], start=False, stop=k == K2 - 1)
                    if n % 4 == 3:
                        last.then_inc(l1.sem, 1)

            def second(j, par):
                e = pe.value_load(expert_of[0:1, bass.ds(j, 1)], min_val=0, max_val=NE - 1)
                pe.wait_ge(yok.sem, yok.at(j - 2))
                o = bank[5 + par][:, 0:D]
                for n in range(KF):
                    if n % 4 == 0:
                        pe.wait_ge(gsp_l.sem, gsp_l.at(j, "ab"[n // 4]))
                    at = e * WN + n * D
                    mm(o, gh[par][:, n, :], w2h[:, bass.ds(at, D)], start=n == 0, stop=False)
                    mm(o, gl[par][:, n, :], w2h[:, bass.ds(at, D)], start=False, stop=False)
                    last = mm(o, gh[par][:, n, :], w2l[:, bass.ds(at, D)], start=False, stop=n == KF - 1)
                last.then_inc(l2.sem, 1)

            pe.wait_ge(sort.sem, sort.at(0, "expert_of"))
            pe.wait_ge(wlo.sem, wlo.at(B - 1))
            expert_x(0, 0, 0)
            expert_x(1, 1, 0)
            first(0, 0)
            with pe.Fori(0, NJ // 2 - 1) as i:
                for par in (1, 0):
                    j = 2 * i + (2 - par)
                    expert_x(j + 1, 1 - par, i + 1)
                    first(j, par)
                    second(j - 1, 1 - par)
            first(NJ - 1, 1)
            second(NJ - 2, 0)
            second(NJ - 1, 1)


SORT_STEPS = ("gmax is_max order pmax first choice rounded rounded_i ntiles_i ntiles first1 first2 first3 places chosen "
              "place place_i tile_i tile lane in_tile id_in_tile lane_a lane_b behind expert expert_of empty rows rows_g "
              "from_rows to_rows").split()


def layout(parts):
    at, n = {}, 0
    for name, width in parts:
        at[name] = n
        n += width
    return at, n


CF, CF_N = layout([("ident", P), ("cos", T), ("sin", T), ("fold", QB), ("headmask", GRP), ("rowid", TILES), ("valid", TILES),
                   ("lanes", P), ("order", NE), ("jrow", NJ)])
CB, CB_N = layout([("ident", P), ("mask_a", P), ("mask_b", T), ("mask_t", T), ("mask_t2", Q2), ("before", P),
                   ("ones", P), ("sel", HEADS)])
RB, ROWS = layout([("ln_w", D), ("ln_b", D), ("bo", D), ("type0", D), ("type1", D), ("wg", NE * D), ("b2", NE * D),
                   ("bg", NE)])
W_SMALL = K2 * (4 * P + 2 * D)
COLS = 4 + K2 + NE * KF


def constants():
    p = np.arange(P)
    f = np.zeros((P, CF_N), np.float32)
    f[:, CF["ident"]:CF["ident"] + P] = np.eye(P)
    t = np.arange(1, T + 1, dtype=np.float32)
    i = np.arange(ROT, dtype=np.float32)
    theta = np.power(np.float32(1.0 / 10000.0), np.float32(2.0) * i / np.float32(HD)).astype(np.float32)
    ang = t[None, :] * theta[p % ROT][:, None]
    f[:, CF["cos"]:CF["cos"] + T] = np.cos(ang) / WS
    f[:, CF["sin"]:CF["sin"] + T] = np.sin(ang) / WS
    f[:, CF["fold"]:CF["fold"] + QB] = p[:, None] % QB == np.arange(QB)[None, :]
    f[:, CF["headmask"]:CF["headmask"] + GRP] = (p[:, None] // ROT) % GRP == np.arange(GRP)[None, :]
    assert B * T <= 2048
    for b in range(B):
        f[:, CF["rowid"] + b] = b * T + IMG + p + 1
    for j in range(IT):
        f[:, CF["rowid"] + B + j] = np.where(p < img_rows(j)[1], (IPB * j + p // IMG) * T + p % IMG + 1, 0)
    f[:, CF["valid"]:CF["valid"] + TILES] = f[:, CF["rowid"]:CF["rowid"] + TILES] > 0
    f[:, CF["lanes"]:CF["lanes"] + P] = np.arange(P)
    f[:, CF["order"]:CF["order"] + NE] = NE - np.arange(NE)
    f[:, CF["jrow"]:CF["jrow"] + NJ] = np.arange(NJ)
    c = np.zeros((P, CB_N), np.float32)
    neg = np.float32(-4e10)
    c[:, CB["ident"]:CB["ident"] + P] = np.eye(P)
    c[:, CB["mask_a"]:CB["mask_a"] + P] = np.where(p[None, :] > p[:, None], neg, 0)
    key, query = np.arange(T), np.arange(T)
    c[:, CB["mask_b"]:CB["mask_b"] + T] = np.where(key[None, :] > QB0 + p[:, None] % QB, neg, 0)
    c[:, CB["mask_t"]:CB["mask_t"] + T] = np.where(p[:, None] > query[None, :], neg, 0)
    c[:, CB["mask_t2"]:CB["mask_t2"] + Q2] = np.where(p[:, None] > np.arange(Q2)[None, :], neg, 0)
    c[:, CB["before"]:CB["before"] + P] = p[:, None] < p[None, :]
    c[:, CB["ones"]:CB["ones"] + P] = 1
    c[:, CB["sel"]:CB["sel"] + HEADS] = (p[:, None] % 32 == np.arange(HEADS)[None, :]) & (p[:, None] < 64)
    bits = (c.view(np.uint32) >> 16).astype(np.uint16)
    return f, bits


def kernel(x, x_txt, mask_BS_i1_0, L0_tok_W, L0_tok_b, L0_tok_cls_token, L0_tok_pos_embedding, L0_txt_token_W,
           L0_txt_pos_W, L0_txt_type_W, L0_txt_ln_w, L0_txt_ln_b, L0_attn_Wq, L0_attn_bq, L0_attn_Wk, L0_attn_bk,
           L0_attn_Wv, L0_attn_bv, L0_attn_Wo, L0_attn_bo, L0_ffn_W1, L0_ffn_b1, L0_ffn_W2, L0_ffn_b2, L0_ffn_Wg,
           L0_ffn_bg):
    import concourse.bacc as bacc
    from concourse.bass_utils import run_bass_kernel_spmd

    a = {k: np.asarray(v) for k, v in locals().items() if k[0] in "xmL"}

    def blocks(w):
        return np.ascontiguousarray(w.reshape(-1, P, w.shape[1]).transpose(1, 0, 2))

    s = 96 // 16
    pt = a["x"].reshape(B, 3, s, 16, s, 16).transpose(1, 3, 5, 0, 2, 4).reshape(PDIM, B, PATCHES)
    pt = np.concatenate([np.zeros((PDIM, B, 1), pt.dtype), pt], axis=2).reshape(PDIM, B * IMG)
    pos = a["L0_tok_pos_embedding"][0]
    add = np.concatenate([a["L0_tok_cls_token"][0], np.tile(a["L0_tok_b"][None], (PATCHES, 1))])

    def even_odd(w):
        w = w.reshape(HEADS, ROT, 2, -1)
        return [w[:, :, j].reshape(P, -1) for j in range(2)]

    qk = np.concatenate(even_odd(a["L0_attn_Wq"]) + even_odd(a["L0_attn_Wk"])).T
    w_small = np.concatenate([blocks(w).reshape(P, -1) for w in (qk, a["L0_attn_Wv"].T, a["L0_attn_Wo"].T)], axis=1)
    cols = np.concatenate(even_odd(a["L0_attn_bq"]) + even_odd(a["L0_attn_bk"])
                          + [a["L0_attn_bv"].reshape(K2, P).T, a["L0_ffn_b1"].reshape(NE * KF, P).T], axis=1)
    rows = {"ln_w": a["L0_txt_ln_w"], "ln_b": a["L0_txt_ln_b"], "bo": a["L0_attn_bo"], "type0": a["L0_txt_type_W"][0],
            "type1": a["L0_txt_type_W"][1], "wg": a["L0_ffn_Wg"].T, "b2": a["L0_ffn_b2"], "bg": a["L0_ffn_bg"]}
    f, bits = constants()
    arrays = {
        "tok_tab": a["L0_txt_token_W"], "patches": blocks(pt), "w_patch": blocks(a["L0_tok_W"].T),
        "base_pos": np.tile(pos, (IPB, 1)), "base_add": np.tile(add, (IPB, 1)), "pos_txt": a["L0_txt_pos_W"],
        "ids": a["x_txt"].T, "types": a["mask_BS_i1_0"].T, "w_small": w_small, "cols": cols,
        "rows_b": np.concatenate([rows[k].reshape(-1) for k in RB]), "w1": a["L0_ffn_W1"], "w2": a["L0_ffn_W2"],
        "c_f32": f, "c_bits": bits,
    }
    arrays = {k: np.ascontiguousarray(v) for k, v in arrays.items()}
    nc = bacc.Bacc("TRN2", target_bir_lowering=False, num_devices=1)
    aps = {k: nc.dram_tensor(k, v.shape, mybir.dt.from_np(v.dtype), kind="ExternalInput").ap()
           for k, v in arrays.items()}
    out = nc.dram_tensor("out", (B * T, D), f32, kind="ExternalOutput").ap()
    program(nc, **aps, out=out)
    r = run_bass_kernel_spmd(nc, [arrays], core_ids=[0])
    return r.results[0]["out"].reshape(B, T, D)
```

```python
import numpy as np
import concourse.bass as bass
from concourse import mybir
from contextlib import ExitStack

f32 = mybir.dt.float32
f16 = mybir.dt.float16
bf16 = mybir.dt.bfloat16
i32 = mybir.dt.int32
u32 = mybir.dt.uint32
ALU = mybir.AluOpType
ACT = mybir.ActivationFunctionType
AX = mybir.AxisListType

B, TXT, PATCHES = 8, 128, 36
IMG = PATCHES + 1
T = IMG + TXT
D, HEADS, HD = 256, 16, 16
ROT = HD // 2
PDIM = 768
FF, NE = 1024, 4
VOCAB = 30522
P = 128
K2 = D // P
KP = PDIM // P
KF = FF // P
GRP = 4
Q2 = T - P
QB = 64
QB0 = T - QB
IPB = 3
IT = -(-B // IPB)
TILES = B + IT
CAP = 14
assert CAP == (B * T + NE * (P - 1)) // P
NJ = CAP
NONE = 1 << 20
WS = 64.0
EPS = 1e-5
LNP = float(np.log(1024.0))
SC = 1.0 / np.sqrt(np.float32(HD))
TG = 4
NPF = 4
CH = 3
HC2 = 8


def img_rows(i):
    n = min(IPB, B - IPB * i)
    return n, n * IMG


class Steps:

    LEAD = 4

    def __init__(self, sem, names, by=1):
        self.sem, self.names, self.by = sem, list(names), by
        self.head = self.LEAD * len(self.names) * by

    def at(self, r, name=None):
        k = len(self.names) if name is None else self.names.index(name) + 1
        return r * (len(self.names) * self.by) + (k * self.by + self.head)


def program(nc, tok_tab, patches, w_patch, base_pos, base_add, pos_txt, ids, types, w_small, cols, rows_b,
            w1, w2, c_f32, c_bits, out):
    ctx = ExitStack()
    with ctx:
        def sb(name, shape, dt):
            return ctx.enter_context(nc.sbuf_tensor(name, shape, dt))

        def sem(name):
            return ctx.enter_context(nc.semaphore(name))

        def steps(name, names, by=1):
            return Steps(sem(name), names.split(), by)

        cf = sb("cf", [P, CF_N], f32)
        ident = cf[:, CF["ident"]:CF["ident"] + P]
        cosw = cf[:, CF["cos"]:CF["cos"] + T]
        sinw = cf[:, CF["sin"]:CF["sin"] + T]
        fold = cf[:, CF["fold"]:CF["fold"] + QB]
        headmask = cf[:, CF["headmask"]:CF["headmask"] + GRP]
        rowid = cf[:, CF["rowid"]:CF["rowid"] + TILES]
        valid = cf[:, CF["valid"]:CF["valid"] + TILES]
        lanes = cf[:, CF["lanes"]:CF["lanes"] + P]
        order = cf[:, CF["order"]:CF["order"] + NE]
        jrow = cf[:, CF["jrow"]:CF["jrow"] + NJ]
        cb = sb("cb", [P, CB_N], bf16)
        identb = cb[:, CB["ident"]:CB["ident"] + P]
        mask_a = cb[:, CB["mask_a"]:CB["mask_a"] + P]
        mask_b = cb[:, CB["mask_b"]:CB["mask_b"] + T]
        mask_t = cb[:, CB["mask_t"]:CB["mask_t"] + T]
        mask_t2 = cb[:, CB["mask_t2"]:CB["mask_t2"] + Q2]
        before = cb[:, CB["before"]:CB["before"] + P]
        onesb = cb[:, CB["ones"]:CB["ones"] + P]
        selcol = cb[:, CB["sel"]:CB["sel"] + HEADS]
        sel = sb("sel", [P, HEADS, P], bf16)
        kz_at = 2 * K2 * FF
        shared = sb("shared", [P, kz_at + HEADS * T], f32)
        xg = [shared[:, i * 2 * D:(i + 1) * 2 * D] for i in range(2)]
        yo = [shared[:, (4 + i) * D:(5 + i) * D] for i in range(2)]
        res = shared[:, 6 * D:(6 + NJ) * D].rearrange("p (j n) -> p j n", j=NJ)
        wst = [shared[:, i * K2 * FF:(i + 1) * K2 * FF] for i in range(2)]
        kz = [shared[:, kz_at + i * HEADS * T // 2:kz_at + (i + 1) * HEADS * T // 2].bitcast(f16)
              .rearrange("p (h n) -> p h n", h=HEADS) for i in range(2)]
        wp = wst[0][:, 0:KP * D].rearrange("p (k n) -> p k n", k=KP)
        xp = wst[1][:, 0:KP * B * IMG].rearrange("p (k n) -> p k n", k=KP)
        wsm = shared[:, kz_at:kz_at + W_SMALL]
        wsh = sb("wsh", [P, W_SMALL], f16)
        wsl = sb("wsl", [P, W_SMALL], f16)

        def small(w, base, width):
            return w[:, base:base + K2 * width].rearrange("p (k n) -> p k n", k=K2)

        col = sb("col", [P, COLS], f32)
        bqk64 = sb("bqk64", [P, 4], f32)
        rb = sb("rb", [P, ROWS], f32)

        def row(name, n=1):
            return rb[:, RB[name]:RB[name] + n * D]

        w1h = sb("w1h", [P, NE * K2 * FF], f16)
        w1l = sb("w1l", [P, NE * K2 * FF], f16)
        w2h = sb("w2h", [P, NE * KF * D], f16)
        w2l = sb("w2l", [P, NE * KF * D], f16)
        ids_sb = sb("ids_sb", [P, B], i32)
        types_i = sb("types_i", [P, B], i32)
        types_f = sb("types_f", [P, B], f32)
        ptype = sb("ptype", [P, D], f32)
        typd = sb("typd", [P, D], f32)
        lnp = sb("lnp", [P, 1], f32)
        neghalf = sb("neghalf", [P, 4], f32)

        h_txt = sb("h_txt", [P, B, D], f32)
        h_img = sb("h_img", [P, IT, D], f32)
        base1 = sb("base1", [P, D], f32)
        base2 = sb("base2", [P, D], f32)
        x1 = sb("x1", [P, IT, D], f32)
        xT = sb("xT", [P, 2, K2, B, T], f16)
        st_txt = sb("st_txt", [P, 2, B, 6], f32)
        mv_txt = sb("mv_txt", [P, 2, B, 2], f32)
        ve_txt = sb("ve_txt", [P, 2, B], f32)
        rs_txt = sb("rs_txt", [P, 2, B], f32)
        off_txt = sb("off_txt", [P, 2, B], f32)
        st6 = sb("st6", [P, IT, 6], f32)
        mv = sb("mv", [P, IT, 2], f32)
        veps = sb("veps", [P, 4], f32)
        rstd = sb("rstd", [P, 4], f32)

        rot_a = sb("rot_a", [P, 2, T], f32)
        rot_b = sb("rot_b", [P, 2, T], f32)
        rot = sb("rot", [P, 2, T], f32)
        parts = [sb(f"parts{i}", [P, 2, 2, T], f16) for i in range(2)]
        stk = [sb(f"stk{i}", [P, 2, GRP, T], f16) for i in range(2)]
        flat = [sb(n, [P, HEADS * T], f16) for n in ("ph", "pl")]
        ph, pl = (t[:, :].rearrange("p (h n) -> p h n", h=HEADS) for t in flat)
        x1t = [t[:, 0:2 * TG * D].bitcast(f32).rearrange("p (b n) -> p b n", b=TG) for t in flat]
        vh = [sb(f"vh{i}", [P, HEADS, HD + 1], f16) for i in range(2)]
        vl = [sb(f"vl{i}", [P, HEADS, HD + 1], f16) for i in range(2)]
        vh2 = [sb(f"vh2{i}", [Q2, HEADS, HD + 1], f16) for i in range(2)]
        vl2 = [sb(f"vl2{i}", [Q2, HEADS, HD + 1], f16) for i in range(2)]
        mx_a = sb("mx_a", [P, HEADS], f32)
        mx_b = sb("mx_b", [P, GRP, 2], f32)
        mx_w = sb("mx_w", [P, GRP, 2, 2], f32)
        nm = [sb(f"nm{i}", [P, T], bf16) for i in range(2)]
        pf = [sb(f"pf{i}", [P, CH * T], f32) for i in range(NPF)]
        ph2 = sb("ph2", [Q2, HEADS, Q2], f16)
        pl2 = sb("pl2", [Q2, HEADS, Q2], f16)
        rden = sb("rden", [P, 2, HEADS], f32)
        yn = sb("yn", [P, D], f32)
        yn2 = sb("yn2", [Q2, D], f32)
        yT = sb("yT", [P, 2, K2, T], f16)
        yTi = sb("yTi", [P, 2 * K2, B, IMG], f16)

        rows = [sb(f"rows{i}", [P, 2 * D], f32) for i in range(3)]
        g6 = [sb(f"g6_{i}", [P, 6], f32) for i in range(2)]
        gmv = [sb(f"gmv{i}", [P, 2], f32) for i in range(2)]
        gve = [sb(f"gve{i}", [P, 1], f32) for i in range(2)]
        grs = [sb(f"grs{i}", [P, 1], f32) for i in range(2)]
        junk = sb("junk", [P, NE, D], f32)
        logit = sb("logit", [P, TILES, NE], f32)
        gmax = sb("gmax", [P, TILES], f32)
        pick = sb("pick", [P, TILES, NE], f32)
        pmax = sb("pmax", [P, TILES], f32)
        chosen = sb("chosen", [P, 2 * TILES - 1, NE], bf16)
        choice = chosen[:, TILES - 1:2 * TILES - 1, :]
        gates = [sb(f"gates{i}", [P, NE], f32) for i in range(2)]
        ntiles = sb("ntiles", [P, NE], f32)
        ntiles_i = sb("ntiles_i", [P, NE], i32)
        first_tile = sb("first_tile", [P, NE], f32)
        place4 = sb("place4", [P, TILES, NE], f32)
        place = sb("place", [P, TILES], f32)
        place_i = sb("place_i", [P, TILES], i32)
        tile_of = sb("tile_of", [P, TILES], f32)
        lane_of = sb("lane_of", [P, TILES], f32)
        in_tile = sb("in_tile", [P, TILES, NJ], f32)
        id_in_tile = sb("id_in_tile", [P, TILES, NJ], f16)
        in_lane = flat[1][:, 0:TILES * P].rearrange("p (r q) -> p r q", r=TILES)
        behind = sb("behind", [1, NE - 1, NJ], f32)
        expert_f = sb("expert_f", [1, NJ + 2], f32)
        expert_of = sb("expert_of", [1, NJ], i32)
        three_f = sb("three_f", [1, 2, NJ], f32)
        three_of = sb("three_of", [1, NJ], i32)
        empty = sb("empty", [P, NJ], f32)
        rows_f = sb("rows_f", [P, NJ], f32)
        rows_g = sb("rows_g", [P, NJ], f32)
        to_rows = sb("to_rows", [P, NJ], i32)
        from_rows = sb("from_rows", [P, NJ], i32)

        from_ids = [sb(f"from_ids{i}", [P, 1], i32) for i in range(2)]
        to_ids = [sb(f"to_ids{i}", [P, 1], i32) for i in range(2)]

        old = [t[:, :] for t in flat]
        gh = [o[:, 0:FF].rearrange("p (k n) -> p k n", k=KF) for o in old]
        gl = [o[:, FF:2 * FF].rearrange("p (k n) -> p k n", k=KF) for o in old]
        xs = [o[:, 2 * FF:2 * FF + 2 * D].rearrange("p (a k n) -> p a k n", a=2, k=K2) for o in old]
        gf = junk[:, :, :].rearrange("p e n -> p (e n)").rearrange("p (k n) -> p k n", k=KF)

        bank = [ctx.enter_context(nc.psum_tensor(f"bank{i}", [P, 512], f32)) for i in range(8)]
        bQ, bK, bV, bM, bS, bY = bank[0], bank[1], bank[2], bank[3:5], bank[5:7], bank[7]

        scr = [nc.dram_tensor(f"scr{i}", (2, 2, P // GRP, GRP, T), f16, kind="Internal").ap() for i in range(2)]
        tokrows = nc.dram_tensor("tokrows", (B * T, 2 * D), f32, kind="Internal").ap()

        ld_x = [sem(f"ld_x{i}") for i in range(KP // 2)]
        ld_txt = sem("ld_txt")
        ld_c, ld_small, ld_rows, ld_ids, ld_pos = (sem(n) for n in
                                                         "ld_c ld_small ld_rows ld_ids ld_pos".split())
        te_in = [sem(f"te_in{i}") for i in range(B // TG)]
        ld_w = [sem(f"ld_w{i}") for i in range(2)]
        spare = sem("spare")
        pool_c = sem("pool_c")
        wsplit_a, wsplit_p = sem("wsplit_a"), sem("wsplit_p")
        sel_ok = sem("sel_ok")
        emb_ps = sem("emb_ps")
        img = sem("img")
        img_rs = sem("img_rs")
        xt_ps, xt_hi, xt_lo = sem("xt_ps"), sem("xt_hi"), sem("xt_lo")
        txt_a = steps("txt_a", "e0 e1 e2 e3 p s0 s1 s2 s3 m0 m1 m2 m3 v")
        txt_b = steps("txt_b", "s0 s1 s2 s3 m0 m1 m2 m3 v")
        txt_off = [steps(f"txt_off{i}", "o") for i in range(2)]
        txt_rs = [steps(f"txt_rs{i}", "r") for i in range(2)]
        txt_n = [steps(f"txt_n{i}", "n0 n1 n2 n3") for i in range(2)]
        txt_w, txt_bias, txt_bo = steps("txt_w", "w"), steps("txt_bias", "b"), steps("txt_bo", "b")
        prep = sem("prep")
        tt_ps, tt_hi, tt_lo = sem("tt_ps"), sem("tt_hi"), sem("tt_lo")
        for x in (txt_a, txt_b, *txt_off, *txt_rs, *txt_n, txt_w, txt_bias, txt_bo):
            x.head = 0

        qkv = steps("qkv", "q k v")
        rope = steps("rope", "qe qo ke ko rot lo")
        rope_hi = steps("rope_hi", "hi")
        v_hi = steps("v_hi", "v1 v2")
        v_lo = steps("v_lo", "v1 v2")
        scr_w = [sem(f"scr_w{i}") for i in range(2)]
        stk_in = [sem(f"stk_in{i}") for i in range(2)]
        kz_ok = steps("kz_ok", "h0 h1 h2 h3")
        mps = steps("mps", "a0 b0 a1 b1 a2 b2 a3 b3 t")
        mx = steps("mx", "a0 b0 a1 b1 a2 b2 a3 b3 w0 w1")
        nm_hi = steps("nm_hi", "n")
        nm_lo = steps("nm_lo", "n")
        sps = steps("sps", "d0 d1 c0 c1 c2 c3 c4 c5")
        ex = steps("ex", "d0 d0h d1 d1h c0 c0h c1 c1h c2 c2h c3 c3h c4 c4h c5 c5h")
        pv_l = steps("pv_l", "d0 d1 c0 c1 c2 c3 c4 c5")
        yps = steps("yps", "y")
        ynorm = steps("ynorm", "r1 r2 y1 y2")
        ytp = steps("ytp", "t")
        yt_hi = steps("yt_hi", "k0 k1")
        yt_lo = steps("yt_lo", "k0 k1")
        yti = steps("yti", "c")
        wops = [steps(f"wops{i}", "o") for i in range(2)]
        fin = [steps(f"fin{i}", "h s m x g0 g1 g2 g3 l") for i in range(2)]
        fin_rs = [steps(f"fin_rs{i}", "e r") for i in range(2)]
        store = [sem(f"store{i}") for i in range(3)]
        w64 = steps("w64", "s0 h0 s1 h1")
        wlo = steps("wlo", "l0 l1")
        total_ps, rank_ps, rows_ps = sem("total_ps"), sem("rank_ps"), sem("rows_ps")
        sort = Steps(sem("sort"), SORT_STEPS)
        sort.head = 0
        gat = [sem(f"gat{i}") for i in range(2)]
        idg, ids_out = steps("idg", "c"), steps("ids_out", "c")
        hbs = steps("hbs", "b")
        xtp = steps("xtp", "t")
        xsh = steps("xsh", "h")
        xsl = steps("xsl", "l")
        l1 = steps("l1", "a b")
        gel = steps("gel", " ".join(f"g{i}" for i in range(KF)))
        gsp_h = steps("gsp_h", "a b")
        gsp_l = steps("gsp_l", "a b")
        l2 = steps("l2", "o")
        yok = steps("yok", "o")
        osc = [sem(f"osc{i}") for i in range(2)]

        chunks = [("d0", 0, HC2), ("d1", HC2, HC2)] + [(f"c{c}", CH * c, min(CH, HEADS - CH * c))
                                                       for c in range(-(-HEADS // CH))]
        W_LOADS = [(w1, w1h, w1l, e) for e in range(NE)] + [(w2, w2h, w2l, e) for e in range(NE)]
        WN = K2 * FF
        assert WN == KF * D and len(W_LOADS) == B

        SCR = 64
        STK = 64

        block = ctx.enter_context(nc.Block())

        @block.sync
        def _(sp):
            for i in range(2):
                sp.sem_inc(stk_in[i], STK * Steps.LEAD)
            for i in range(3):
                sp.sem_inc(store[i], 16 * Steps.LEAD)
            sp.dma_start(ids_sb[:, :], ids).then_inc(ld_ids, 16)
            sp.dma_start(types_i[:, :], types).then_inc(ld_txt, 16)
            sp.dma_start(ptype[:, :], pos_txt).then_inc(ld_txt, 16)
            sp.dma_start(rb[:, 0:RB["wg"]], rows_b[0:RB["wg"]].partition_broadcast(P)).then_inc(ld_txt, 16)
            for k in range(KP // 2):
                sp.dma_start(xp[:, 2 * k:2 * k + 2, :], patches[:, 2 * k:2 * k + 2, :]).then_inc(ld_x[k], 16)
                sp.dma_start(wp[:, 2 * k:2 * k + 2, :], w_patch[:, 2 * k:2 * k + 2, :]).then_inc(ld_x[k], 16)
            sp.dma_start(base1[0:IPB * IMG, :], base_pos).then_inc(ld_pos, 16)
            sp.dma_start(base2[0:IPB * IMG, :], base_add).then_inc(ld_pos, 16)
            sp.wait_ge(te_in[0], 16 * TG)
            sp.dma_start(wsm, w_small).then_inc(ld_small, 16)
            sp.dma_start(col[:, :], cols).then_inc(ld_small, 16)
            sp.dma_start(cf[:, :], c_f32).then_inc(ld_c, 16)
            sp.dma_start(cb[:, :].bitcast(mybir.dt.uint16), c_bits).then_inc(ld_small, 16)
            sp.dma_start(rb[:, RB["wg"]:ROWS], rows_b[RB["wg"]:ROWS].partition_broadcast(P)).then_inc(ld_rows, 16)

            def w_load(src, n, e):
                s = src[e].rearrange("(k p) n -> p k n", p=P)
                sp.dma_start(wst[n % 2][:, :].rearrange("p (k n) -> p k n", k=s.shape[1]), s).then_inc(ld_w[n % 2], 16)

            sp.wait_ge(emb_ps, 1)
            w_load(w1, 0, 0)
            w_load(w1, 1, 1)

            def unstack(b, par, half):
                sp.wait_ge(rope.sem, rope.at(b, "lo"))
                sp.wait_ge(rope_hi.sem, rope_hi.at(b))
                sp.wait_ge(stk_in[par], STK * Steps.LEAD + half * STK)
                for w in range(2):
                    for a in range(2):
                        sp.dma_start(scr[par][w, a].rearrange("p g n -> g p n"), parts[par][:, a, w, :])\
                            .then_inc(scr_w[par], 16)

            def stack(b, par, half):
                sp.wait_ge(scr_w[par], half * SCR + SCR)
                sp.wait_ge(sps.sem, sps.at(b - 2))
                for a in range(2):
                    sp.dma_start(stk[par][64 * a:64 * a + 64, 0, :, :].rearrange("p g n -> p (g n)"),
                                 scr[par][0, a].rearrange("p g n -> p (g n)").unsqueeze(0)
                                 .to_broadcast([2, 32, GRP * T])).then_inc(stk_in[par], 16)
                    sp.dma_start(stk[par][64 * a:64 * a + 64, 1, :, :].rearrange("p g n -> p (g n)"),
                                 scr[par][1].rearrange("c p g n -> (c p) (g n)")).then_inc(stk_in[par], 16)

            def keep(b, buf):
                sp.wait_ge(fin[0].sem, fin[0].at(b, "x"))
                sp.dma_start(tokrows[bass.ds(b * T + IMG, TXT), :], rows[buf][:, :]).then_inc(store[buf], 16)

            def keep_img(i):
                n, m = img_rows(i)
                sp.wait_ge(fin[1].sem, fin[1].at(i, "x"))
                for j in range(n):
                    sp.dma_start(tokrows[(IPB * i + j) * T:(IPB * i + j) * T + IMG, :],
                                 rows[2][j * IMG:(j + 1) * IMG, :]).then_inc(store[2], 16)

            def weights(t):
                sp.wait_ge(wlo.sem, wlo.at(t))
                src, _, _, e = W_LOADS[t + 2]
                w_load(src, t + 2, e)

            for t, par, half in ((0, 0, 0), (1, 1, 0), (2, 0, 1)):
                unstack(t, par, half)
                stack(t, par, half)
            weights(0)
            for i in range(2):
                for par in (1, 0):
                    t = 2 * i + 2 - par
                    unstack(t + 2, par, (t + 2) // 2)
                    keep(t - 1, 1 - par)
                    stack(t + 2, par, (t + 2) // 2)
                    weights(t)
            unstack(7, 1, 3)
            keep(4, 0)
            stack(7, 1, 3)
            weights(5)
            keep_img(0)
            keep(5, 1)
            keep_img(1)
            keep(6, 0)
            keep(7, 1)
            keep_img(2)
            sp.wait_ge(osc[0], 16 * ((NJ + 1) // 2))
            sp.wait_ge(osc[1], 16 * (NJ // 2))

        @block.gpsimd
        def _(pool):
            for s in (pv_l, *fin_rs, wlo, yti, idg, ids_out):
                pool.sem_inc(s.sem, s.head)
            pool.wait_ge(ld_ids, 16)
            for b in range(B):
                pool.indirect_dma_start(h_txt[:, b, :], None, tok_tab,
                                        bass.IndirectOffsetOnAxis(ids_sb[:, b:b + 1], 0)).then_inc(te_in[b // TG], 16)
            pool.memset(neghalf[:, :], -0.5)
            for i in range(2):
                pool.memset(nm[i][:, :], 0.0)
                pool.memset(vh[i][:, :, :], 1.0)
                pool.memset(vl[i][:, :, :], 0.0)
                pool.memset(vh2[i][:, :, :], 1.0)
                pool.memset(vl2[i][:, :, :], 0.0)
            pool.memset(mx_w[:, :, :, :], 0.0)
            pool.memset(logit[:, :, :], 0.0)
            pool.memset(first_tile[:, :], 0.0)
            pool.memset(expert_f[:, :], 0.0)
            pool.memset(chosen[:, :, :], 0.0)
            pool.memset(mv[:, :, :], 1.0)
            for i in range(2):
                pool.memset(gmv[i][:, :], 1.0)
            pool.memset(lnp[:, :], LNP).then_inc(pool_c, 1)

            def group(x, g):
                return x[:, TG * g:TG * g + TG]

            def inverse_std_txt(u, g):
                st = (txt_a, txt_b)[u]
                pool.wait_ge(st.sem, st.at(g, "v"))
                pool.tensor_tensor(group(rs_txt[:, u, :], g), group(ve_txt[:, u, :], g), neghalf[:, 0:TG], ALU.pow)\
                    .then_inc(txt_rs[u].sem, 1)

            def bias_txt(g):
                pool.wait_ge(txt_w.sem, txt_w.at(g))
                h = group(h_txt[:, :, :], g)
                pool.tensor_tensor(h, h, row("ln_b").unsqueeze(1).to_broadcast([P, TG, D]), ALU.add)\
                    .then_inc(txt_bias.sem, 1)

            pool.wait_ge(pool_c, 1)
            inverse_std_txt(0, 0)
            inverse_std_txt(0, 1)
            bias_txt(0)
            pool.wait_ge(img, 3 * IT + 2)
            pool.tensor_tensor(rstd[:, 0:IT], veps[:, 0:IT], neghalf[:, 0:IT], ALU.pow).then_inc(img_rs, 1)
            bias_txt(1)
            def w_small_low(c):
                pool.wait_ge(wsplit_a, 2)
                pool.tensor_tensor(wsl[:, c], wsm[:, c], wsh[:, c], ALU.subtract).then_inc(wsplit_p, 1)

            inverse_std_txt(1, 0)
            w_small_low(slice(0, K2 * 4 * P))
            inverse_std_txt(1, 1)
            w_small_low(slice(K2 * 4 * P, W_SMALL))
            for g in range(B // TG):
                pool.wait_ge(txt_n[1].sem, txt_n[1].at(g))
                h = group(h_txt[:, :, :], g)
                pool.tensor_tensor(h, h, row("bo").unsqueeze(1).to_broadcast([P, TG, D]), ALU.add).then_inc(txt_bo.sem, 1)
            pool.wait_ge(img, 4 * IT + 2)
            for i in range(IT):
                n, m = img_rows(i)
                pool.tensor_tensor(h_img[0:m, i, :], h_img[0:m, i, :], row("bo")[0:m, :], ALU.add).then_inc(img_rs, 1)

            def low(b, n):
                name, h0, hn = chunks[n]
                pool.wait_ge(ex.sem, ex.at(b, name + "h"))
                if name[0] == "d":
                    pool.tensor_tensor(pl2[:, h0:h0 + hn, :], pf[n % NPF][0:Q2, 0:hn * Q2]
                                       .rearrange("p (h n) -> p h n", h=hn), ph2[:, h0:h0 + hn, :], ALU.subtract)\
                        .then_inc(pv_l.sem, 1)
                else:
                    pool.tensor_tensor(pl[:, h0:h0 + hn, :], pf[n % NPF][:, 0:hn * T]
                                       .rearrange("p (h n) -> p h n", h=hn), ph[:, h0:h0 + hn, :], ALU.subtract)\
                        .then_inc(pv_l.sem, 1)

            def image_columns(b):
                pool.wait_ge(yt_hi.sem, yt_hi.at(b))
                pool.wait_ge(yt_lo.sem, yt_lo.at(b))
                pool.tensor_copy(yTi[:, :, bass.ds(b, 1), :].rearrange("p a b n -> p a (b n)"),
                                 yT[:, :, :, 0:IMG].rearrange("p a k n -> p (a k) n")).then_inc(yti.sem, 1)

            def inverse_std(r, u):
                pool.wait_ge(fin[u].sem, fin[u].at(r, "m"))
                pool.tensor_scalar(gve[u][:, :], gmv[u][:, 1:2], EPS, None, ALU.add).then_inc(fin_rs[u].sem, 1)
                pool.wait_ge(fin_rs[u].sem, fin_rs[u].at(r, "e"))
                pool.tensor_tensor(grs[u][:, :], gve[u][:, :], neghalf[:, 0:1], ALU.pow).then_inc(fin_rs[u].sem, 1)

            def w_low(n, k):
                _, hi, lo, e = W_LOADS[n]
                c = slice(k * WN // 2, (k + 1) * WN // 2)
                pool.wait_ge(w64.sem, w64.at(n, f"h{k}"))
                pool.tensor_tensor(lo[:, e * WN + c.start:e * WN + c.stop], wst[n % 2][:, c],
                                   hi[:, e * WN + c.start:e * WN + c.stop], ALU.subtract).then_inc(wlo.sem, 1)

            def batch(t, prev=True, img=None):
                w_low(t, 0)
                low(t, 0)
                low(t, 1)
                w_low(t, 1)
                if img is not None:
                    inverse_std(img, 1)
                low(t, 2)
                if prev:
                    image_columns(t - 1)
                low(t, 3)
                low(t, 4)
                low(t, 5)
                if prev:
                    inverse_std(t - 1, 0)
                low(t, 6)
                low(t, 7)

            batch(0, prev=False)
            for t in range(1, 6):
                batch(t)
            batch(6, img=0)
            batch(7, img=1)
            image_columns(7)
            inverse_std(7, 0)
            inverse_std(2, 1)

            pool.wait_ge(store[0], 16 * (Steps.LEAD + B // 2))
            pool.wait_ge(store[1], 16 * (Steps.LEAD + B // 2))
            pool.wait_ge(store[2], 16 * (Steps.LEAD + B))
            pool.wait_ge(sort.sem, sort.at(0, "from_rows"))

            def gather(j, par):
                pool.tensor_copy(from_ids[par][:, :], from_rows[:, bass.ds(j, 1)]).then_inc(idg.sem, 1)
                pool.wait_ge(idg.sem, idg.at(j))
                pool.sem_inc(spare, 1)
                pool.indirect_dma_start(xg[par][:, :], None, tokrows,
                                        bass.IndirectOffsetOnAxis(from_ids[par][:, :], 0)).then_inc(gat[par], 16)

            def scatter_out(j, par):
                pool.tensor_copy(to_ids[par][:, :], to_rows[:, bass.ds(j, 1)]).then_inc(ids_out.sem, 1)
                pool.wait_ge(ids_out.sem, ids_out.at(j))
                pool.wait_ge(yok.sem, yok.at(j))
                pool.sem_inc(spare, 1)
                pool.indirect_dma_start(out, bass.IndirectOffsetOnAxis(to_ids[par][:, :], 0),
                                        yo[par], None,
                                        bounds_check=B * T - 1, oob_is_err=False).then_inc(osc[par], 16)

            def gather_next(j, par):
                pool.wait_ge(xtp.sem, xtp.at(j - 2))
                pool.wait_ge(hbs.sem, hbs.at(j - 2))
                gather(j, par)

            gather(0, 0)
            gather(1, 1)
            pool.wait_ge(sort.sem, sort.at(0, "to_rows"))
            for j in (2, 3):
                gather_next(j, j % 2)
            scatter_out(0, 0)
            gather_next(4, 0)
            scatter_out(1, 1)
            gather_next(5, 1)
            with pool.Fori(1, NJ // 2 - 2) as i:
                for par in range(2):
                    pool.wait_ge(osc[par], i * 16)
                    scatter_out(2 * i + par, par)
                    gather_next(2 * i + par + 4, par)
            for j in range(NJ - 4, NJ):
                pool.wait_ge(osc[j % 2], 16 * (j // 2))
                scatter_out(j, j % 2)

        @block.scalar
        def _(act):
            for s in (rope_hi, v_hi, nm_hi, ex, yt_hi, w64, gel):
                act.sem_inc(s.sem, s.head)

            def normalise_txt(u, g):
                act.wait_ge(txt_off[u].sem, txt_off[u].at(g))
                for k in range(TG):
                    b = TG * g + k
                    act.activation(h_txt[:, b, :] if u == 0 else x1t[g][:, k, :], h_txt[:, b, :], ACT.Identity,
                                   bias=off_txt[:, u, b:b + 1], scale=rs_txt[:, u, b:b + 1]).then_inc(txt_n[u].sem, 1)

            def transposed_txt(g):
                for q in range(TG // 2 * g, TG // 2 * (g + 1)):
                    act.wait_ge(tt_ps, q + 1)
                    act.activation(xT[:, 0, :, 2 * q:2 * q + 2, IMG:T],
                                   bank[3 + q][:, :].rearrange("p (k b n) -> p k b n", k=K2, b=2), ACT.Copy)\
                       .then_inc(tt_hi, 1)

            normalise_txt(0, 0)
            act.wait_ge(ld_small, 48)
            act.activation(wsm, wsm, ACT.Copy, scale=WS).then_inc(wsplit_a, 1)
            normalise_txt(0, 1)
            act.wait_ge(wsplit_a, 1)
            act.activation(wsh[:, :], wsm, ACT.Copy).then_inc(wsplit_a, 1)
            act.activation(bqk64[:, :], col[:, 0:4], ACT.Copy, scale=WS).then_inc(wsplit_a, 1)
            for i in range(IT):
                n, m = img_rows(i)
                act.wait_ge(xt_ps, i + 1)
                act.activation(xT[:, 0, :, IPB * i:IPB * i + n, 0:IMG],
                               bank[i][:, 0:K2 * m].rearrange("p (k b n) -> p k b n", k=K2, b=n), ACT.Copy)\
                   .then_inc(xt_hi, 1)
            normalise_txt(1, 0)
            transposed_txt(0)
            normalise_txt(1, 1)

            def rope_high(b, par):
                act.wait_ge(rope.sem, rope.at(b, "rot"))
                act.wait_ge(scr_w[par], (b // 2) * SCR) if b >= 2 else None
                act.activation(parts[par][:, 0, :, :], rot[:, :, :], ACT.Copy).then_inc(rope_hi.sem, 1)

            def v_high(b, par):
                act.wait_ge(qkv.sem, qkv.at(b, "v"))
                act.wait_ge(yps.sem, yps.at(b - 2))
                act.activation(vh[par][:, :, 0:HD], bV[:, 0:D].rearrange("p (h n) -> p h n", h=HEADS), ACT.Copy,
                               scale=1 / WS).then_inc(v_hi.sem, 1)
                act.activation(vh2[par][:, :, 0:HD], bV[0:Q2, D:2 * D].rearrange("p (h n) -> p h n", h=HEADS), ACT.Copy,
                               scale=1 / WS).then_inc(v_hi.sem, 1)

            def exps(b, n):
                name, h0, hn = chunks[n]
                act.wait_ge(sps.sem, sps.at(b, name))
                act.wait_ge(pv_l.sem, pv_l.at(b if n >= NPF else b - 1, chunks[n - NPF][0]))
                m, w = (Q2, Q2) if name[0] == "d" else (P, T)
                s = bS[n % 2][0:m, 0:hn * w]
                act.activation(pf[n % NPF][0:m, 0:hn * w], s, ACT.Exp, bias=lnp[0:m, :], scale=SC).then_inc(ex.sem, 1)
                act.wait_ge(yps.sem, yps.at(b - 1))
                act.activation((ph2 if name[0] == "d" else ph)[:, h0:h0 + hn, :], s.rearrange("p (h n) -> p h n", h=hn),
                               ACT.Exp, bias=lnp[0:m, :], scale=SC).then_inc(ex.sem, 1)

            def turned(b):
                act.wait_ge(ytp.sem, ytp.at(b))
                act.wait_ge(wops[0].sem, wops[0].at(b - 1))
                act.wait_ge(yti.sem, yti.at(b - 1))
                for k in range(K2):
                    act.activation(yT[:, 0, k, :], bV[:, k * T:(k + 1) * T], ACT.Identity, bias=col[:, 4 + k:5 + k])\
                       .then_inc(yt_hi.sem, 1)

            def maxima(b, par):
                act.wait_ge(mps.sem, mps.at(b, "t"))
                act.wait_ge(sps.sem, sps.at(b - 2))
                act.activation(nm[par][0:HEADS, :], bM[0][0:HEADS, 0:T], ACT.Copy, scale=-1.0).then_inc(nm_hi.sem, 1)

            def w_scale(n, k):
                c = slice(k * WN // 2, (k + 1) * WN // 2)
                act.wait_ge(ld_w[n % 2], 16 * (n // 2 + 1))
                act.activation(wst[n % 2][:, c], wst[n % 2][:, c], ACT.Copy, scale=WS).then_inc(w64.sem, 1)

            def w_high(n, k):
                _, hi, _, e = W_LOADS[n]
                c = slice(k * WN // 2, (k + 1) * WN // 2)
                act.wait_ge(w64.sem, w64.at(n, f"s{k}"))
                act.activation(hi[:, e * WN + c.start:e * WN + c.stop], wst[n % 2][:, c], ACT.Copy).then_inc(w64.sem, 1)

            def batch(t, par, prev=True, ahead=2):
                exps(t, 0)
                exps(t, 1)
                if prev:
                    turned(t - 1)
                exps(t, 2)
                if t + 1 < B:
                    w_scale(t + 1, 0)
                exps(t, 3)
                if ahead == 2:
                    rope_high(t + 2, par)
                if t + 1 < B:
                    w_high(t + 1, 0)
                exps(t, 4)
                exps(t, 5)
                if t + 1 < B:
                    w_scale(t + 1, 1)
                exps(t, 6)
                if t + 1 < B:
                    w_high(t + 1, 1)
                exps(t, 7)
                if ahead >= 1:
                    maxima(t + 1, 1 - par)
                if ahead == 2:
                    v_high(t + 2, par)

            act.wait_ge(pool_c, 1)
            for b in range(2):
                rope_high(b, b)
                v_high(b, b)
                if b == 0:
                    transposed_txt(1)
            for k in range(2):
                w_scale(0, k)
                w_high(0, k)
            maxima(0, 0)
            batch(0, 0, prev=False)
            for t in range(1, B):
                batch(t, t % 2, ahead=min(2, B - 1 - t))
            turned(7)

            def gelus(j):
                e = act.value_load(expert_of[0:1, bass.ds(j, 1)], min_val=0, max_val=NE - 1)
                for n in range(KF):
                    if n % 4 == 0:
                        half = "ab"[n // 4]
                        act.wait_ge(l1.sem, l1.at(j, half))
                        act.wait_ge(gsp_l.sem, gsp_l.at(j - 1, half))
                    act.activation(gf[:, n, :], bank[1 + n // 4][:, (n % 4) * P:(n % 4 + 1) * P], ACT.Gelu,
                                   bias=col[:, bass.ds(e * KF + (6 + n), 1)], scale=1 / WS).then_inc(gel.sem, 1)

            act.wait_ge(sort.sem, sort.at(0, "expert_of"))
            gelus(0)
            gelus(1)
            with act.Fori(1, NJ // 2) as i:
                for par in range(2):
                    gelus(2 * i + par)

        @block.vector
        def _(dve):
            v = dve
            for s in (rope, v_lo, kz_ok, mx, nm_lo, ynorm, yt_lo, *fin, hbs, xsl, xsh, gsp_h, gsp_l,
                      yok):
                dve.sem_inc(s.sem, s.head)

            def group(x, g):
                return x[:, TG * g:TG * g + TG]

            def over_tiles(x):
                return x.unsqueeze(1).to_broadcast([P, TG, D])

            def statistics_txt(u, g):
                st = (txt_a, txt_b)[u]
                for k in range(TG):
                    v.bn_stats(st_txt[:, u, TG * g + k, :], h_txt[:, TG * g + k, :]).then_inc(st.sem, 1)
                for k in range(TG):
                    dve.wait_ge(st.sem, st.at(g, f"s{k}"))
                    v.bn_aggr(mv_txt[:, u, TG * g + k, :], st_txt[:, u, TG * g + k, :]).then_inc(st.sem, 1)
                dve.wait_ge(st.sem, st.at(g, f"m{TG - 1}"))
                v.tensor_scalar(group(ve_txt[:, u, :], g), group(mv_txt[:, u, :, 1], g), EPS, None, ALU.add)\
                 .then_inc(st.sem, 1)

            def embed_txt(g):
                dve.wait_ge(te_in[g], 16 * TG)
                for k in range(TG):
                    b = TG * g + k
                    v.scalar_tensor_tensor(h_txt[:, b, :], typd[:, :], types_f[:, b:b + 1], h_txt[:, b, :],
                                           ALU.mult, ALU.add).then_inc(txt_a.sem, 1)
                dve.wait_ge(txt_a.sem, txt_a.at(g, f"e{TG - 1}"))
                h = group(h_txt[:, :, :], g)
                v.tensor_tensor(h, h, over_tiles(ptype[:, :]), ALU.add).then_inc(txt_a.sem, 1)
                dve.wait_ge(txt_a.sem, txt_a.at(g, "p"))
                statistics_txt(0, g)

            def offset_txt(u, g):
                dve.wait_ge(txt_rs[u].sem, txt_rs[u].at(g))
                v.scalar_tensor_tensor(group(off_txt[:, u, :], g), group(mv_txt[:, u, :, 0], g), -1.0,
                                       group(rs_txt[:, u, :], g), ALU.mult, ALU.mult).then_inc(txt_off[u].sem, 1)

            def weigh_txt(g):
                dve.wait_ge(txt_n[0].sem, txt_n[0].at(g))
                h = group(h_txt[:, :, :], g)
                v.tensor_tensor(h, h, over_tiles(row("ln_w")), ALU.mult).then_inc(txt_w.sem, 1)

            def transposed_txt(g):
                for q in range(TG // 2 * g, TG // 2 * (g + 1)):
                    dve.wait_ge(tt_hi, q + 1)
                    x = xT[:, :, :, 2 * q:2 * q + 2, IMG:T]
                    v.tensor_tensor(x[:, 1], bank[3 + q][:, :].rearrange("p (k b n) -> p k b n", k=K2, b=2), x[:, 0],
                                    ALU.subtract).then_inc(tt_lo, 1)

            dve.wait_ge(ld_txt, 48)
            v.tensor_copy(types_f[:, :], types_i[:, :]).then_inc(prep, 1)
            v.tensor_tensor(typd[:, :], row("type1"), row("type0"), ALU.subtract).then_inc(prep, 1)
            v.tensor_tensor(ptype[:, :], ptype[:, :], row("type0"), ALU.add).then_inc(prep, 1)
            dve.wait_ge(prep, 3)
            embed_txt(0)
            embed_txt(1)
            offset_txt(0, 0)
            dve.wait_ge(ld_pos, 32)
            v.tensor_tensor(base1[0:IPB * IMG, :], base1[0:IPB * IMG, :], base2[0:IPB * IMG, :], ALU.add).then_inc(img, 1)
            offset_txt(0, 1)
            weigh_txt(0)
            dve.wait_ge(img, 1)
            dve.wait_ge(pool_c, 1)
            for i in range(IT):
                n, m = img_rows(i)
                dve.wait_ge(emb_ps, 1)
                v.tensor_tensor(h_img[0:m, i, :], bank[i][0:m, 0:D], base1[0:m, :], ALU.add).then_inc(img, 1)
            for i in range(IT):
                n, m = img_rows(i)
                dve.wait_ge(img, i + 2)
                v.bn_stats(st6[0:m, i, :], h_img[0:m, i, :]).then_inc(img, 1)
            for i in range(IT):
                n, m = img_rows(i)
                dve.wait_ge(img, IT + 2 + i)
                v.bn_aggr(mv[0:m, i, :], st6[0:m, i, :]).then_inc(img, 1)
            dve.wait_ge(img, 3 * IT + 1)
            v.tensor_scalar(veps[:, 0:IT], mv[:, :, 1], EPS, None, ALU.add).then_inc(img, 1)
            weigh_txt(1)
            dve.wait_ge(txt_bias.sem, txt_bias.at(0))
            statistics_txt(1, 0)
            dve.wait_ge(img_rs, 1)
            for i in range(IT):
                n, m = img_rows(i)
                v.tensor_scalar(x1[0:m, i, :], h_img[0:m, i, :], mv[0:m, i, 0:1], rstd[0:m, i:i + 1],
                                ALU.subtract, ALU.mult).then_inc(img, 1)
            offset_txt(1, 0)
            dve.wait_ge(txt_bias.sem, txt_bias.at(1))
            statistics_txt(1, 1)
            for i in range(IT):
                n, m = img_rows(i)
                dve.wait_ge(xt_hi, i + 1)
                v.tensor_tensor(xT[:, 1, :, IPB * i:IPB * i + n, 0:IMG],
                                bank[i][:, 0:K2 * m].rearrange("p (k b n) -> p k b n", k=K2, b=n),
                                xT[:, 0, :, IPB * i:IPB * i + n, 0:IMG], ALU.subtract).then_inc(xt_lo, 1)
            offset_txt(1, 1)
            transposed_txt(0)

            def rotate(b, a):
                bk, one, two = ((bQ, "qe", "qo"), (bK, "ke", "ko"))[a]
                dve.wait_ge(qkv.sem, qkv.at(b, "qk"[a]))
                if a == 0:
                    dve.wait_ge(rope.sem, rope.at(b - 1, "rot"))
                v.scalar_tensor_tensor(rot_a[:, a, :], bk[:, 0:T], bqk64[:, 2 * a:2 * a + 1], cosw, ALU.add, ALU.mult)\
                 .then_inc(rope.sem, 1)
                v.scalar_tensor_tensor(rot_b[:, a, :], bk[:, T:2 * T], bqk64[:, 2 * a + 1:2 * a + 2], sinw,
                                       ALU.add, ALU.mult).then_inc(rope.sem, 1)
                if a == 1:
                    dve.wait_ge(rope.sem, rope.at(b, "ko"))
                    dve.wait_ge(rope_hi.sem, rope_hi.at(b - 1))
                    v.tensor_tensor(rot[:, :, :], rot_a[:, :, :], rot_b[:, :, :], ALU.subtract).then_inc(rope.sem, 1)

            def rope_low(b, par, half):
                dve.wait_ge(rope_hi.sem, rope_hi.at(b))
                if not isinstance(half, int) or half > 0:
                    dve.wait_ge(scr_w[par], half * SCR)
                v.tensor_tensor(parts[par][:, 1, :, :], rot[:, :, :], parts[par][:, 0, :, :], ALU.subtract)\
                 .then_inc(rope.sem, 1)

            def v_low(b, par):
                dve.wait_ge(v_hi.sem, v_hi.at(b))
                v.scalar_tensor_tensor(vl[par][:, :, 0:HD], bV[:, 0:D].rearrange("p (h n) -> p h n", h=HEADS), 1 / WS,
                                       vh[par][:, :, 0:HD], ALU.mult, ALU.subtract).then_inc(v_lo.sem, 1)
                v.scalar_tensor_tensor(vl2[par][:, :, 0:HD], bV[0:Q2, D:2 * D].rearrange("p (h n) -> p h n", h=HEADS),
                                       1 / WS, vh2[par][:, :, 0:HD], ALU.mult, ALU.subtract).then_inc(v_lo.sem, 1)

            def spread(b, par, half):
                dve.wait_ge(stk_in[par], STK * (Steps.LEAD + 1) + half * STK)
                dve.wait_ge(sps.sem, sps.at(b - 2))
                kv = kz[par][:, :, :].rearrange("p (g h) n -> p g h n", g=GRP)
                for h in range(GRP):
                    v.tensor_scalar(kv[:, :, h, :], stk[par][:, 1, :, :], headmask[:, h:h + 1], None, ALU.mult)\
                     .then_inc(kz_ok.sem, 1)

            def maxima(b, g, pairs=(bM,)):
                bM = pairs[g % len(pairs)]
                dve.wait_ge(mps.sem, mps.at(b, f"a{g}"))
                if g == 0:
                    dve.wait_ge(mps.sem, mps.at(b - 1))
                v.tensor_reduce(mx_a[:, GRP * g:GRP * g + GRP], bM[0][:, :].rearrange("p (h n) -> p h n", h=GRP),
                                AX.X, ALU.max).then_inc(mx.sem, 1)
                dve.wait_ge(mps.sem, mps.at(b, f"b{g}"))
                v.tensor_reduce(mx_b[:, g, :], bM[1][:, 0:2 * T].rearrange("p (h n) -> p h n", h=2),
                                AX.X, ALU.max).then_inc(mx.sem, 1)
                if g == GRP - 1:
                    dve.wait_ge(mx.sem, mx.at(b, "b3"))
                    for u in range(2):
                        v.tensor_copy(mx_w[QB * u:QB * u + QB, :, u, :], mx_b[QB * u:QB * u + QB, :, :]).then_inc(mx.sem, 1)

            def maxima_low(b, par):
                dve.wait_ge(nm_hi.sem, nm_hi.at(b))
                dve.wait_ge(sps.sem, sps.at(b - 2))
                v.scalar_tensor_tensor(nm[par][32:32 + HEADS, :], bM[0][0:HEADS, 0:T], -1.0, nm[par][0:HEADS, :],
                                       ALU.mult, ALU.subtract).then_inc(nm_lo.sem, 1)

            def normalise(b):
                dve.wait_ge(yps.sem, yps.at(b))
                y1 = bY[:, 0:HEADS * (HD + 1)].rearrange("p (h n) -> p h n", h=HEADS)
                y2 = bK[0:Q2, 0:HEADS * (HD + 1)].rearrange("p (h n) -> p h n", h=HEADS)
                v.reciprocal(rden[:, 0, :], y1[:, :, HD]).then_inc(ynorm.sem, 1)
                v.reciprocal(rden[0:Q2, 1, :], y2[:, :, HD]).then_inc(ynorm.sem, 1)
                dve.wait_ge(ytp.sem, ytp.at(b - 1))
                dve.wait_ge(ynorm.sem, ynorm.at(b, "r1"))
                v.tensor_tensor(yn[:, :].rearrange("p (h n) -> p h n", h=HEADS), y1[:, :, 0:HD],
                                rden[:, 0, :].unsqueeze(2).to_broadcast([P, HEADS, HD]), ALU.mult).then_inc(ynorm.sem, 1)
                dve.wait_ge(ynorm.sem, ynorm.at(b, "r2"))
                v.tensor_tensor(yn2[:, :].rearrange("p (h n) -> p h n", h=HEADS), y2[:, :, 0:HD],
                                rden[0:Q2, 1, :].unsqueeze(2).to_broadcast([Q2, HEADS, HD]), ALU.mult)\
                 .then_inc(ynorm.sem, 1)

            def turned(b):
                dve.wait_ge(yt_hi.sem, yt_hi.at(b))
                for k in range(K2):
                    v.scalar_tensor_tensor(yT[:, 1, k, :], bV[:, k * T:(k + 1) * T], col[:, 4 + k:5 + k], yT[:, 0, k, :],
                                           ALU.add, ALU.subtract).then_inc(yt_lo.sem, 1)

            def residual_rows(r, u, buf, bk, kept, residual, m=P):
                dve.wait_ge(wops[u].sem, wops[u].at(r))
                dve.wait_ge(store[buf], kept)
                hr = rows[buf][0:m, D:2 * D]
                v.scalar_tensor_tensor(hr, bk[0:m, 0:D], 1 / WS, residual, ALU.mult, ALU.add).then_inc(fin[u].sem, 1)
                dve.wait_ge(fin[u].sem, fin[u].at(r, "h"))
                dve.sem_inc(spare, 1)
                v.bn_stats(g6[u][0:m, :], hr).then_inc(fin[u].sem, 1)
                dve.wait_ge(fin[u].sem, fin[u].at(r, "s"))
                dve.wait_ge(fin_rs[u].sem, fin_rs[u].at(r - 1))
                dve.sem_inc(spare, 1)
                v.bn_aggr(gmv[u][0:m, :], g6[u][0:m, :]).then_inc(fin[u].sem, 1)

            def gate(r, u, buf, at, m=P, parts=(0, 1)):
                hr = rows[buf][0:m, D:2 * D]
                xr = rows[buf][0:m, 0:D]
                if 0 in parts:
                    dve.wait_ge(fin_rs[u].sem, fin_rs[u].at(r))
                    v.tensor_scalar(xr, hr, gmv[u][0:m, 0:1], grs[u][0:m, :], ALU.subtract, ALU.mult)\
                     .then_inc(fin[u].sem, 1)
                    dve.wait_ge(fin[u].sem, fin[u].at(r, "x"))
                for e in (e for part in parts for e in range(2 * part, 2 * part + 2)):
                    v.tensor_tensor_reduce(out=junk[0:m, e, :], in0=xr, in1=rb[0:m, RB["wg"] + e * D:RB["wg"] + (e + 1) * D],
                                           scale=1.0, scalar=0.0, op0=ALU.mult, op1=ALU.add,
                                           accum_out=gates[u][0:m, e:e + 1]).then_inc(fin[u].sem, 1)
                if 1 in parts:
                    dve.wait_ge(fin[u].sem, fin[u].at(r, "g3"))
                    v.tensor_tensor(logit[0:m, bass.ds(at, 1), :].rearrange("p r e -> p (r e)"), gates[u][0:m, :],
                                    rb[0:m, RB["bg"]:RB["bg"] + NE], ALU.add).then_inc(fin[u].sem, 1)

            def text_rows(b):
                return h_txt[:, bass.ds(b, 1), :].rearrange("p b n -> p (b n)")

            L = Steps.LEAD

            def batch(t, par, half, before, prev=True, ahead=2, img=None):
                if prev:
                    normalise(t - 1)
                if prev and ahead >= 1:
                    v_low(t + 1, 1 - par)
                if ahead == 2:
                    rotate(t + 2, 0)
                if img is not None:
                    residual_rows(img, 1, 2, bQ, 16 * (L + IPB * img), h_img[0:img_rows(img)[1], img, :], img_rows(img)[1])
                if prev:
                    turned(t - 1)
                if ahead == 2:
                    rotate(t + 2, 1)
                if ahead >= 1:
                    spread(t + 1, 1 - par, before + 1)
                if img is not None:
                    gate(img, 1, 2, B + img, img_rows(img)[1])
                if ahead >= 1:
                    maxima(t + 1, 0)
                if ahead == 2:
                    rope_low(t + 2, par, half + 1)
                if prev:
                    residual_rows(t - 1, 0, 1 - par, bQ, 16 * L + before * 16, text_rows(t - 1))
                if ahead >= 1:
                    maxima(t + 1, 1)
                if ahead >= 1:
                    maxima(t + 1, 2)
                if ahead >= 1:
                    maxima(t + 1, 3)
                if prev:
                    gate(t - 1, 0, 1 - par, t - 1, parts=(0,))
                if ahead >= 1:
                    maxima_low(t + 1, 1 - par)
                if prev:
                    gate(t - 1, 0, 1 - par, t - 1, parts=(1,))

            dve.wait_ge(wsplit_a, 3)
            dve.wait_ge(ld_c, 16)
            for b in range(2):
                rotate(b, 0)
                rotate(b, 1)
                rope_low(b, b, 0)
                v_low(b, b)
                if b == 0:
                    transposed_txt(1)
                else:
                    v.tensor_copy(sel[:, :, :], selcol.unsqueeze(2).to_broadcast([P, HEADS, P])).then_inc(sel_ok, 1)
            spread(0, 0, 0)
            for g in range(GRP):
                maxima(0, g, (bM, bS))
            maxima_low(0, 0)
            dve.wait_ge(txt_bo.sem, txt_bo.at(B // TG - 1))
            dve.wait_ge(ld_rows, 16)
            dve.wait_ge(img_rs, 1 + IT)
            batch(0, 0, 0, -1, prev=False)
            with dve.Fori(0, 2) as i:
                batch(2 * i + 1, 1, i, i)
                batch(2 * i + 2, 0, i + 1, i)
            batch(5, 1, 2, 2)
            batch(6, 0, 3, 2, ahead=1, img=0)
            batch(7, 1, 3, 3, ahead=0, img=1)
            normalise(7)
            turned(7)
            residual_rows(7, 0, 1, bQ, 16 * (L + 3), text_rows(7))
            n, m = img_rows(2)
            residual_rows(2, 1, 2, bK, 16 * (L + 2 * IPB), h_img[0:m, 2, :], m)
            gate(7, 0, 1, 7)
            gate(2, 1, 2, B + 2, m)

            def link(ins, name):
                ins.then_inc(sort.sem, 1)
                dve.wait_ge(sort.sem, sort.at(0, name))

            def over_e(x):
                return x.unsqueeze(2).to_broadcast([P, TILES, NE])

            def over_r(x, n):
                return x.unsqueeze(1).to_broadcast([P, TILES, n])

            dve.wait_ge(fin[0].sem, fin[0].at(B - 1))
            dve.wait_ge(fin[1].sem, fin[1].at(IT - 1))
            link(v.tensor_reduce(gmax[:, :], logit[:, :, :], AX.X, ALU.max), "gmax")
            link(v.tensor_tensor(pick[:, :, :], logit[:, :, :], over_e(gmax[:, :]), ALU.is_ge), "is_max")
            link(v.tensor_tensor(pick[:, :, :], pick[:, :, :], over_r(order, NE), ALU.mult), "order")
            link(v.tensor_reduce(pmax[:, :], pick[:, :, :], AX.X, ALU.max), "pmax")
            link(v.tensor_tensor(pick[:, :, :], pick[:, :, :], over_e(pmax[:, :]), ALU.is_equal), "first")
            link(v.tensor_tensor(choice[:, :, :], pick[:, :, :], over_e(valid), ALU.mult), "choice")
            dve.wait_ge(total_ps, 1)
            link(v.tensor_scalar(ntiles[:, :], bM[0][:, 0:NE], float(P - 1), None, ALU.add), "rounded")
            link(v.tensor_copy(ntiles_i[:, :], ntiles[:, :]), "rounded_i")
            link(v.tensor_scalar(ntiles_i[:, :], ntiles_i[:, :], 7, None, ALU.arith_shift_right), "ntiles_i")
            link(v.tensor_copy(ntiles[:, :], ntiles_i[:, :]), "ntiles")
            v.tensor_copy(first_tile[:, 1:2], ntiles[:, 0:1]).then_inc(sort.sem, 1)
            link(v.tensor_tensor(first_tile[:, 2:3], ntiles[:, 0:1], ntiles[:, 1:2], ALU.add), "first2")
            link(v.tensor_tensor(first_tile[:, 3:4], first_tile[:, 2:3], ntiles[:, 2:3], ALU.add), "first3")
            dve.wait_ge(rank_ps, 1)
            link(v.scalar_tensor_tensor(place4[:, :, :], over_r(first_tile[:, :], NE), float(P),
                                        bM[1][:, 0:TILES * NE].rearrange("p (r e) -> p r e", r=TILES),
                                        ALU.mult, ALU.add), "places")
            link(v.tensor_tensor(place4[:, :, :], place4[:, :, :], choice[:, :, :], ALU.mult), "chosen")
            link(v.tensor_reduce(place[:, :], place4[:, :, :], AX.X, ALU.add), "place")
            link(v.tensor_copy(place_i[:, :], place[:, :]), "place_i")
            link(v.tensor_scalar(place_i[:, :], place_i[:, :], 7, None, ALU.arith_shift_right), "tile_i")
            link(v.tensor_copy(tile_of[:, :], place_i[:, :]), "tile")
            v.scalar_tensor_tensor(lane_of[:, :], tile_of[:, :], -float(P), place[:, :], ALU.mult, ALU.add)\
             .then_inc(sort.sem, 1)
            link(v.tensor_tensor(in_tile[:, :, :], over_r(jrow, NJ), tile_of[:, :].unsqueeze(2).to_broadcast([P, TILES, NJ]),
                                 ALU.is_equal), "in_tile")
            v.tensor_tensor(id_in_tile[:, :, :], in_tile[:, :, :], rowid.unsqueeze(2).to_broadcast([P, TILES, NJ]),
                            ALU.mult).then_inc(sort.sem, 1)
            for name, r0, r1 in (("lane_a", 0, TILES // 2), ("lane_b", TILES // 2, TILES)):
                n = r1 - r0
                v.tensor_tensor(in_lane[:, r0:r1, :], lanes.unsqueeze(1).to_broadcast([P, n, P]),
                                lane_of[:, r0:r1].unsqueeze(2).to_broadcast([P, n, P]), ALU.is_equal)\
                 .then_inc(sort.sem, 1)
            link(v.tensor_tensor(behind[:, :, :], jrow[0:1, :].unsqueeze(1).to_broadcast([1, NE - 1, NJ]),
                                 first_tile[0:1, 1:NE].unsqueeze(2).to_broadcast([1, NE - 1, NJ]), ALU.is_ge), "behind")
            link(v.tensor_reduce(expert_f[:, 0:NJ], behind[:, :, :].rearrange("p e j -> p j e"), AX.X, ALU.add), "expert")
            v.tensor_copy(expert_of[:, :], expert_f[:, 0:NJ]).then_inc(sort.sem, 1)
            link(v.scalar_tensor_tensor(three_f[:, 0, :], expert_f[:, 1:NJ + 1], float(NE), expert_f[:, 0:NJ],
                                        ALU.mult, ALU.add), "two")
            link(v.scalar_tensor_tensor(three_f[:, 1, :], expert_f[:, 2:NJ + 2], float(NE * NE), three_f[:, 0, :],
                                        ALU.mult, ALU.add), "three")
            v.tensor_copy(three_of[:, :], three_f[:, 1, :]).then_inc(sort.sem, 1)
            dve.wait_ge(rows_ps, 1)
            link(v.tensor_scalar(empty[:, :], bM[0][:, 0:NJ], 0.0, float(NONE), ALU.is_equal, ALU.mult), "empty")
            link(v.scalar_tensor_tensor(rows_f[:, :], bM[0][:, 0:NJ], -1.0, empty[:, :], ALU.add, ALU.add), "rows")
            link(v.tensor_scalar(rows_g[:, :], rows_f[:, :], float(B * T - 1), None, ALU.min), "rows_g")
            v.tensor_copy(from_rows[:, :], rows_g[:, :]).then_inc(sort.sem, 1)
            link(v.tensor_copy(to_rows[:, :], rows_f[:, :]), "to_rows")

            def expert_x(j, par):
                dve.wait_ge(xtp.sem, xtp.at(j))
                dve.wait_ge(l1.sem, l1.at(j - 2))
                xt = bank[0][:, 0:D].rearrange("p (k n) -> p k n", k=K2)
                v.tensor_copy(xs[par][:, 0, :, :], xt).then_inc(xsh.sem, 1)
                dve.wait_ge(xsh.sem, xsh.at(j))
                v.tensor_tensor(xs[par][:, 1, :, :], xt, xs[par][:, 0, :, :], ALU.subtract).then_inc(xsl.sem, 1)

            def start(j, par, half):
                e = dve.value_load(expert_of[0:1, bass.ds(j, 1)], min_val=0, max_val=NE - 1)
                dve.wait_ge(gat[par], 16 + 16 * half)
                hj = res[:, bass.ds(j, 1), :].rearrange("p j n -> p (j n)")
                v.tensor_tensor(hj, xg[par][:, D:2 * D], rb[:, bass.ds(e * D + RB["b2"], D)], ALU.add).then_inc(hbs.sem, 1)

            def split(j, par):
                for n, half in enumerate("ab"):
                    s = slice(4 * n, 4 * n + 4)
                    dve.wait_ge(gel.sem, gel.at(j, f"g{4 * n + 3}"))
                    dve.wait_ge(l2.sem, l2.at(j - 2))
                    v.tensor_copy(gh[par][:, s, :], gf[:, s, :]).then_inc(gsp_h.sem, 1)
                    dve.wait_ge(gsp_h.sem, gsp_h.at(j, half))
                    v.tensor_tensor(gl[par][:, s, :], gf[:, s, :], gh[par][:, s, :], ALU.subtract).then_inc(gsp_l.sem, 1)

            def result(j, par, half):
                dve.wait_ge(l2.sem, l2.at(j))
                dve.wait_ge(hbs.sem, hbs.at(j))
                if not isinstance(half, int) or half > 0:
                    dve.wait_ge(osc[par], half * 16)
                hj = res[:, bass.ds(j, 1), :].rearrange("p j n -> p (j n)")
                v.scalar_tensor_tensor(yo[par], bank[5 + par][:, 0:D], 1 / WS, hj, ALU.mult, ALU.add).then_inc(yok.sem, 1)

            expert_x(0, 0)
            start(0, 0, 0)
            expert_x(1, 1)
            start(1, 1, 0)
            split(0, 0)
            with dve.Fori(0, NJ // 2 - 1) as i:
                for par in (1, 0):
                    j = 2 * i + (2 - par)
                    expert_x(j + 1, 1 - par)
                    split(j, par)
                    start(j + 1, 1 - par, i + 1)
                    result(j - 1, 1 - par, i)
            split(NJ - 1, 1)
            result(NJ - 2, 0, NJ // 2 - 1)
            result(NJ - 1, 1, NJ // 2 - 1)

        @block.tensor
        def _(pe):
            mm = nc.tensor.matmul
            for s in (qkv, mps, sps, yps, ytp, *wops, xtp, l1, l2):
                pe.sem_inc(s.sem, s.head)
            for k in range(KP):
                pe.wait_ge(ld_x[k // 2], 32)
                for i in range(IT):
                    n, m = img_rows(i)
                    last = mm(bank[i][0:m, 0:D], xp[:, k, IPB * i * IMG:IPB * i * IMG + m], wp[:, k, :],
                              start=k == 0, stop=k == KP - 1)
            last.then_inc(emb_ps, 1)
            pe.wait_ge(ld_c, 16)
            for i in range(IT):
                n, m = img_rows(i)
                pe.wait_ge(img, 3 * IT + 3 + i)
                for k in range(K2):
                    last = nc.tensor.transpose(bank[i][:, k * m:(k + 1) * m], x1[0:m, i, k * P:(k + 1) * P],
                                               ident[0:m, 0:m])
                last.then_inc(xt_ps, 1)

            def transpose_txt(g):
                for q in range(TG // 2):
                    for b in range(2):
                        at = 2 * q + b
                        pe.wait_ge(txt_n[1].sem, txt_n[1].at(g, f"n{at}"))
                        for k in range(K2):
                            last = nc.tensor.transpose(bank[3 + TG // 2 * g + q][:, (2 * k + b) * P:(2 * k + b + 1) * P],
                                                       x1t[g][:, at, k * P:(k + 1) * P], ident)
                    last.then_inc(tt_ps, 1)

            qkh, qkl = small(wsh, 0, 4 * P), small(wsl, 0, 4 * P)
            vwh, vwl = small(wsh, K2 * 4 * P, D), small(wsl, K2 * 4 * P, D)
            owh, owl = small(wsh, K2 * (4 * P + D), D), small(wsl, K2 * (4 * P + D), D)

            def project(b, a):
                xh, xl = ([xT[:, c, k, bass.ds(b, 1), :].rearrange("p b n -> p (b n)") for k in range(K2)] for c in range(2))
                if a == 0:
                    pe.wait_ge(fin[0].sem, fin[0].at(b - 4, "h"))
                    pe.wait_ge(rope.sem, rope.at(b - 1, "qo"))
                else:
                    pe.wait_ge(ynorm.sem, ynorm.at(b - 3))
                    pe.wait_ge(rope.sem, rope.at(b - 1, "ko"))
                bk = (bQ, bK)[a]
                for eo in range(2):
                    m = 2 * a + eo
                    for k in range(K2):
                        for c, (w, x) in enumerate(((qkh, xh), (qkl, xh), (qkh, xl))):
                            last = mm(bk[:, eo * T:(eo + 1) * T], w[:, k, m * P:(m + 1) * P], x[k],
                                      start=k == 0 and c == 0, stop=k == K2 - 1 and c == 2)
                last.then_inc(qkv.sem, 1)

            def project_v(b):
                pe.wait_ge(yt_lo.sem, yt_lo.at(b - 3))
                pe.wait_ge(v_lo.sem, v_lo.at(b - 1))
                for s in range(2):
                    o = bV[:, 0:D] if s == 0 else bV[0:Q2, D:2 * D]
                    for k in range(K2):
                        for c, (a, w) in enumerate(((0, vwh), (0, vwl), (1, vwh))):
                            x = xT[:, a, k, bass.ds(b, 1), (0 if s == 0 else P):(P if s == 0 else T)]\
                                .rearrange("p b n -> p (b n)")
                            last = mm(o, x, w[:, k, :], start=k == 0 and c == 0, stop=k == K2 - 1 and c == 2)
                last.then_inc(qkv.sem, 1)

            def maxima(b, par, g, pairs=(bM,)):
                pe.wait_ge(kz_ok.sem, kz_ok.at(b))
                bM, back = pairs[g % len(pairs)], g - len(pairs)
                if g == 0:
                    pe.wait_ge(nm_lo.sem, nm_lo.at(b - 1))
                if back >= 0:
                    pe.wait_ge(mx.sem, mx.at(b, f"a{back}"))
                mm(bM[0][:, :], identb, mask_a.unsqueeze(1).to_broadcast([P, GRP, P]), start=True, stop=False)
                mm(bM[0][:, :], stk[par][:, 0, g, 0:P], kz[par][:, GRP * g:GRP * g + GRP, 0:P], start=False, stop=True)\
                    .then_inc(mps.sem, 1)
                if back >= 0:
                    pe.wait_ge(mx.sem, mx.at(b, f"b{back}"))
                mm(bM[1][:, 0:2 * T], identb, mask_b.unsqueeze(1).to_broadcast([P, 2, T]), start=True, stop=False,
                   skip_group_check=True)
                for u in range(2):
                    last = mm(bM[1][QB * u:QB * u + QB, 0:2 * T], stk[par][:, 0, g, QB0:T],
                              kz[par][:, GRP * g + 2 * u:GRP * g + 2 * u + 2, :], start=False, stop=True,
                              skip_group_check=True)
                last.then_inc(mps.sem, 1)

            def maxima_rows(b):
                pe.wait_ge(mx.sem, mx.at(b, "w1"))
                mm(bM[0][0:HEADS, 0:P], mx_a[:, :], ident, start=True, stop=True)
                mm(bM[0][0:HEADS, P:T], mx_w[:, :, :, :].rearrange("p g u e -> p (g u e)"), fold[:, QB - Q2:QB],
                   start=True, stop=True).then_inc(mps.sem, 1)

            def scores(b, par, n):
                name, h0, hn = chunks[n]
                if n == 0:
                    pe.wait_ge(nm_lo.sem, nm_lo.at(b))
                pe.wait_ge(ex.sem, ex.at(b if n >= 2 else b - 1, chunks[n - 2][0] + "h"))
                o = bS[n % 2]
                if name[0] == "d":
                    pe.sem_inc(spare, 1)
                    mm(o[0:Q2, 0:hn * Q2], identb[0:Q2, 0:Q2], mask_t2[0:Q2, :].unsqueeze(1).to_broadcast([Q2, hn, Q2]),
                       start=True, stop=False)
                else:
                    mm(o[:, 0:hn * T], identb, mask_t.unsqueeze(1).to_broadcast([P, hn, T]), start=True, stop=False)
                for h in range(h0, h0 + hn):
                    j = h - h0
                    if name[0] == "d":
                        oj, kk, qq = o[0:Q2, j * Q2:(j + 1) * Q2], slice(P, T), slice(P, T)
                    else:
                        oj, kk, qq = o[:, j * T:(j + 1) * T], slice(0, P), slice(0, T)
                    mm(oj, sel[:, h, 0:kk.stop - kk.start], nm[par][:, qq], start=False, stop=False)
                    last = mm(oj, kz[par][:, h, kk], stk[par][:, 0, h // GRP, qq], start=False, stop=h == h0 + hn - 1)
                last.then_inc(sps.sem, 1)

            def products(b, par, n, ahead):
                name, h0, hn = chunks[n]
                pe.wait_ge(pv_l.sem, pv_l.at(b, name))
                if name == "c0":
                    pe.wait_ge(v_lo.sem, v_lo.at(b))
                    pe.wait_ge(ynorm.sem, ynorm.at(b - 1))
                    if ahead == 2:
                        pe.wait_ge(rope.sem, rope.at(b + 2, "ko"))
                for h in range(h0, h0 + hn):
                    o1 = bY[:, h * (HD + 1):(h + 1) * (HD + 1)]
                    mm(o1, ph[:, h, 0:P], vh[par][:, h, :], start=True, stop=False)
                    mm(o1, ph[:, h, 0:P], vl[par][:, h, :], start=False, stop=False)
                    mm(o1, pl[:, h, 0:P], vh[par][:, h, :], start=False, stop=True)
                    o2 = bK[0:Q2, h * (HD + 1):(h + 1) * (HD + 1)]
                    mm(o2, ph[:, h, P:T], vh[par][:, h, :], start=True, stop=False)
                    mm(o2, ph[:, h, P:T], vl[par][:, h, :], start=False, stop=False)
                    mm(o2, pl[:, h, P:T], vh[par][:, h, :], start=False, stop=False)
                    mm(o2, ph2[:, h, :], vh2[par][:, h, :], start=False, stop=False)
                    mm(o2, ph2[:, h, :], vl2[par][:, h, :], start=False, stop=False)
                    last = mm(o2, pl2[:, h, :], vh2[par][:, h, :], start=False, stop=True)
                if n == len(chunks) - 1:
                    last.then_inc(yps.sem, 1)

            def turn(b, newest):
                pe.wait_ge(ynorm.sem, ynorm.at(b))
                pe.wait_ge(v_lo.sem, v_lo.at(newest))
                for k in range(K2):
                    nc.tensor.transpose(bV[:, k * T:k * T + P], yn[:, k * P:(k + 1) * P], ident)
                    last = nc.tensor.transpose(bV[:, k * T + P:(k + 1) * T], yn2[:, k * P:(k + 1) * P],
                                               ident[0:Q2, 0:Q2])
                last.then_inc(ytp.sem, 1)

            def output(bk, u, at, m=P):
                for k in range(K2):
                    for c, (a, w) in enumerate(((0, owh), (0, owl), (1, owh))):
                        last = mm(bk[0:m, 0:D], at(a, k), w[:, k, :], start=k == 0 and c == 0, stop=k == K2 - 1 and c == 2)
                last.then_inc(wops[u].sem, 1)

            def text_output(b, ahead, img=None):
                pe.wait_ge(yt_lo.sem, yt_lo.at(b))
                if ahead == 2:
                    pe.wait_ge(rope.sem, rope.at(b + 3, "qo"))
                if img is not None:
                    pe.wait_ge(fin[1].sem, fin[1].at(img, "h"))
                pe.wait_ge(fin[0].sem, fin[0].at(b - 1, "h"))
                output(bQ, 0, lambda a, k: yT[:, a, k, IMG:T])

            def image_output(i, bk):
                n, m = img_rows(i)
                pe.wait_ge(yti.sem, yti.at(IPB * i + n - 1))
                output(bk, 1, lambda a, k: yTi[:, K2 * a + k, IPB * i:IPB * i + n, :].rearrange("p b n -> p (b n)"), m)

            def batch(t, par, prev=True, ahead=2, img=None):
                scores(t, par, 0)
                scores(t, par, 1)
                if ahead == 2:
                    project(t + 2, 0)
                if img is not None:
                    pe.wait_ge(fin[0].sem, fin[0].at(t - 2, "h"))
                    image_output(img, bQ)
                if prev:
                    turn(t - 1, t + min(ahead + 0, 1))
                scores(t, par, 2)
                if ahead == 2:
                    project(t + 2, 1)
                scores(t, par, 3)
                if prev:
                    text_output(t - 1, ahead, img)
                for g in range(GRP):
                    if ahead >= 1:
                        maxima(t + 1, 1 - par, g)
                    scores(t, par, 4 + g)
                    products(t, par, 2 + g, ahead)
                if ahead >= 1:
                    maxima_rows(t + 1)
                if ahead == 2:
                    project_v(t + 2)
                products(t, par, 6, ahead)
                products(t, par, 7, ahead)

            transpose_txt(0)
            pe.wait_ge(wsplit_p, 1)
            pe.wait_ge(pool_c, 1)
            pe.wait_ge(xt_lo, IT)
            pe.wait_ge(tt_lo, TG // 2)
            for b in range(2):
                project(b, 0)
                project(b, 1)
                pe.wait_ge(wsplit_p, 2)
                project_v(b)
                if b == 0:
                    transpose_txt(1)
            pe.wait_ge(tt_lo, B // 2)
            pe.wait_ge(sel_ok, 1)
            for g in range(GRP):
                maxima(0, 0, g, (bM, bS))
            maxima_rows(0)
            batch(0, 0, prev=False)
            with pe.Fori(0, 2) as i:
                batch(2 * i + 1, 1)
                batch(2 * i + 2, 0)
            batch(5, 1)
            batch(6, 0, ahead=1, img=0)
            batch(7, 1, ahead=0, img=1)
            turn(7, 7)
            pe.wait_ge(fin[0].sem, fin[0].at(6, "h"))
            text_output(7, 0)
            pe.wait_ge(ynorm.sem, ynorm.at(7))
            image_output(2, bK)
            pe.wait_ge(sort.sem, sort.at(0, "choice"))
            for r in range(TILES):
                last = mm(bM[0][:, 0:NE], onesb, choice[:, r, :], start=r == 0, stop=r == TILES - 1)
            last.then_inc(total_ps, 1)
            ch = chosen[:, :, :].rearrange("p r e -> p (r e)")
            for back in range(TILES):
                at = (TILES - 1 - back) * NE
                last = mm(bM[1][:, 0:TILES * NE], onesb if back else before, ch[:, at:at + TILES * NE],
                          start=back == 0, stop=back == TILES - 1)
            last.then_inc(rank_ps, 1)
            pe.wait_ge(sort.sem, sort.at(0, "lane_a"))
            for r in range(TILES):
                if r == TILES // 2:
                    pe.wait_ge(sort.sem, sort.at(0, "lane_b"))
                last = mm(bM[0][:, 0:NJ], in_lane[:, r, :], id_in_tile[:, r, :], start=r == 0, stop=r == TILES - 1)
            last.then_inc(rows_ps, 1)

            def expert_x(j, par, half):
                pe.wait_ge(gat[par], 16 + 16 * half)
                pe.wait_ge(xsl.sem, xsl.at(j - 1))
                for k in range(K2):
                    last = nc.tensor.transpose(bank[0][:, k * P:(k + 1) * P], xg[par][:, k * P:(k + 1) * P], ident)
                last.then_inc(xtp.sem, 1)

            def experts(j):
                c = pe.value_load(three_of[0:1, bass.ds(j, 1)], min_val=0, max_val=NE ** 3 - 1)
                return c & (NE - 1), (c >> 2) & (NE - 1), (c >> 4) & (NE - 1)

            def first(j, par, e):
                pe.wait_ge(xsl.sem, xsl.at(j))
                for n in range(KF):
                    if n % 4 == 0:
                        pe.wait_ge(gel.sem, gel.at(j - 1, f"g{n + 3}"))
                    for k in range(K2):
                        wh, wl = (w[:, :].rearrange("p (e k n) -> p e k n", e=NE, k=K2)[:, bass.ds(e, 1), k, n * P:(n + 1) * P]
                                  .rearrange("p e n -> p (e n)") for w in (w1h, w1l))
                        o = bank[1 + n // 4][:, (n % 4) * P:(n % 4 + 1) * P]
                        mm(o, wh, xs[par][:, 0, k, :], start=k == 0, stop=False)
                        mm(o, wh, xs[par][:, 1, k, :], start=False, stop=False)
                        last = mm(o, wl, xs[par][:, 0, k, :], start=False, stop=k == K2 - 1)
                    if n % 4 == 3:
                        last.then_inc(l1.sem, 1)

            def second(j, par, e):
                pe.wait_ge(yok.sem, yok.at(j - 2))
                o = bank[5 + par][:, 0:D]
                for n in range(KF):
                    if n % 4 == 0:
                        pe.wait_ge(gsp_l.sem, gsp_l.at(j, "ab"[n // 4]))
                    wh, wl = (w[:, :].rearrange("p (e k n) -> p e k n", e=NE, k=KF)[:, bass.ds(e, 1), n, :]
                              .rearrange("p e n -> p (e n)") for w in (w2h, w2l))
                    mm(o, gh[par][:, n, :], wh, start=n == 0, stop=False)
                    mm(o, gl[par][:, n, :], wh, start=False, stop=False)
                    last = mm(o, gh[par][:, n, :], wl, start=False, stop=n == KF - 1)
                last.then_inc(l2.sem, 1)

            pe.wait_ge(sort.sem, sort.at(0, "three_of"))
            pe.wait_ge(wlo.sem, wlo.at(B - 1))
            expert_x(0, 0, 0)
            expert_x(1, 1, 0)
            assert NE == 4
            ea, eb, _ = experts(0)
            first(0, 0, ea)
            with pe.Fori(0, NJ // 2 - 1) as i:
                e = experts(2 * i)
                for n, par in ((1, 1), (2, 0)):
                    j = 2 * i + n
                    expert_x(j + 1, 1 - par, i + 1)
                    first(j, par, e[n])
                    second(j - 1, 1 - par, e[n - 1])
            ea, eb, _ = experts(NJ - 2)
            first(NJ - 1, 1, eb)
            second(NJ - 2, 0, ea)
            second(NJ - 1, 1, eb)


SORT_STEPS = ("gmax is_max order pmax first choice rounded rounded_i ntiles_i ntiles first1 first2 first3 places chosen "
              "place place_i tile_i tile lane in_tile id_in_tile lane_a lane_b behind expert expert_of two three three_of empty rows rows_g "
              "from_rows to_rows").split()


def layout(parts):
    at, n = {}, 0
    for name, width in parts:
        at[name] = n
        n += width
    return at, n


CF, CF_N = layout([("ident", P), ("cos", T), ("sin", T), ("fold", QB), ("headmask", GRP), ("rowid", TILES), ("valid", TILES),
                   ("lanes", P), ("order", NE), ("jrow", NJ)])
CB, CB_N = layout([("ident", P), ("mask_a", P), ("mask_b", T), ("mask_t", T), ("mask_t2", Q2), ("before", P),
                   ("ones", P), ("sel", HEADS)])
RB, ROWS = layout([("ln_w", D), ("ln_b", D), ("bo", D), ("type0", D), ("type1", D), ("wg", NE * D), ("b2", NE * D),
                   ("bg", NE)])
W_SMALL = K2 * (4 * P + 2 * D)
COLS = 4 + K2 + NE * KF


def constants():
    p = np.arange(P)
    f = np.zeros((P, CF_N), np.float32)
    f[:, CF["ident"]:CF["ident"] + P] = np.eye(P)
    t = np.arange(1, T + 1, dtype=np.float32)
    i = np.arange(ROT, dtype=np.float32)
    theta = np.power(np.float32(1.0 / 10000.0), np.float32(2.0) * i / np.float32(HD)).astype(np.float32)
    ang = t[None, :] * theta[p % ROT][:, None]
    f[:, CF["cos"]:CF["cos"] + T] = np.cos(ang) / WS
    f[:, CF["sin"]:CF["sin"] + T] = np.sin(ang) / WS
    f[:, CF["fold"]:CF["fold"] + QB] = p[:, None] % QB == np.arange(QB)[None, :]
    f[:, CF["headmask"]:CF["headmask"] + GRP] = (p[:, None] // ROT) % GRP == np.arange(GRP)[None, :]
    assert B * T <= 2048
    for b in range(B):
        f[:, CF["rowid"] + b] = b * T + IMG + p + 1
    for j in range(IT):
        f[:, CF["rowid"] + B + j] = np.where(p < img_rows(j)[1], (IPB * j + p // IMG) * T + p % IMG + 1, 0)
    f[:, CF["valid"]:CF["valid"] + TILES] = f[:, CF["rowid"]:CF["rowid"] + TILES] > 0
    f[:, CF["lanes"]:CF["lanes"] + P] = np.arange(P)
    f[:, CF["order"]:CF["order"] + NE] = NE - np.arange(NE)
    f[:, CF["jrow"]:CF["jrow"] + NJ] = np.arange(NJ)
    c = np.zeros((P, CB_N), np.float32)
    neg = np.float32(-4e10)
    c[:, CB["ident"]:CB["ident"] + P] = np.eye(P)
    c[:, CB["mask_a"]:CB["mask_a"] + P] = np.where(p[None, :] > p[:, None], neg, 0)
    key, query = np.arange(T), np.arange(T)
    c[:, CB["mask_b"]:CB["mask_b"] + T] = np.where(key[None, :] > QB0 + p[:, None] % QB, neg, 0)
    c[:, CB["mask_t"]:CB["mask_t"] + T] = np.where(p[:, None] > query[None, :], neg, 0)
    c[:, CB["mask_t2"]:CB["mask_t2"] + Q2] = np.where(p[:, None] > np.arange(Q2)[None, :], neg, 0)
    c[:, CB["before"]:CB["before"] + P] = p[:, None] < p[None, :]
    c[:, CB["ones"]:CB["ones"] + P] = 1
    c[:, CB["sel"]:CB["sel"] + HEADS] = (p[:, None] % 32 == np.arange(HEADS)[None, :]) & (p[:, None] < 64)
    bits = (c.view(np.uint32) >> 16).astype(np.uint16)
    return f, bits


def kernel(x, x_txt, mask_BS_i1_0, L0_tok_W, L0_tok_b, L0_tok_cls_token, L0_tok_pos_embedding, L0_txt_token_W,
           L0_txt_pos_W, L0_txt_type_W, L0_txt_ln_w, L0_txt_ln_b, L0_attn_Wq, L0_attn_bq, L0_attn_Wk, L0_attn_bk,
           L0_attn_Wv, L0_attn_bv, L0_attn_Wo, L0_attn_bo, L0_ffn_W1, L0_ffn_b1, L0_ffn_W2, L0_ffn_b2, L0_ffn_Wg,
           L0_ffn_bg):
    import concourse.bacc as bacc
    from concourse.bass_utils import run_bass_kernel_spmd

    a = {k: np.asarray(v) for k, v in locals().items() if k[0] in "xmL"}

    def blocks(w):
        return np.ascontiguousarray(w.reshape(-1, P, w.shape[1]).transpose(1, 0, 2))

    s = 96 // 16
    pt = a["x"].reshape(B, 3, s, 16, s, 16).transpose(1, 3, 5, 0, 2, 4).reshape(PDIM, B, PATCHES)
    pt = np.concatenate([np.zeros((PDIM, B, 1), pt.dtype), pt], axis=2).reshape(PDIM, B * IMG)
    pos = a["L0_tok_pos_embedding"][0]
    add = np.concatenate([a["L0_tok_cls_token"][0], np.tile(a["L0_tok_b"][None], (PATCHES, 1))])

    def even_odd(w):
        w = w.reshape(HEADS, ROT, 2, -1)
        return [w[:, :, j].reshape(P, -1) for j in range(2)]

    qk = np.concatenate(even_odd(a["L0_attn_Wq"]) + even_odd(a["L0_attn_Wk"])).T
    w_small = np.concatenate([blocks(w).reshape(P, -1) for w in (qk, a["L0_attn_Wv"].T, a["L0_attn_Wo"].T)], axis=1)
    cols = np.concatenate(even_odd(a["L0_attn_bq"]) + even_odd(a["L0_attn_bk"])
                          + [a["L0_attn_bv"].reshape(K2, P).T, a["L0_ffn_b1"].reshape(NE * KF, P).T], axis=1)
    rows = {"ln_w": a["L0_txt_ln_w"], "ln_b": a["L0_txt_ln_b"], "bo": a["L0_attn_bo"], "type0": a["L0_txt_type_W"][0],
            "type1": a["L0_txt_type_W"][1], "wg": a["L0_ffn_Wg"].T, "b2": a["L0_ffn_b2"], "bg": a["L0_ffn_bg"]}
    f, bits = constants()
    arrays = {
        "tok_tab": a["L0_txt_token_W"], "patches": blocks(pt), "w_patch": blocks(a["L0_tok_W"].T),
        "base_pos": np.tile(pos, (IPB, 1)), "base_add": np.tile(add, (IPB, 1)), "pos_txt": a["L0_txt_pos_W"],
        "ids": a["x_txt"].T, "types": a["mask_BS_i1_0"].T, "w_small": w_small, "cols": cols,
        "rows_b": np.concatenate([rows[k].reshape(-1) for k in RB]), "w1": a["L0_ffn_W1"], "w2": a["L0_ffn_W2"],
        "c_f32": f, "c_bits": bits,
    }
    arrays = {k: np.ascontiguousarray(v) for k, v in arrays.items()}
    nc = bacc.Bacc("TRN2", target_bir_lowering=False, num_devices=1)
    aps = {k: nc.dram_tensor(k, v.shape, mybir.dt.from_np(v.dtype), kind="ExternalInput").ap()
           for k, v in arrays.items()}
    out = nc.dram_tensor("out", (B * T, D), f32, kind="ExternalOutput").ap()
    program(nc, **aps, out=out)
    r = run_bass_kernel_spmd(nc, [arrays], core_ids=[0])
    return r.results[0]["out"].reshape(B, T, D)
```
